# Optimizing a Trainium2 kernel written in Bass

```python
import numpy as np
import jax
import jax.numpy as jnp

def _softmax(x, axis=-1):
    return jax.nn.softmax(x, axis=axis)

def _gelu(x):
    return jax.nn.gelu(x, approximate=True)

def _silu(x):
    return jax.nn.silu(x)

def _sigmoid(x):
    return jax.nn.sigmoid(x)

def _layernorm(x, axis=-1, eps=1e-05):
    m = jnp.mean(x, axis=axis, keepdims=True)
    v = jnp.var(x, axis=axis, keepdims=True)
    return (x - m) / jnp.sqrt(v + eps)

def _scatter_add(tgt, idx, src, axis=0):
    return tgt.at[idx].add(src)

def _segment_sum(src, seg, n):
    return jax.ops.segment_sum(src, seg, n)
kernel_name = 'mk_cond_seq_d1_seqx_r4_1f72d1'

def setup_inputs(seed: int=0):
    np.random.seed(seed)
    _w = jnp.asarray

    def _rec_inputs():
        import jax
        import jax.numpy as jnp
        _rk = jax.random.key(seed)
        x = -0.0003482 + 1 * jax.random.normal(jax.random.fold_in(_rk, 1), (16, 256, 288), jnp.float32)
        _lenS = 256 - jax.random.randint(jax.random.fold_in(_rk, 7), (16,), 0, max(1, 256 // 4) + 1, jnp.int32)
        _lenS2 = 256 - jax.random.randint(jax.random.fold_in(_rk, 8), (16,), 0, max(1, 256 // 4) + 1, jnp.int32)
        cond_1152 = 0.00257642 + 1.0011 * jax.random.normal(jax.random.fold_in(_rk, 11), (16, 288), jnp.float32)
        return (x, cond_1152)
    x, cond_1152 = _rec_inputs()

    def _L0_cond_setup():
        import jax, jax.numpy as jnp
        import numpy as np
        H = 288
        NH = 16
        HD = H // NH
        MLP = int(H * 4.0)
        EPS = 1e-06

        def _ln(z, scale=None):
            m = jnp.mean(z, axis=-1, keepdims=True)
            v = jnp.mean(jnp.square(z - m), axis=-1, keepdims=True)
            y = (z - m) * jax.lax.rsqrt(v + EPS)
            if scale is not None:
                y = y * scale
            return y
        key = jax.random.key(seed)
        ks = jax.random.split(key, 16)
        B, N = (16, 256)
        x = jax.random.normal(ks[0], (B, N, H), dtype=jnp.float32)
        c = jax.random.normal(ks[1], (B, H), dtype=jnp.float32)

        def xav(k, fan_in, fan_out):
            lim = np.sqrt(6.0 / (fan_in + fan_out))
            return jax.random.uniform(k, (fan_in, fan_out), jnp.float32, -lim, lim)
        w_mod = 0.02 * jax.random.normal(ks[2], (H, 6 * H), dtype=jnp.float32)
        b_mod = 0.02 * jax.random.normal(ks[3], (6 * H,), dtype=jnp.float32)
        w_qkv = xav(ks[4], H, 3 * H)
        b_qkv = jnp.zeros((3 * H,), jnp.float32)
        g_q = jnp.ones((HD,), jnp.float32)
        g_k = jnp.ones((HD,), jnp.float32)
        w_proj = xav(ks[5], H, H)
        b_proj = jnp.zeros((H,), jnp.float32)
        w1 = xav(ks[6], H, MLP)
        b1 = jnp.zeros((MLP,), jnp.float32)
        w2 = xav(ks[7], MLP, H)
        b2 = jnp.zeros((H,), jnp.float32)
        return dict(x=x, c=c, w_mod=w_mod, b_mod=b_mod, w_qkv=w_qkv, b_qkv=b_qkv, g_q=g_q, g_k=g_k, w_proj=w_proj, b_proj=b_proj, w1=w1, b1=b1, w2=w2, b2=b2)
    _L0_cond_all = _L0_cond_setup()
    _L0_cond_in = {k: v for k, v in _L0_cond_all.items() if k in ('w_mod', 'b_mod', 'w_qkv', 'b_qkv', 'g_q', 'g_k', 'w_proj', 'b_proj', 'w1', 'b1', 'w2', 'b2')}
    del _L0_cond_all
    return {'x': x, 'cond_1152': cond_1152, 'L0_cond_w_mod': _L0_cond_in['w_mod'], 'L0_cond_b_mod': _L0_cond_in['b_mod'], 'L0_cond_w_qkv': _L0_cond_in['w_qkv'], 'L0_cond_b_qkv': _L0_cond_in['b_qkv'], 'L0_cond_g_q': _L0_cond_in['g_q'], 'L0_cond_g_k': _L0_cond_in['g_k'], 'L0_cond_w_proj': _L0_cond_in['w_proj'], 'L0_cond_b_proj': _L0_cond_in['b_proj'], 'L0_cond_w1': _L0_cond_in['w1'], 'L0_cond_b1': _L0_cond_in['b1'], 'L0_cond_w2': _L0_cond_in['w2'], 'L0_cond_b2': _L0_cond_in['b2']}

def reference(x, cond_1152, L0_cond_w_mod, L0_cond_b_mod, L0_cond_w_qkv, L0_cond_b_qkv, L0_cond_g_q, L0_cond_g_k, L0_cond_w_proj, L0_cond_b_proj, L0_cond_w1, L0_cond_b1, L0_cond_w2, L0_cond_b2):
    import jax
    import jax.numpy as jnp

    def _L0_cond_ref(x, c, w_mod, b_mod, w_qkv, b_qkv, g_q, g_k, w_proj, b_proj, w1, b1, w2, b2):
        import jax, jax.numpy as jnp
        import numpy as np
        H = 288
        NH = 16
        HD = H // NH
        MLP = int(H * 4.0)
        EPS = 1e-06

        def _ln(z, scale=None):
            m = jnp.mean(z, axis=-1, keepdims=True)
            v = jnp.mean(jnp.square(z - m), axis=-1, keepdims=True)
            y = (z - m) * jax.lax.rsqrt(v + EPS)
            if scale is not None:
                y = y * scale
            return y
        B, N, _ = x.shape
        mod = jax.nn.swish(c) @ w_mod + b_mod
        sh_msa, sc_msa, g_msa, sh_mlp, sc_mlp, g_mlp = jnp.split(mod, 6, axis=1)
        xn = _ln(x) * (1 + sc_msa[:, None, :]) + sh_msa[:, None, :]
        qkv = xn @ w_qkv + b_qkv
        qkv = qkv.reshape(B, N, 3, NH, HD).transpose(2, 0, 3, 1, 4)
        q, k, v = (qkv[0], qkv[1], qkv[2])
        q = _ln(q, g_q)
        k = _ln(k, g_k)
        attn = jax.nn.softmax(jnp.einsum('bhqd,bhkd->bhqk', q, k) * HD ** (-0.5), axis=-1)
        o = jnp.einsum('bhqk,bhkd->bhqd', attn, v)
        o = o.transpose(0, 2, 1, 3).reshape(B, N, H) @ w_proj + b_proj
        x = x + g_msa[:, None, :] * o
        xn2 = _ln(x) * (1 + sc_mlp[:, None, :]) + sh_mlp[:, None, :]
        h = jax.nn.gelu(xn2 @ w1 + b1, approximate=True)
        x = x + g_mlp[:, None, :] * (h @ w2 + b2)
        return x
    x = _L0_cond_ref(x, cond_1152, L0_cond_w_mod, L0_cond_b_mod, L0_cond_w_qkv, L0_cond_b_qkv, L0_cond_g_q, L0_cond_g_k, L0_cond_w_proj, L0_cond_b_proj, L0_cond_w1, L0_cond_b1, L0_cond_w2, L0_cond_b2)
    return x

_drawn_inputs = setup_inputs


def setup_inputs(seed=0):
    import zlib

    import numpy as np

    out = dict(_drawn_inputs(seed))
    spreads = {'L0_cond_b_qkv': (0.0, 0.376),
     'L0_cond_g_q': (1.0, 0.6),
     'L0_cond_g_k': (1.0, 0.6),
     'L0_cond_b_proj': (0.0, 0.387),
     'L0_cond_b1': (0.0, 0.515),
     'L0_cond_b2': (0.0, 0.43)}
    factors = {'L0_cond_b_mod': 5.122}
    for name, (base, spread) in spreads.items():
        noise = np.random.default_rng([zlib.crc32(name.encode()), seed]).standard_normal(out[name].shape)
        drawn = base * np.exp(spread * noise) if base else spread * noise
        out[name] = jnp.asarray(drawn.astype(out[name].dtype))
    for name, factor in factors.items():
        out[name] = (out[name] * factor).astype(out[name].dtype)
    return out
```

```python
import concourse.bass as bass
from concourse import mybir
from contextlib import ExitStack

F32 = mybir.dt.float32
F32R = mybir.dt.float32r
F16 = mybir.dt.float16
I32 = mybir.dt.int32
ALU = mybir.AluOpType
ACT = mybir.ActivationFunctionType
AX = mybir.AxisListType

BATCH, TOK, HID = 16, 256, 288
NH, HD, MLP = 16, 18, 1152
P = 128
TT = TOK // P
REST = HID - 2 * P
MT = MLP // P
QUADS = NH // 4
GROUPS = 2 * QUADS
HALF = (3 * HID) // 2
VH = HID // 2
SLOT = 64
MROW = 3 * HD
EPS = 1e-6
RSQRT_SEED = float(0x5F3759DF)

CB = 96
CK = CB + 2
WIDE = 2 * P + CB


def cond_block_kernel(nc, x, cond, w_mod, b_mod, w_qkv, b_qkv, g_q, g_k, w_proj, b_proj, w1, b1, w2, b2, out):
    ctx = ExitStack()
    with ctx:
        def sb(name, shape, dt=F32):
            return ctx.enter_context(nc.sbuf_tensor(name, shape, dt))

        def sem(name):
            return ctx.enter_context(nc.semaphore(name))

        gates_dram = nc.dram_tensor("gates_scratch", [BATCH, 2, HID], F32).ap()
        bias_dram = nc.dram_tensor("bias_scratch", [BATCH, 2, 3 * HID], F32).ap()

        wq_hi = sb("wq_hi", [P, 2, 2, HALF], F32R)
        wq_lo = sb("wq_lo", [P, 2, 2, HALF], F32R)
        wq_c = sb("wq_c", [P, 2, HALF], F32R)
        wp_hi = sb("wp_hi", [P, 2, HID], F32R)
        wp_lo = sb("wp_lo", [P, 2, HID], F32R)
        wp_c = sb("wp_c", [P, HID], F32R)
        w1_hi = sb("w1_hi", [P, 2, MLP], F32R)
        w1_lo = sb("w1_lo", [P, 2, MLP], F32R)
        w1_c = sb("w1_c", [P, MLP], F32R)
        w2_hi = sb("w2_hi", [P, MT, HID], F32R)
        w2_lo = sb("w2_lo", [P, MT, HID], F32R)
        w2_b = sb("w2_b", [2, HID], F32R)
        ones2 = sb("ones2", [2, P], F32R)

        ident = sb("ident", [P, P])
        ident16 = sb("ident16", [P, P], F16)
        neg_half = sb("neg_half", [P, TT])
        gain = sb("gain", [P, HD])
        score_scale = sb("score_scale", [P, 1])
        columns = sb("columns", [P, BATCH, 6 + MT])
        sc1 = sb("sc1", [P, 3])
        sc2 = sb("sc2", [P, 3])
        bias2 = sb("bias2", [P, MT])
        gate1 = sb("gate1", [P, HID])
        gate2 = sb("gate2", [P, HID])

        xt_c = sb("xt_c", [P, TOK], F32R)
        stack = sb("stack", [P, TT, 2, NH, SLOT], F16)
        v = sb("v", [P, TT, NH, 32])
        ot_c = sb("ot_c", [P, TOK], F32R)

        ps_s0 = ctx.enter_context(nc.psum_tensor("ps_s0", [P, 1024], F32))
        ps_s1 = ctx.enter_context(nc.psum_tensor("ps_s1", [P, 1024], F32))
        ps_o = ctx.enter_context(nc.psum_tensor("ps_o", [P, 1024], F32))
        ps_m = ctx.enter_context(nc.psum_tensor("ps_m", [P, 1024], F32))
        ps_s = (ps_s0, ps_s1)
        ps_qkv = (ps_o, ps_s1)

        (x_a_in, bias_rows_in, sc1_in, x_b_in, gate1_in, sc2_in, gate2_in, bias2_in, x1_moved, out_stored,
         max_rows_in) = [sem(n) for n in (
             "x_a_in", "bias_rows_in", "sc1_in", "x_b_in", "gate1_in", "sc2_in", "gate2_in", "bias2_in",
             "x1_moved", "out_stored", "max_rows_in")]
        (ln1_stats, ln1_var, ln1_eps, ln1_rstd, xhat_ready, x_turned, xt_hi_kept, xt_lo_kept, qkv_done, squared,
         v_kept, ssq_ready, newton, factor_ready, qk_normed, qk_hi_kept, qk_lo_kept, qk_turned, qk_kept,
         max_scores, max_done, max_split, max_turned, max_kept) = [sem(n) for n in (
             "ln1_stats", "ln1_var", "ln1_eps", "ln1_rstd", "xhat_ready", "x_turned", "xt_hi_kept", "xt_lo_kept",
             "qkv_done", "squared", "v_kept", "ssq_ready", "newton", "factor_ready", "qk_normed", "qk_hi_kept",
             "qk_lo_kept", "qk_turned", "qk_kept", "max_scores", "max_done", "max_split", "max_turned", "max_kept")]
        (scores_done, exps_done, pv_done, oT_kept, o_back, recip_ready, o_normed, o_turned, ot_hi_kept, ot_lo_kept,
         projected, gated1_ready, x1_ready, ln2_stats, ln2_var, ln2_eps, ln2_rstd, xhat2_ready, ln2_turned,
         lt_hi_kept, lt_lo_kept) = [sem(n) for n in (
             "scores_done", "exps_done", "pv_done", "oT_kept", "o_back", "recip_ready", "o_normed", "o_turned",
             "ot_hi_kept", "ot_lo_kept", "projected", "gated1_ready", "x1_ready", "ln2_stats", "ln2_var", "ln2_eps",
             "ln2_rstd", "xhat2_ready", "ln2_turned", "lt_hi_kept", "lt_lo_kept")]
        (up_done, gelu_done, g_hi_kept, g_lo_kept, down_done, gated2_ready, y_ready) = [sem(n) for n in (
            "up_done", "gelu_done", "g_hi_kept", "g_lo_kept", "down_done", "gated2_ready", "y_ready")]
        NEWTON = 11

        with ExitStack() as prep:
            def tmp(name, shape, dt=F32):
                return prep.enter_context(nc.sbuf_tensor(name, shape, dt))

            def tsem(name):
                return prep.enter_context(nc.semaphore(name))

            wm = tmp("wm", [P, 3, 2 * HID])
            wqs = tmp("wqs", [P, 3, 3 * HID])
            c_in = tmp("c_in", [BATCH, HID])
            c_e = tmp("c_e", [BATCH, HID])
            c_r = tmp("c_r", [BATCH, HID])
            c_s = tmp("c_s", [BATCH, HID])
            cT = tmp("cT", [P, 3, BATCH])
            sc_rest = tmp("sc_rest", [BATCH, 2, CB])
            gqk = tmp("gqk", [P, 2, HD])
            gprod = tmp("gprod", [P, HD])
            gmax = tmp("gmax", [P, 3])
            head_mean = tmp("head_mean", [P, 3, 2 * NH])
            bq_row = tmp("bq_row", [1, 3 * HID])
            bq_mean = tmp("bq_mean", [1, 2 * NH])
            b_rows = tmp("b_rows", [1, 2, HID])
            b_hi = tmp("b_hi", [1, 2, HID], F32R)
            b_lo = tmp("b_lo", [1, 2, HID], F32R)
            ones_row = tmp("ones_row", [1, BATCH])
            b1_cols = tmp("b1_cols", [P, MT])
            shT = tmp("shT", [P, 2, 3, BATCH])
            raw = tmp("w1_raw", [P, 2 * MLP])
            mod = tmp("mod", [BATCH, 6 * HID])
            bias_parts_hi = tmp("bias_parts_hi", [BATCH, 2, HALF], F32R)
            bias_parts_lo = tmp("bias_parts_lo", [BATCH, 2, HALF], F32R)
            w1_raw = raw[:, 0:2 * MLP].rearrange("p (k n) -> p k n", k=2)
            w1_rawc = tmp("w1_rawc", [CB, MLP])
            wp_raw = tmp("wp_raw", [P, 3, HID])
            w2_raw = tmp("w2_raw", [P, MT, HID])

            (c_loaded, wm_in, wq_in, w1_in, wp_in, w2_in, g_in, small_in, id_set, set_up, silu_e, silu,
             cT_turned, cT_kept, mod_done, mod_kept, gates_out, shT_turned, shT_kept, centred, brow_done, brow_kept,
             brow_out, b2_done, split_hi, split_lo, rows_hi, rows_lo, rows_in, gains, sc_rest_kept, w1_lo_done, wq_hi_done, ones_set) = [tsem(n) for n in (
                 "c_loaded", "wm_in", "wq_in", "w1_in", "wp_in", "w2_in", "g_in", "small_in", "id_set",
                 "set_up", "silu_e", "silu", "cT_turned", "cT_kept", "mod_done", "mod_kept", "gates_out",
                 "shT_turned", "shT_kept", "centred", "brow_done", "brow_kept", "brow_out", "b2_done", "split_hi",
                 "split_lo", "rows_hi", "rows_lo", "rows_in", "gains", "sc_rest_kept", "w1_lo_done",
                 "wq_hi_done", "ones_set")]

            with nc.Block() as block:
                @block.sync
                def _(sp):
                    sp.dma_start(c_in[:, :], cond).then_inc(c_loaded, 16)
                    for part in range(3):
                        if part:
                            sp.wait_ge(mod_done, 2 * part)
                        cols = slice(part * 2 * HID, (part + 1) * 2 * HID)
                        sp.dma_start(wm[:, 0:2, :], w_mod[0:2 * P, cols].rearrange("(k p) n -> p k n", p=P)).then_inc(wm_in, 16)
                        sp.dma_start(wm[0:REST, 2, :], w_mod[2 * P:HID, cols]).then_inc(wm_in, 16)
                        sp.dma_start(wm[REST:REST + 1, 2, :], b_mod[cols].rearrange("(a n) -> a n", a=1)).then_inc(wm_in, 16)
                        if part == 0:
                            sp.dma_start(w1_raw, w1[0:2 * P, :].rearrange("(k p) n -> p k n", p=P)).then_inc(w1_in, 16)
                            for r in range(3):
                                sp.dma_start(w1_rawc[r * REST:(r + 1) * REST, :], w1[2 * P:HID, :]).then_inc(w1_in, 16)
                    sp.wait_ge(mod_kept, 6)
                    for g, chunk in ((0, 2), (1, 5)):
                        sp.dma_start(gates_dram[:, g, :], mod[:, chunk * HID:(chunk + 1) * HID]).then_inc(gates_out, 16)
                    sp.wait_ge(brow_kept, 8)
                    sp.dma_start(bias_dram[:, 0, :], bias_parts_hi[:, :, :].rearrange("b c n -> b (c n)").bitcast(F32)).then_inc(brow_out, 16)
                    sp.dma_start(bias_dram[:, 1, :], bias_parts_lo[:, :, :].rearrange("b c n -> b (c n)").bitcast(F32)).then_inc(brow_out, 16)
                    sp.wait_ge(gates_out, 32)
                    sp.wait_ge(brow_out, 32)

                @block.scalar
                def _(act):
                    act.dma_start(wqs[:, 0:2, :], w_qkv[0:2 * P, :].rearrange("(k p) n -> p k n", p=P)).then_inc(wq_in, 16)
                    for r in range(3):
                        act.dma_start(wqs[r * REST:(r + 1) * REST, 2, :], w_qkv[2 * P:HID, :]).then_inc(wq_in, 16)
                    act.dma_start(gqk[:, 0, :], g_q.partition_broadcast(P)).then_inc(g_in, 16)
                    act.dma_start(gqk[:, 1, :], g_k.partition_broadcast(P)).then_inc(g_in, 16)
                    act.dma_start(bq_row[:, :], b_qkv.rearrange("(a n) -> a n", a=1)).then_inc(small_in, 16)
                    act.dma_start(b_rows[:, 0, :], b_proj.rearrange("(a n) -> a n", a=1)).then_inc(small_in, 16)
                    act.dma_start(b_rows[:, 1, :], b2.rearrange("(a n) -> a n", a=1)).then_inc(small_in, 16)
                    act.dma_start(b1_cols[:, :], b1.rearrange("(m p) -> p m", p=P), allow_slow_non_contiguous=True).then_inc(small_in, 16)
                    act.dma_start(wp_raw[:, 0:2, :], w_proj[0:2 * P, :].rearrange("(k p) n -> p k n", p=P)).then_inc(wp_in, 16)
                    for r in range(3):
                        act.dma_start(wp_raw[r * REST:(r + 1) * REST, 2, :], w_proj[2 * P:HID, :]).then_inc(wp_in, 16)
                    act.dma_start(w2_raw[:, :, :], w2.rearrange("(m p) n -> p m n", p=P)).then_inc(w2_in, 16)
                    act.wait_ge(c_loaded, 16)
                    act.activation(c_e[:, :], c_in[:, :], ACT.Exp, scale=-1.0).then_inc(silu_e, 1)
                    for n in range(6):
                        act.wait_ge(mod_done, n + 1)
                        act.activation(mod[:, n * HID:(n + 1) * HID], ps_s[n % 2][0:BATCH, 512 * (n // 2 % 2):512 * (n // 2 % 2) + HID],
                                       ACT.Copy).then_inc(mod_kept, 1)
                    act.wait_ge(w1_in, 64)
                    act.activation(w1_hi[:, :, :], w1_raw, ACT.Copy).then_inc(split_hi, 1)
                    act.activation(w1_c[0:CB, :], w1_rawc[:, :], ACT.Copy).then_inc(split_hi, 1)
                    act.wait_ge(wp_in, 64)
                    act.activation(wp_hi[:, :, :], wp_raw[:, 0:2, :], ACT.Copy).then_inc(split_hi, 1)
                    act.activation(wp_c[0:CB, :], wp_raw[0:CB, 2, :], ACT.Copy).then_inc(split_hi, 1)
                    act.wait_ge(w2_in, 16)
                    act.activation(w2_hi[:, :, :], w2_raw[:, :, :], ACT.Copy).then_inc(split_hi, 1)
                    act.wait_ge(rows_hi, 1)
                    act.wait_ge(rows_lo, 1)
                    act.dma_start(wp_c[CB:CB + 1, :].bitcast(F32), b_hi[:, 0, :].bitcast(F32)).then_inc(rows_in, 16)
                    act.dma_start(wp_c[CB + 1:CK, :].bitcast(F32), b_lo[:, 0, :].bitcast(F32)).then_inc(rows_in, 16)
                    act.dma_start(w2_b[0:1, :].bitcast(F32), b_hi[:, 1, :].bitcast(F32)).then_inc(rows_in, 16)
                    act.dma_start(w2_b[1:2, :].bitcast(F32), b_lo[:, 1, :].bitcast(F32)).then_inc(rows_in, 16)
                    act.wait_ge(rows_in, 64)

                @block.gpsimd
                def _(pool):
                    pool.memset(ident[:, :], 0.0).then_inc(id_set, 1)
                    pool.memset(ident16[:, :], 0.0).then_inc(id_set, 1)
                    pool.wait_ge(id_set, 2)
                    for n, m in enumerate((ident, ident16)):
                        pool.affine_select(out=m[:, :], in_=m[:, :], compare_op=ALU.not_equal, fill=1.0, base=0,
                                           pattern=[[-1, P]], channel_multiplier=1).then_inc(id_set, 1)
                    pool.memset(neg_half[:, :], -0.5).then_inc(set_up, 1)
                    pool.memset(v[:, :, :, HD:HD + 1], 1.0).then_inc(set_up, 1)
                    pool.memset(v[:, :, :, HD + 1:32], 0.0).then_inc(set_up, 1)
                    pool.memset(stack[:, :, 0, :, MROW:SLOT], 0.0).then_inc(set_up, 1)
                    pool.memset(stack[:, :, 1, :, MROW:MROW + 2], 1.0).then_inc(set_up, 1)
                    pool.memset(stack[:, :, 1, :, MROW + 2:SLOT], 0.0).then_inc(set_up, 1)
                    pool.wait_ge(set_up, 6)
                    pool.wait_ge(split_hi, 2)
                    pool.tensor_tensor(w1_lo[:, 0, :], w1_raw[:, 0, :], w1_hi[:, 0, :].bitcast(F32), ALU.subtract).then_inc(w1_lo_done, 1)
                    pool.wait_ge(w1_lo_done, 1)

                @block.vector
                def _(dve):
                    dve.memset(ones_row[:, :], 1.0).then_inc(ones_set, 1)
                    dve.memset(xt_c[CB:CK, :].bitcast(F32), 1.0)
                    dve.memset(ot_c[CB:CK, :].bitcast(F32), 1.0)
                    dve.memset(ones2[:, :].bitcast(F32), 1.0)
                    dve.memset(columns[CB:P, :, :], 0.0)
                    dve.memset(cT[REST:REST + 1, 2, :], 1.0).then_inc(ones_set, 1)
                    dve.wait_ge(silu_e, 1)
                    dve.tensor_scalar_add(c_r[:, :], c_e[:, :], 1.0).then_inc(silu, 1)
                    dve.wait_ge(silu, 1)
                    dve.reciprocal(c_e[:, :], c_r[:, :]).then_inc(silu, 1)
                    dve.wait_ge(silu, 2)
                    dve.tensor_tensor(c_s[:, :], c_in[:, :], c_e[:, :], ALU.mult).then_inc(silu, 1)
                    dve.wait_ge(cT_turned, 1)
                    dve.tensor_copy(cT[:, 0:2, :], ps_m[:, 0:2 * BATCH].rearrange("p (k b) -> p k b", k=2)).then_inc(cT_kept, 1)
                    dve.tensor_copy(cT[0:REST, 2, :], ps_m[0:REST, 2 * BATCH:3 * BATCH]).then_inc(cT_kept, 1)
                    dve.wait_ge(wq_in, 64)
                    for k, rows in ((0, P), (1, P), (2, CB)):
                        dve.tensor_reduce(head_mean[0:rows, k, :], wqs[0:rows, k, 0:2 * HID].rearrange("p (h d) -> p h d", d=HD),
                                          AX.X, ALU.add).then_inc(centred, 1)
                    dve.wait_ge(small_in, 64)
                    dve.tensor_reduce(bq_mean[:, :], bq_row[:, 0:2 * HID].rearrange("p (h d) -> p h d", d=HD),
                                      AX.X, ALU.add).then_inc(centred, 1)
                    dve.wait_ge(centred, 4)
                    for k, rows in ((0, P), (1, P), (2, CB)):
                        w = wqs[0:rows, k, 0:2 * HID].rearrange("p (h d) -> p h d", d=HD)
                        dve.scalar_tensor_tensor(out=w, in0=head_mean[0:rows, k, :, None].broadcast_to([rows, 2 * NH, HD]),
                                                 scalar=-1.0 / HD, in1=w, op0=ALU.mult, op1=ALU.add).then_inc(centred, 1)
                    w = bq_row[:, 0:2 * HID].rearrange("p (h d) -> p h d", d=HD)
                    dve.scalar_tensor_tensor(out=w, in0=bq_mean[:, :, None].broadcast_to([1, 2 * NH, HD]),
                                             scalar=-1.0 / HD, in1=w, op0=ALU.mult, op1=ALU.add).then_inc(centred, 1)
                    dve.wait_ge(centred, 8)
                    wq_moves = []
                    for k in range(2):
                        wq_moves.append((wq_hi[:, k, :, 0:HID], wq_lo[:, k, :, 0:HID], wqs[:, k, 0:2 * HID].rearrange("p (c n) -> p c n", c=2)))
                        wq_moves.append((wq_hi[:, k, :, HID:HALF], wq_lo[:, k, :, HID:HALF], wqs[:, k, 2 * HID:].rearrange("p (c n) -> p c n", c=2)))
                    for hi, lo, src in wq_moves:
                        dve.tensor_copy(hi, src).then_inc(wq_hi_done, 1)
                    qk_c = wqs[0:CB, 2, 0:2 * HID].rearrange("p (c n) -> p c n", c=2)
                    v_c = wqs[0:CB, 2, 2 * HID:].rearrange("p (c n) -> p c n", c=2)
                    dve.tensor_copy(wq_c[0:CB, :, 0:HID], qk_c).then_inc(wq_hi_done, 1)
                    dve.tensor_copy(wq_c[0:CB, :, HID:HALF], v_c).then_inc(wq_hi_done, 1)
                    dve.wait_ge(wq_hi_done, 6)
                    dve.wait_ge(split_hi, 5)
                    for hi, lo, src in wq_moves:
                        dve.tensor_tensor(lo, src, hi.bitcast(F32), ALU.subtract).then_inc(split_lo, 1)
                    for dst, src in ((wq_c[2 * REST:CB, :, 0:HID], qk_c[2 * REST:CB]), (wq_c[2 * REST:CB, :, HID:HALF], v_c[2 * REST:CB]),
                                     (w1_c[2 * REST:CB, :], w1_rawc[2 * REST:CB, :]), (wp_c[2 * REST:CB, :], wp_raw[2 * REST:CB, 2, :])):
                        dve.tensor_tensor(dst, src, dst.bitcast(F32), ALU.subtract).then_inc(split_lo, 1)
                    dve.tensor_tensor(w1_lo[:, 1, :], w1_raw[:, 1, :], w1_hi[:, 1, :].bitcast(F32), ALU.subtract).then_inc(split_lo, 1)
                    dve.tensor_tensor(wp_lo[:, :, :], wp_raw[:, 0:2, :], wp_hi[:, :, :].bitcast(F32), ALU.subtract).then_inc(split_lo, 1)
                    dve.tensor_tensor(w2_lo[:, :, :], w2_raw[:, :, :], w2_hi[:, :, :].bitcast(F32), ALU.subtract).then_inc(split_lo, 1)
                    dve.tensor_copy(b_hi[:, :, :], b_rows[:, :, :]).then_inc(rows_hi, 1)
                    dve.wait_ge(rows_hi, 1)
                    dve.tensor_tensor(b_lo[:, :, :], b_rows[:, :, :], b_hi[:, :, :].bitcast(F32), ALU.subtract).then_inc(rows_lo, 1)
                    dve.wait_ge(g_in, 32)
                    dve.tensor_tensor(gprod[:, :], gqk[:, 0, :], gqk[:, 1, :], ALU.mult).then_inc(gains, 1)
                    dve.wait_ge(gains, 1)
                    dve.tensor_reduce(gmax[:, 0:1], gprod[:, :], AX.X, ALU.max, apply_absolute_value=True).then_inc(gains, 1)
                    dve.wait_ge(gains, 2)
                    dve.tensor_scalar_max(gmax[:, 1:2], gmax[:, 0:1], 1e-30).then_inc(gains, 1)
                    dve.wait_ge(gains, 3)
                    dve.reciprocal(gmax[:, 2:3], gmax[:, 1:2]).then_inc(gains, 1)
                    dve.tensor_scalar_mul(score_scale[:, :], gmax[:, 1:2], float(HD) ** -0.5).then_inc(gains, 1)
                    dve.wait_ge(gains, 5)
                    dve.tensor_scalar(gain[:, :], gprod[:, :], gmax[:, 2:3], None, ALU.mult).then_inc(gains, 1)
                    dve.wait_ge(gains, 6)
                    dve.wait_ge(mod_kept, 6)
                    for s, chunk in enumerate((1, 4)):
                        rest = mod[:, None, chunk * HID + 2 * P:(chunk + 1) * HID].broadcast_to([BATCH, 3, REST])
                        dve.tensor_copy(sc_rest[:, s, :].rearrange("b (r n) -> b r n", r=3), rest).then_inc(sc_rest_kept, 1)
                    dve.wait_ge(shT_turned, 1)
                    turned = ps_m[:, 64:64 + 4 * 3 * BATCH].rearrange("p (s k b) -> p s k b", s=4, k=3)
                    for s in range(2):
                        dve.tensor_copy(shT[:, s, 0:2, :], turned[:, s, 0:2, :]).then_inc(shT_kept, 1)
                        dve.tensor_copy(shT[0:REST, s, 2, :], turned[0:REST, s, 2, :]).then_inc(shT_kept, 1)
                        cols = columns[:, :, 3 * s:3 * s + 3].rearrange("p b k -> p k b")
                        dve.tensor_scalar_add(cols[:, 0:2, :], turned[:, 2 + s, 0:2, :], 1.0).then_inc(shT_kept, 1)
                        dve.tensor_scalar_add(cols[0:CB, 2, :], turned[0:CB, 2 + s, 2, :], 1.0).then_inc(shT_kept, 1)
                    dve.wait_ge(brow_done, 1)
                    rows_ps = ps_o[0:BATCH, :].rearrange("b (c n) -> b c n", c=2)
                    qk_ps = ((rows_ps[:, 0, 0:HID], 0, 0), (rows_ps[:, 0, HID:HALF], 1, 0), (rows_ps[:, 1, 0:VH], 1, VH))
                    flat = ps_o[0:BATCH, :]
                    pieces = (
                        (bias_parts_hi[:, 0, 0:HID], bias_parts_lo[:, 0, 0:HID], flat[:, 0:HID]),
                        (bias_parts_hi[:, 1, 0:VH], bias_parts_lo[:, 1, 0:VH], flat[:, HID:HALF]),
                        (bias_parts_hi[:, 1, VH:HID], bias_parts_lo[:, 1, VH:HID], flat[:, 512:512 + VH]),
                        (bias_parts_hi[:, :, HID:HALF], bias_parts_lo[:, :, HID:HALF],
                         flat[:, 512 + VH:512 + HALF].rearrange("b (c n) -> b c n", c=2)))
                    for hi, lo, src in pieces:
                        dve.tensor_copy(hi, src).then_inc(brow_kept, 1)
                    dve.wait_ge(brow_kept, 4)
                    for n, (hi, lo, src) in enumerate(pieces):
                        dve.tensor_tensor(lo, src, hi.bitcast(F32), ALU.subtract).then_inc(brow_kept, 1)
                    dve.wait_ge(b2_done, 1)
                    dve.tensor_tensor(columns[:, :, 6:6 + MT].rearrange("p b m -> p m b"),
                                      ps_s1[:, 0:MT * BATCH].rearrange("p (m b) -> p m b", m=MT),
                                      b1_cols[:, :, None].broadcast_to([P, MT, BATCH]), ALU.add).then_inc(shT_kept, 1)
                    dve.wait_ge(shT_kept, 9)
                    dve.wait_ge(split_lo, 11)

                @block.tensor
                def _(pe):
                    pe.wait_ge(id_set, 4)
                    pe.wait_ge(silu, 3)
                    for k, w in ((0, P), (1, P), (2, REST)):
                        mm = pe.transpose(ps_m[0:w, k * BATCH:(k + 1) * BATCH], c_s[:, k * P:k * P + w], ident[0:BATCH, 0:BATCH])
                    mm.then_inc(cT_turned, 1)
                    pe.wait_ge(cT_kept, 2)
                    pe.wait_ge(ones_set, 2)
                    for part in range(3):
                        pe.wait_ge(wm_in, 48 * (part + 1))
                        for h in range(2):
                            n = 2 * part + h
                            if n >= 4:
                                pe.wait_ge(mod_kept, n - 3)
                            dst = ps_s[n % 2][0:BATCH, 512 * (n // 2 % 2):512 * (n // 2 % 2) + HID]
                            for k, rows in ((0, P), (1, P), (2, REST + 1)):
                                mm = pe.matmul(dst, cT[0:rows, k, :], wm[0:rows, k, h * HID:(h + 1) * HID],
                                               start=(k == 0), stop=(k == 2))
                            mm.then_inc(mod_done, 1)
                    pe.wait_ge(mod_kept, 6)
                    pe.wait_ge(sc_rest_kept, 2)
                    for s, chunk in enumerate((0, 3, 1, 4)):
                        for k, w in ((0, P), (1, P), (2, REST)):
                            src = mod[:, chunk * HID + k * P:chunk * HID + k * P + w]
                            if k == 2 and s >= 2:
                                src, w = sc_rest[:, s - 2, :], CB
                            col = 64 + (s * 3 + k) * BATCH
                            mm = pe.transpose(ps_m[0:w, col:col + BATCH], src, ident[0:BATCH, 0:BATCH])
                    mm.then_inc(shT_turned, 1)
                    pe.wait_ge(shT_kept, 8)
                    pe.wait_ge(centred, 8)
                    for half in range(2):
                        cols = slice(half * HALF, (half + 1) * HALF)
                        dst = ps_o[0:BATCH, 512 * half:512 * half + HALF]
                        for k, rows in ((0, P), (1, P), (2, REST)):
                            pe.matmul(dst, shT[0:rows, 0, k, :], wqs[0:rows, k, cols], start=(k == 0), stop=False)
                        mm = pe.matmul(dst, ones_row[:, :], bq_row[:, cols], start=False, stop=True)
                    mm.then_inc(brow_done, 1)
                    pe.wait_ge(w1_in, 64)
                    for m in range(MT):
                        cols = slice(m * P, (m + 1) * P)
                        for k, rows in ((0, P), (1, P), (2, REST)):
                            w = w1_raw[:, k, cols] if k < 2 else w1_rawc[0:REST, cols]
                            mm = pe.matmul(ps_s1[:, m * BATCH:(m + 1) * BATCH], w, shT[0:rows, 1, k, :], start=(k == 0), stop=(k == 2))
                    mm.then_inc(b2_done, 1)

        x_a = sb("x_a", [P, TT, HID])
        waited = sb("waited", [P, 1])
        stats = sb("stats", [P, TT, 6])
        moments = sb("moments", [P, TT, 2])
        var_eps = sb("var_eps", [P, TT])
        rstd = sb("rstd", [P, TT])
        xhat = sb("xhat", [P, TT, WIDE])
        xt_hi = sb("xt_hi", [P, 2, TOK], F32R)
        xt_lo = sb("xt_lo", [P, 2, TOK], F32R)
        squares = sb("squares", [P, TT, 2 * HID])
        ssq = sb("ssq", [P, TT, 2 * NH])
        qk_var = sb("qk_var", [P, TT, 2 * NH])
        qk_r = sb("qk_r", [P, TT, 2 * NH])
        qk_tmp = sb("qk_tmp", [P, TT, 2 * NH])
        q_factor = sb("q_factor", [P, TT, HID])
        qk_n = sb("qk_n", [P, TT, 2, HID])
        qT = sb("qT", [P, NH // 2, TOK], F16)
        kT = sb("kT", [P, NH // 2, TOK], F16)
        neg_max = sb("neg_max", [P, TT, 2, NH // 2])
        max_parts = sb("max_parts", [P, TT, 2, 2, NH // 2], F16)
        max_rows = sb("max_rows", [2 * NH, TOK], F16)

        x_b = sb("x_b", [P, TT, HID])
        probs = sb("probs", [P, 2, 4 * TOK])
        oT = sb("oT", [P, QUADS * TOK])
        recip = sb("recip", [P, TT, NH])
        o_n = sb("o_n", [P, TT, WIDE])
        ot_hi = sb("ot_hi", [P, 2, TOK], F32R)
        ot_lo = sb("ot_lo", [P, 2, TOK], F32R)
        gated1 = sb("gated1", [P, TT, HID])
        x1_new = sb("x1_new", [P, TT, HID])
        stats2 = sb("stats2", [P, TT, 6])
        moments2 = sb("moments2", [P, TT, 2])
        var_eps2 = sb("var_eps2", [P, TT])
        rstd2 = sb("rstd2", [P, TT])
        xhat2 = sb("xhat2", [P, TT, WIDE])
        lt_hi = sb("lt_hi", [P, 2, TOK], F32R)
        lt_lo = sb("lt_lo", [P, 2, TOK], F32R)
        lt_c = sb("lt_c", [P, TOK], F32R)

        x1_c = sb("x1_c", [P, TT, HID])
        g_full = sb("g_full", [P, MT, TOK])
        g_hi = sb("g_hi", [P, MT, TOK], F32R)
        g_lo = sb("g_lo", [P, MT, TOK], F32R)
        gated2 = sb("gated2", [P, TT, HID])
        y = sb("y", [P, TT, HID])

        def place(j):
            return (2 * (j % 2) + j // 2) * TOK

        def reuse(eng, semaphore, per_sequence, n):
            if not (isinstance(n, int) and n == 0):
                eng.wait_ge(semaphore, per_sequence * n)

        def iterations(eng, body):
            body(0, None, None)
            body(1, 0, None)
            body(2, 1, 0)
            with eng.Fori(2, BATCH - 1) as i:
                body(i + 1, i, i - 1)
            body(None, BATCH - 1, BATCH - 2)
            body(None, None, BATCH - 1)

        x_t = x.rearrange("b (t p) n -> b p t n", p=P)
        out_t = out.rearrange("b (t p) n -> b p t n", p=P)

        with nc.Block() as block:
            @block.sync
            def _(sp):
                def body(a, b, c):
                    if a is not None:
                        reuse(sp, xhat_ready, 4, a)
                        sp.dma_start(x_a[:, :, :], x_t[a]).then_inc(x_a_in, 16)
                        reuse(sp, xt_hi_kept, 3, a)
                        reuse(sp, xt_lo_kept, 3, a)
                        sp.dma_start(sc1[:, :], columns[:, a, 0:3]).then_inc(sc1_in, 16)
                        reuse(sp, qkv_done, 2, a)
                        sp.dma_start(wq_c[CB:CK, :, :].bitcast(F32), bias_dram[a].rearrange("r (c n) -> r c n", c=2)).then_inc(bias_rows_in, 16)
                    if b is not None:
                        reuse(sp, x1_ready, 2, b)
                        sp.dma_start(x_b[:, :, :], x_t[b]).then_inc(x_b_in, 16)
                        reuse(sp, gated1_ready, 2, b)
                        sp.dma_start(gate1[:, :], gates_dram[b, 0, :].partition_broadcast(P)).then_inc(gate1_in, 16)
                        reuse(sp, lt_hi_kept, 3, b)
                        reuse(sp, lt_lo_kept, 3, b)
                        sp.dma_start(sc2[:, :], columns[:, b, 3:6]).then_inc(sc2_in, 16)
                    if c is not None:
                        reuse(sp, gelu_done, MT, c)
                        sp.dma_start(bias2[:, :], columns[:, c, 6:6 + MT]).then_inc(bias2_in, 16)
                        reuse(sp, gated2_ready, 2, c)
                        sp.dma_start(gate2[:, :], gates_dram[c, 1, :].partition_broadcast(P)).then_inc(gate2_in, 16)
                        reuse(sp, y_ready, 2, c)
                        sp.wait_ge(x1_ready, 2 * (c + 1))
                        sp.dma_start(x1_c[:, :, :], x1_new[:, :, :]).then_inc(x1_moved, 16)
                    if a is not None:
                        sp.wait_ge(max_kept, a + 1)
                        for parity in range(2):
                            for part in range(2):
                                row = SLOT * parity + MROW + part
                                at = NH * parity + NH // 2 * part
                                sp.dma_start(qT[row:row + 1, :, :], max_rows[at:at + NH // 2, :]).then_inc(max_rows_in, 16)
                    if c is not None:
                        sp.wait_ge(y_ready, 2 * (c + 1))
                        sp.dma_start(out_t[c], y[:, :, :]).then_inc(out_stored, 16)

                iterations(sp, body)
                sp.wait_ge(out_stored, 16 * BATCH)

            @block.tensor
            def _(pe):
                def attend(b):
                    def pv(g):
                        quad, kt = g // 2, g % 2
                        pe.wait_ge(exps_done, GROUPS * b + g + 1)
                        for j in range(4):
                            at = place(j)
                            mm = pe.matmul(ps_o[32 * j:32 * j + 32, quad * TOK:(quad + 1) * TOK], v[:, kt, 4 * quad + j, :],
                                           probs[:, g % 2, at:at + TOK], start=(kt == 0), stop=(kt == 1))
                        mm.then_inc(pv_done, 1)

                    pe.wait_ge(max_rows_in, 64 * (b + 1))
                    pe.wait_ge(max_done, GROUPS * (b + 1))
                    pe.wait_ge(max_kept, b + 1)
                    reuse(pe, lt_hi_kept, 3, b)
                    reuse(pe, lt_lo_kept, 3, b)
                    for g in range(GROUPS):
                        quad, kt = g // 2, g % 2
                        if g >= 2:
                            pe.wait_ge(exps_done, GROUPS * b + g - 1)
                        for j in range(4):
                            h = 4 * quad + j
                            at = SLOT * (h % 2)
                            mm = pe.matmul(ps_s[g % 2][:, place(j):place(j) + TOK], kT[at:at + MROW + 2, h // 2, kt * P:(kt + 1) * P],
                                           qT[at:at + MROW + 2, h // 2, :], start=True, stop=True)
                        mm.then_inc(scores_done, 1)
                        if g >= 1:
                            pv(g - 1)
                    pv(GROUPS - 1)

                def turn(src, dst):
                    for k in range(3):
                        for t in range(TT):
                            rows = P if k < 2 else CB
                            mm = pe.transpose(dst[0:rows, k * TOK + t * P:k * TOK + (t + 1) * P], src[:, t, k * P:k * P + rows], ident[:, :])
                    return mm

                def turn_x(a, b):
                    pe.wait_ge(xhat_ready, 4 * (a + 1))
                    if b is not None:
                        pe.wait_ge(exps_done, GROUPS * b + GROUPS - 1)
                    turn(xhat, ps_s0).then_inc(x_turned, 1)

                def qkv(a, b, t):
                    if t == 0:
                        pe.wait_ge(xt_hi_kept, 3 * (a + 1))
                        pe.wait_ge(xt_lo_kept, 3 * (a + 1))
                        pe.wait_ge(bias_rows_in, 16 * (a + 1))
                        if b is not None:
                            pe.wait_ge(oT_kept, 2 * (b + 1))
                    elif b is not None:
                        pe.wait_ge(o_normed, 3 * (b + 1))
                    tok = slice(t * P, (t + 1) * P)
                    for half in range(2):
                        dst = ps_qkv[t][:, 512 * half:512 * half + HALF]
                        for k in range(2):
                            pe.matmul(dst, xt_hi[:, k, tok], wq_hi[:, k, half, :], start=(k == 0), stop=False)
                            pe.matmul(dst, xt_hi[:, k, tok], wq_lo[:, k, half, :], start=False, stop=False)
                            pe.matmul(dst, xt_lo[:, k, tok], wq_hi[:, k, half, :], start=False, stop=False)
                        mm = pe.matmul(dst, xt_c[0:CK, tok], wq_c[0:CK, half, :], start=False, stop=True)
                    mm.then_inc(qkv_done, 1)

                def turn_qk(a, t):
                    pe.wait_ge(qk_hi_kept, 4 * a + 2 * t + 2)
                    pe.wait_ge(qk_lo_kept, 4 * a + 2 * t + 2)
                    pe.wait_ge(v_kept, 2 * a + t + 1)
                    dst = ps_qkv[t][:, :].bitcast(F16)
                    for c in range(2):
                        for j in range(NH // 2):
                            mm = pe.transpose(dst[:, c * 1024 + j * P:c * 1024 + (j + 1) * P],
                                              stack[:, t, c, 2 * j:2 * j + 2, :].rearrange("p h s -> p (h s)"), ident16[:, :])
                        mm.then_inc(qk_turned, 1)

                def maxima(a, g):
                    quad, qt = g // 2, g % 2
                    if g == 0:
                        pe.wait_ge(qk_kept, 4 * (a + 1))
                    if g >= 2:
                        pe.wait_ge(max_done, GROUPS * a + g - 1)
                    for jj in range(2):
                        for parity in range(2):
                            j = 2 * quad + jj
                            at = SLOT * parity
                            n = 2 * parity + jj
                            mm = pe.matmul(ps_qkv[g % 2][:, n * TOK:(n + 1) * TOK], qT[at:at + MROW, j, qt * P:(qt + 1) * P],
                                           kT[at:at + MROW, j, :], start=True, stop=True)
                    mm.then_inc(max_scores, 1)

                def turn_max(a, b):
                    pe.wait_ge(max_split, 2 * (a + 1))
                    if b is not None:
                        pe.wait_ge(lt_hi_kept, 3 * (b + 1))
                        pe.wait_ge(lt_lo_kept, 3 * (b + 1))
                    dst = ps_s0[:, :].bitcast(F16)
                    for t in range(TT):
                        mm = pe.transpose(dst[0:2 * NH, 1536 + t * P:1536 + (t + 1) * P],
                                          max_parts[:, t].rearrange("p a s j -> p (a s j)"), ident16[:, :])
                    mm.then_inc(max_turned, 1)

                def turn_o_back(b):
                    pe.wait_ge(oT_kept, 2 * (b + 1))
                    pe.wait_ge(exps_done, GROUPS * (b + 1))
                    for t in range(TT):
                        for quad in range(QUADS):
                            mm = pe.transpose(ps_s1[:, t * 512 + quad * P:t * 512 + (quad + 1) * P],
                                              oT[:, quad * TOK + t * P:quad * TOK + (t + 1) * P], ident[:, :])
                        mm.then_inc(o_back, 1)

                def turn_o(a, b):
                    pe.wait_ge(o_normed, 3 * (b + 1))
                    if a is not None:
                        pe.wait_ge(xt_hi_kept, 3 * (a + 1))
                        pe.wait_ge(xt_lo_kept, 3 * (a + 1))
                    turn(o_n, ps_s0).then_inc(o_turned, 1)

                def project(b):
                    pe.wait_ge(ot_hi_kept, 2 * (b + 1))
                    pe.wait_ge(ot_lo_kept, 2 * (b + 1))
                    for t in range(TT):
                        tok = slice(t * P, (t + 1) * P)
                        dst = ps_s0[:, 512 * t:512 * t + HID]
                        for k in range(2):
                            pe.matmul(dst, ot_hi[:, k, tok], wp_hi[:, k, :], start=(k == 0), stop=False)
                            pe.matmul(dst, ot_hi[:, k, tok], wp_lo[:, k, :], start=False, stop=False)
                            pe.matmul(dst, ot_lo[:, k, tok], wp_hi[:, k, :], start=False, stop=False)
                        pe.matmul(dst, ot_c[0:CK, tok], wp_c[0:CK, :], start=False, stop=True).then_inc(projected, 1)

                def turn_ln2(b):
                    pe.wait_ge(xhat2_ready, 4 * (b + 1))
                    pe.wait_ge(gated1_ready, 2 * (b + 1))
                    turn(xhat2, ps_s0).then_inc(ln2_turned, 1)

                def mlp_up(c, m):
                    if m == 0:
                        pe.wait_ge(lt_hi_kept, 3 * (c + 1))
                        pe.wait_ge(lt_lo_kept, 3 * (c + 1))
                        reuse(pe, gated2_ready, 2, c)
                    if m >= 2:
                        pe.wait_ge(gelu_done, MT * c + m - 1)
                    dst = ps_m[:, 512 * (m % 2):512 * (m % 2) + TOK]
                    cols = slice(m * P, (m + 1) * P)
                    for k in range(2):
                        pe.matmul(dst, w1_hi[:, k, cols], lt_hi[:, k, :], start=(k == 0), stop=False)
                        pe.matmul(dst, w1_hi[:, k, cols], lt_lo[:, k, :], start=False, stop=False)
                        pe.matmul(dst, w1_lo[:, k, cols], lt_hi[:, k, :], start=False, stop=False)
                    pe.matmul(dst, w1_c[0:CB, cols], lt_c[0:CB, :], start=False, stop=True).then_inc(up_done, 1)

                def mlp_down(c, first, last):
                    for n in range(first, last):
                        t, r = n // (3 * MT + 1), n % (3 * MT + 1)
                        dst = ps_m[:, 512 * t:512 * t + HID]
                        tok = slice(t * P, (t + 1) * P)
                        if r == 0:
                            if t == 0:
                                pe.wait_ge(gelu_done, MT * (c + 1))
                            pe.matmul(dst, ones2[:, :], w2_b[:, :], start=True, stop=False)
                            continue
                        m, part = (r - 1) // 3, (r - 1) % 3
                        if t == 0 and part == 0:
                            pe.wait_ge(g_hi_kept, MT * c + m + 1)
                        if t == 0 and part == 2:
                            pe.wait_ge(g_lo_kept, MT * c + m + 1)
                        g = g_lo if part == 2 else g_hi
                        w = w2_lo if part == 1 else w2_hi
                        mm = pe.matmul(dst, g[:, m, tok], w[:, m, :], start=False, stop=(r == 3 * MT))
                        if r == 3 * MT:
                            mm.then_inc(down_done, 1)

                DOWN = 2 * (3 * MT + 1)
                PIECE = 5

                def body(a, b, c):
                    A, B, C = a is not None, b is not None, c is not None
                    if B:
                        attend(b)
                    if A:
                        turn_x(a, b)
                    if C:
                        for m in range(0, 3):
                            mlp_up(c, m)
                    if B:
                        turn_o_back(b)
                    if A:
                        qkv(a, b, 0)
                    if B:
                        turn_o(a, b)
                    if A:
                        qkv(a, b, 1)
                    if B:
                        project(b)
                    if C:
                        for m in range(3, 6):
                            mlp_up(c, m)
                    if A:
                        turn_qk(a, 0)
                    if C:
                        for m in range(6, 8):
                            mlp_up(c, m)
                    if A:
                        turn_qk(a, 1)
                    if B:
                        turn_ln2(b)
                    if C:
                        mlp_up(c, 8)
                    for g in range(GROUPS):
                        if A:
                            maxima(a, g)
                        if C:
                            mlp_down(c, g * PIECE, (g + 1) * PIECE)
                    if A:
                        turn_max(a, b)
                    if C:
                        mlp_down(c, GROUPS * PIECE, DOWN)

                iterations(pe, body)

            @block.scalar
            def _(act):
                def exps(b, g):
                    act.wait_ge(scores_done, GROUPS * b + g + 1)
                    if g >= 2:
                        act.wait_ge(pv_done, GROUPS * b + g - 1)
                    act.activation(probs[:, g % 2, :], ps_s[g % 2][:, :], ACT.Exp, scale=score_scale[:, 0:1]).then_inc(exps_done, 1)

                def keep_oT(b, half):
                    act.wait_ge(pv_done, GROUPS * b + 4 * half + 4)
                    if half == 0:
                        reuse(act, o_back, 2, b)
                    act.activation(oT[:, half * 512:(half + 1) * 512], ps_o[:, half * 512:(half + 1) * 512], ACT.Copy).then_inc(oT_kept, 1)

                def keep_hi(n, turned, scales_in, scales, hi, stacked, kept, used, used_per):
                    act.wait_ge(turned, n + 1)
                    act.wait_ge(scales_in, 16 * (n + 1))
                    reuse(act, used, used_per, n)
                    for k in range(2):
                        act.activation(hi[:, k, :], ps_s0[:, k * TOK:(k + 1) * TOK], ACT.Copy, scale=scales[:, k:k + 1]).then_inc(kept, 1)
                    act.activation(stacked[0:CB, :], ps_s0[0:CB, 512:512 + TOK], ACT.Copy, scale=scales[0:CB, 2:3]).then_inc(kept, 1)

                def keep_o_hi(b):
                    act.wait_ge(o_turned, b + 1)
                    reuse(act, projected, 2, b)
                    act.activation(ot_hi[:, :, :].rearrange("p k t -> p (k t)"), ps_s0[:, 0:512], ACT.Copy).then_inc(ot_hi_kept, 1)
                    act.activation(ot_c[0:CB, :], ps_s0[0:CB, 512:512 + TOK], ACT.Copy).then_inc(ot_hi_kept, 1)

                def square(a, t):
                    act.wait_ge(qkv_done, 2 * a + t + 1)
                    reuse(act, ssq_ready, 2, a)
                    qkv = ps_qkv[t][:, :].rearrange("p (c n) -> p c n", c=2)
                    act.activation(squares[:, t, :].rearrange("p (c n) -> p c n", c=2), qkv[:, :, 0:HID], ACT.Square).then_inc(squared, 1)

                def keep_v(a, t, b):
                    if b is not None:
                        act.wait_ge(pv_done, GROUPS * (b + 1))
                    qkv = ps_qkv[t][:, :].rearrange("p (c n) -> p c n", c=2)
                    for half in range(2):
                        ins = act.activation(v[:, t, 8 * half:8 * half + 8, 0:HD],
                                             qkv[:, half, HID:HALF].rearrange("p (h d) -> p h d", d=HD), ACT.Copy)
                    ins.then_inc(v_kept, 1)

                def keep_qk_hi(a, t):
                    if t == 0:
                        reuse(act, qk_turned, 4, a)
                    for c, second in ((0, 2), (1, 1)):
                        act.wait_ge(qk_normed, 4 * a + 2 * t + c + 1)
                        dst = stack[:, t, c, :, 0:MROW].rearrange("p h (s d) -> p h s d", d=HD)[:, :, 0:second + 1:second, :]
                        src = qk_n[:, t, c, :].rearrange("p (h d) -> p h d", d=HD)[:, :, None, :].broadcast_to([P, NH, 2, HD])
                        act.activation(dst, src, ACT.Copy).then_inc(qk_hi_kept, 1)

                def keep_max(a, b):
                    act.wait_ge(max_turned, a + 1)
                    reuse(act, max_rows_in, 64, a)
                    act.activation(max_rows[:, :], ps_s0[0:2 * NH, :].bitcast(F16)[:, 1536:1536 + TOK], ACT.Copy).then_inc(max_kept, 1)

                def gelu(c, m):
                    if m == 0:
                        act.wait_ge(bias2_in, 16 * (c + 1))
                        reuse(act, g_lo_kept, MT, c)
                        reuse(act, down_done, 2, c)
                    act.wait_ge(up_done, MT * c + m + 1)
                    act.activation(g_full[:, m, :], ps_m[:, 512 * (m % 2):512 * (m % 2) + TOK], ACT.Gelu_apprx_tanh,
                                   bias=bias2[:, m:m + 1]).then_inc(gelu_done, 1)

                def keep_g_hi(c, m):
                    act.wait_ge(gelu_done, MT * c + m + 1)
                    act.activation(g_hi[:, m, :], g_full[:, m, :], ACT.Copy).then_inc(g_hi_kept, 1)

                def gelus(c, first, last):
                    for m in range(first, last):
                        gelu(c, m)
                        if m > first:
                            keep_g_hi(c, m - 1)
                    keep_g_hi(c, last - 1)

                def body(a, b, c):
                    A, B, C = a is not None, b is not None, c is not None
                    if B:
                        for g in range(GROUPS):
                            exps(b, g)
                            if g == 5:
                                keep_oT(b, 0)
                    if A:
                        keep_hi(a, x_turned, sc1_in, sc1, xt_hi, xt_c, xt_hi_kept, qkv_done, 2)
                    if B:
                        keep_oT(b, 1)
                    if C:
                        gelus(c, 0, 3)
                    if A:
                        square(a, 0)
                        keep_v(a, 0, b)
                    if B:
                        keep_o_hi(b)
                    if A:
                        square(a, 1)
                        keep_v(a, 1, b)
                    if C:
                        gelus(c, 3, 6)
                    if A:
                        keep_qk_hi(a, 0)
                        keep_qk_hi(a, 1)
                    if C:
                        gelus(c, 6, 8)
                    if B:
                        keep_hi(b, ln2_turned, sc2_in, sc2, lt_hi, lt_c, lt_hi_kept, up_done, MT)
                    if C:
                        gelus(c, 8, 9)
                    if A:
                        keep_max(a, b)

                iterations(act, body)

            @block.vector
            def _(dve):
                def moments_of(n, src_in, src_count, src, st, mo, ve, stats_sem, var_sem, eps_sem):
                    dve.wait_ge(src_in, src_count * (n + 1))
                    for t in range(TT):
                        dve.bn_stats(st[:, t, :], src[:, t, :]).then_inc(stats_sem, 1)
                    dve.wait_ge(stats_sem, 2 * (n + 1))
                    dve.memset(waited[:, :], 0.0)
                    for t in range(TT):
                        dve.bn_aggr(mo[:, t, :], st[:, t, :]).then_inc(var_sem, 1)
                    dve.wait_ge(var_sem, 2 * (n + 1))
                    dve.tensor_scalar_add(ve[:, :], mo[:, :, 1], EPS).then_inc(eps_sem, 1)

                def normalise(n, src, mo, rs, rs_ready, dst, ready, turned):
                    dve.wait_ge(rs_ready, n + 1)
                    reuse(dve, turned, 1, n)
                    for t in range(TT):
                        dve.tensor_scalar(dst[:, t, 0:2 * P], src[:, t, 0:2 * P], mo[:, t, 0:1], rs[:, t:t + 1],
                                          ALU.subtract, ALU.mult).then_inc(ready, 1)
                        dve.tensor_scalar(dst[:, t, 2 * P:WIDE].rearrange("p (r n) -> p r n", r=3),
                                          src[:, t, None, 2 * P:HID].broadcast_to([P, 3, REST]), mo[:, t, 0:1], rs[:, t:t + 1],
                                          ALU.subtract, ALU.mult).then_inc(ready, 1)

                def keep_lo(n, scales, hi, lo, stacked, hi_kept, kept):
                    dve.wait_ge(hi_kept, 3 * n + 2)
                    for k in range(2):
                        dve.scalar_tensor_tensor(out=lo[:, k, :], in0=ps_s0[:, k * TOK:(k + 1) * TOK], scalar=scales[:, k:k + 1],
                                                 in1=hi[:, k, :].bitcast(F32), op0=ALU.mult, op1=ALU.subtract).then_inc(kept, 1)
                    dve.wait_ge(hi_kept, 3 * n + 3)
                    mid = slice(REST, 2 * REST)
                    dve.scalar_tensor_tensor(out=stacked[mid, :], in0=ps_s0[mid, 512:512 + TOK], scalar=scales[mid, 2:3],
                                             in1=stacked[mid, :].bitcast(F32), op0=ALU.mult, op1=ALU.subtract).then_inc(kept, 1)

                def keep_o_lo(b):
                    dve.wait_ge(ot_hi_kept, 2 * b + 1)
                    dve.tensor_tensor(ot_lo[:, :, :].rearrange("p k t -> p (k t)"), ps_s0[:, 0:512],
                                      ot_hi[:, :, :].rearrange("p k t -> p (k t)").bitcast(F32), ALU.subtract).then_inc(ot_lo_kept, 1)
                    dve.wait_ge(ot_hi_kept, 2 * b + 2)
                    mid = slice(REST, 2 * REST)
                    dve.tensor_tensor(ot_c[mid, :], ps_s0[mid, 512:512 + TOK], ot_c[mid, :].bitcast(F32), ALU.subtract).then_inc(ot_lo_kept, 1)

                def o_over_sum(b):
                    reuse(dve, o_turned, 1, b)
                    for t in range(TT):
                        dve.wait_ge(o_back, 2 * b + t + 1)
                        heads = ps_s1[:, t * 512:(t + 1) * 512].rearrange("p (h e) -> p h e", e=32)
                        dve.reciprocal(recip[:, t, :], heads[:, :, HD]).then_inc(recip_ready, 1)
                        dve.wait_ge(recip_ready, 2 * b + t + 1)
                        dve.tensor_tensor(o_n[:, t, 0:HID].rearrange("p (h d) -> p h d", d=HD), heads[:, :, 0:HD],
                                          recip[:, t, :, None].broadcast_to([P, NH, HD]), ALU.mult).then_inc(o_normed, 1)
                    dve.wait_ge(o_normed, 3 * b + 2)
                    dve.tensor_copy(o_n[:, :, HID:WIDE].rearrange("p t (r n) -> p t r n", r=2),
                                    o_n[:, :, None, 2 * P:HID].broadcast_to([P, TT, 2, REST])).then_inc(o_normed, 1)

                def sum_squares(a, t):
                    dve.wait_ge(squared, 2 * a + t + 1)
                    dve.tensor_reduce(ssq[:, t, :], squares[:, t, :].rearrange("p (h d) -> p h d", d=HD), AX.X, ALU.add).then_inc(ssq_ready, 1)

                def rsqrt(a):
                    flat = lambda u: u[:, :, :].rearrange("p t h -> p (t h)")
                    var, r, tmp = flat(qk_var), flat(qk_r), flat(qk_tmp)
                    step = [NEWTON * a]

                    def link(ins):
                        ins.then_inc(newton, 1)
                        step[0] = step[0] + 1
                        dve.wait_ge(newton, step[0])

                    dve.wait_ge(ssq_ready, 2 * (a + 1))
                    link(dve.tensor_scalar(var, flat(ssq), 1.0 / HD, EPS, ALU.mult, ALU.add))
                    link(dve.tensor_scalar(r.bitcast(I32), var.bitcast(I32), -0.5, RSQRT_SEED, ALU.mult, ALU.add))
                    for _ in range(3):
                        link(dve.scalar_tensor_tensor(out=tmp, in0=r, scalar=-0.5, in1=r, op0=ALU.mult, op1=ALU.mult))
                        link(dve.tensor_tensor(tmp, tmp, var, ALU.mult))
                        link(dve.scalar_tensor_tensor(out=r, in0=tmp, scalar=1.5, in1=r, op0=ALU.add, op1=ALU.mult))

                def norm_qk(a, t):
                    if t == 0:
                        reuse(dve, qk_lo_kept, 4, a)
                        reuse(dve, qk_hi_kept, 4, a)
                    qkv = ps_qkv[t][:, :].rearrange("p (c n) -> p c n", c=2)
                    heads = lambda u: u.rearrange("p (h d) -> p h d", d=HD)
                    dve.wait_ge(factor_ready, 2 * a + t + 1)
                    dve.wait_ge(v_kept, 2 * a + t + 1)
                    dve.tensor_tensor(heads(qk_n[:, t, 0, :]), heads(qkv[:, 0, 0:HID]), heads(q_factor[:, t, :]), ALU.mult).then_inc(qk_normed, 1)
                    dve.tensor_tensor(heads(qk_n[:, t, 1, :]), heads(qkv[:, 1, 0:HID]),
                                      qk_r[:, t, NH:2 * NH, None].broadcast_to([P, NH, HD]), ALU.mult).then_inc(qk_normed, 1)

                def keep_qk(a, t, b):
                    if b is not None and t == 0:
                        dve.wait_ge(scores_done, GROUPS * (b + 1))
                    src = ps_qkv[t][:, :].bitcast(F16)
                    for c, dst in ((0, qT), (1, kT)):
                        dve.wait_ge(qk_turned, 4 * a + 2 * t + c + 1)
                        dve.tensor_copy(dst[:, :, t * P:(t + 1) * P],
                                        src[:, c * 1024:(c + 1) * 1024].rearrange("p (j n) -> p j n", n=P)).then_inc(qk_kept, 1)

                def row_max(a, g):
                    quad, qt = g // 2, g % 2
                    dve.wait_ge(max_scores, GROUPS * a + g + 1)
                    dve.tensor_reduce(neg_max[:, qt, :, 2 * quad:2 * quad + 2],
                                      ps_qkv[g % 2][:, :].rearrange("p (a j n) -> p a j n", a=2, j=2), AX.X, ALU.max,
                                      negate=True).then_inc(max_done, 1)

                def split_max(a):
                    dve.wait_ge(max_done, GROUPS * (a + 1))
                    reuse(dve, max_turned, 1, a)
                    dve.tensor_copy(max_parts[:, :, :, 0, :], neg_max[:, :, :, :]).then_inc(max_split, 1)
                    dve.wait_ge(max_split, 2 * a + 1)
                    dve.tensor_tensor(max_parts[:, :, :, 1, :], neg_max[:, :, :, :], max_parts[:, :, :, 0, :], ALU.subtract).then_inc(max_split, 1)

                def gate(n, done, gate_in, src, g, dst, ready, used):
                    dve.wait_ge(gate_in, 16 * (n + 1))
                    reuse(dve, used, 2, n)
                    for t in range(TT):
                        dve.wait_ge(done, 2 * n + t + 1)
                        dve.tensor_tensor(dst[:, t, :], src[:, 512 * t:512 * t + HID], g[:, :], ALU.mult).then_inc(ready, 1)

                def body(a, b, c):
                    A, B, C = a is not None, b is not None, c is not None
                    if A:
                        moments_of(a, x_a_in, 16, x_a, stats, moments, var_eps, ln1_stats, ln1_var, ln1_eps)
                        normalise(a, x_a, moments, rstd, ln1_rstd, xhat, xhat_ready, x_turned)
                        dve.wait_ge(sc1_in, 16 * (a + 1))
                        keep_lo(a, sc1, xt_hi, xt_lo, xt_c, xt_hi_kept, xt_lo_kept)
                    if B:
                        o_over_sum(b)
                        keep_o_lo(b)
                    if A:
                        sum_squares(a, 0)
                        sum_squares(a, 1)
                        rsqrt(a)
                    if B:
                        gate(b, projected, gate1_in, ps_s0, gate1, gated1, gated1_ready, x1_ready)
                    if A:
                        norm_qk(a, 0)
                        norm_qk(a, 1)
                    if B:
                        moments_of(b, x1_ready, 2, x1_new, stats2, moments2, var_eps2, ln2_stats, ln2_var, ln2_eps)
                        normalise(b, x1_new, moments2, rstd2, ln2_rstd, xhat2, xhat2_ready, ln2_turned)
                    if A:
                        keep_qk(a, 0, b)
                        keep_qk(a, 1, b)
                    if B:
                        dve.wait_ge(sc2_in, 16 * (b + 1))
                        keep_lo(b, sc2, lt_hi, lt_lo, lt_c, lt_hi_kept, lt_lo_kept)
                    if A:
                        for g in range(GROUPS):
                            row_max(a, g)
                        split_max(a)
                    if C:
                        gate(c, down_done, gate2_in, ps_m, gate2, gated2, gated2_ready, y_ready)

                iterations(dve, body)

            @block.gpsimd
            def _(pool):
                def power(n, ve, eps_added, rs, ready):
                    pool.wait_ge(eps_added, n + 1)
                    pool.tensor_tensor(rs[:, :], ve[:, :], neg_half[:, :], ALU.pow).then_inc(ready, 1)

                def factor(a, t):
                    if t == 0:
                        pool.wait_ge(newton, NEWTON * (a + 1))
                    pool.tensor_tensor(q_factor[:, t, :].rearrange("p (h d) -> p h d", d=HD),
                                       qk_r[:, t, 0:NH, None].broadcast_to([P, NH, HD]),
                                       gain[:, None, :].broadcast_to([P, NH, HD]), ALU.mult).then_inc(factor_ready, 1)

                def keep_qk_lo(a, t):
                    for c, lo in ((0, 1), (1, 2)):
                        pool.wait_ge(qk_hi_kept, 4 * a + 2 * t + c + 1)
                        pool.tensor_tensor(stack[:, t, c, :, lo * HD:(lo + 1) * HD],
                                           qk_n[:, t, c, :].rearrange("p (h d) -> p h d", d=HD),
                                           stack[:, t, c, :, 0:HD], ALU.subtract).then_inc(qk_lo_kept, 1)

                def add_x(b):
                    pool.wait_ge(x_b_in, 16 * (b + 1))
                    reuse(pool, x1_moved, 16, b)
                    reuse(pool, xhat2_ready, 4, b)
                    for t in range(TT):
                        pool.wait_ge(gated1_ready, 2 * b + t + 1)
                        pool.tensor_tensor(x1_new[:, t, :], x_b[:, t, :], gated1[:, t, :], ALU.add).then_inc(x1_ready, 1)

                def keep_g_lo(c, m):
                    if m == 0:
                        reuse(pool, down_done, 2, c)
                    pool.wait_ge(g_hi_kept, MT * c + m + 1)
                    pool.tensor_tensor(g_lo[:, m, :], g_full[:, m, :], g_hi[:, m, :].bitcast(F32), ALU.subtract).then_inc(g_lo_kept, 1)

                def add_x1(c):
                    pool.wait_ge(x1_moved, 16 * (c + 1))
                    reuse(pool, out_stored, 16, c)
                    for t in range(TT):
                        pool.wait_ge(gated2_ready, 2 * c + t + 1)
                        pool.tensor_tensor(y[:, t, :], x1_c[:, t, :], gated2[:, t, :], ALU.add).then_inc(y_ready, 1)

                def body(a, b, c):
                    A, B, C = a is not None, b is not None, c is not None
                    if A:
                        power(a, var_eps, ln1_eps, rstd, ln1_rstd)
                    if C:
                        for m in range(0, 3):
                            keep_g_lo(c, m)
                    if A:
                        factor(a, 0)
                        factor(a, 1)
                    if B:
                        add_x(b)
                        power(b, var_eps2, ln2_eps, rstd2, ln2_rstd)
                    if A:
                        keep_qk_lo(a, 0)
                        keep_qk_lo(a, 1)
                    if C:
                        for m in range(3, MT):
                            keep_g_lo(c, m)
                        add_x1(c)

                iterations(pool, body)


_INS = ['x', 'cond_1152', 'L0_cond_w_mod', 'L0_cond_b_mod', 'L0_cond_w_qkv', 'L0_cond_b_qkv', 'L0_cond_g_q',
        'L0_cond_g_k', 'L0_cond_w_proj', 'L0_cond_b_proj', 'L0_cond_w1', 'L0_cond_b1', 'L0_cond_w2', 'L0_cond_b2']
_OUT = ((BATCH, TOK, HID), 'float32')


def kernel(**inputs):
    import numpy as _np
    import concourse.bacc as _bacc
    from concourse import mybir as _mybir
    from concourse.bass_utils import run_bass_kernel_spmd as _run

    nc = _bacc.Bacc("TRN2", target_bir_lowering=False, num_devices=1)
    arrays, args = {}, []
    for name in _INS:
        a = _np.ascontiguousarray(inputs[name])
        arrays[f"in_{name}_dram"] = a
        args.append(nc.dram_tensor(f"in_{name}_dram", a.shape, _mybir.dt.from_np(a.dtype), kind="ExternalInput").ap())
    shape, dtype = _OUT
    args.append(nc.dram_tensor("out_0_dram", shape, _mybir.dt.from_np(_np.dtype(dtype)), kind="ExternalOutput").ap())
    cond_block_kernel(nc, *args)
    r = _run(nc, [arrays], core_ids=[0])
    return r.results[0]["out_0_dram"]
```

```python
import concourse.bass as bass
from concourse import mybir
from contextlib import ExitStack

F32 = mybir.dt.float32
F32R = mybir.dt.float32r
F16 = mybir.dt.float16
I32 = mybir.dt.int32
ALU = mybir.AluOpType
ACT = mybir.ActivationFunctionType
AX = mybir.AxisListType

BATCH, TOK, HID = 16, 256, 288
NH, HD, MLP = 16, 18, 1152
P = 128
TT = TOK // P
REST = HID - 2 * P
MT = MLP // P
QUADS = NH // 4
GROUPS = 2 * QUADS
MAXIMA = 2 * GROUPS
HALF = (3 * HID) // 2
VH = HID // 2
SLOT = 64
MROW = 3 * HD
EPS = 1e-6
RSQRT_SEED = float(0x5F3759DF)

CB = 96
CK = CB + 2
WIDE = 2 * P + CB


def cond_block_kernel(nc, x, cond, w_mod, b_mod, w_qkv, b_qkv, g_q, g_k, w_proj, b_proj, w1, b1, w2, b2, out):
    ctx = ExitStack()
    with ctx:
        def sb(name, shape, dt=F32):
            return ctx.enter_context(nc.sbuf_tensor(name, shape, dt))

        def sem(name):
            return ctx.enter_context(nc.semaphore(name))

        gates_dram = nc.dram_tensor("gates_scratch", [BATCH, 2, HID], F32).ap()
        bias_dram = nc.dram_tensor("bias_scratch", [BATCH, 2, 3 * HID], F32).ap()

        wq_hi = sb("wq_hi", [P, 2, 2, HALF], F32R)
        wq_lo = sb("wq_lo", [P, 2, 2, HALF], F32R)
        wq_c = sb("wq_c", [P, 2, HALF], F32R)
        wp_hi = sb("wp_hi", [P, 2, HID], F32R)
        wp_lo = sb("wp_lo", [P, 2, HID], F32R)
        wp_c = sb("wp_c", [P, HID], F32R)
        w1_hi = sb("w1_hi", [P, 2, MLP], F32R)
        w1_lo = sb("w1_lo", [P, 2, MLP], F32R)
        w1_c = sb("w1_c", [P, MLP], F32R)
        w2_hi = sb("w2_hi", [P, MT, HID], F32R)
        w2_lo = sb("w2_lo", [P, MT, HID], F32R)
        w2_b = sb("w2_b", [2, HID], F32R)
        ones2 = sb("ones2", [2, P], F32R)

        ident = sb("ident", [P, P])
        ident16 = sb("ident16", [P, P], F16)
        neg_half = sb("neg_half", [P, TT])
        gain = sb("gain", [P, HD])
        score_scale = sb("score_scale", [P, 1])
        columns = sb("columns", [P, BATCH, 6 + MT])
        sc1 = sb("sc1", [P, 3])
        sc2 = sb("sc2", [P, 3])
        bias2 = sb("bias2", [P, MT])
        gate1 = sb("gate1", [P, HID])
        gate2 = sb("gate2", [P, HID])

        xt_c = sb("xt_c", [P, TOK], F32R)
        stack = sb("stack", [P, TT, 2, NH, SLOT], F16)
        v = sb("v", [P, TT, NH, 32])
        ot_c = sb("ot_c", [P, TOK], F32R)

        ps_s0 = ctx.enter_context(nc.psum_tensor("ps_s0", [P, 1024], F32))
        ps_s1 = ctx.enter_context(nc.psum_tensor("ps_s1", [P, 1024], F32))
        ps_o = ctx.enter_context(nc.psum_tensor("ps_o", [P, 1024], F32))
        ps_m = ctx.enter_context(nc.psum_tensor("ps_m", [P, 1024], F32))
        ps_s = (ps_s0, ps_s1)

        (x_a_in, bias_rows_in, sc1_in, x_b_in, gate1_in, sc2_in, gate2_in, bias2_in, x1_moved, out_stored,
         max_rows_in) = [sem(n) for n in (
             "x_a_in", "bias_rows_in", "sc1_in", "x_b_in", "gate1_in", "sc2_in", "gate2_in", "bias2_in",
             "x1_moved", "out_stored", "max_rows_in")]
        (ln1_stats, ln1_var, ln1_eps, ln1_rstd, xhat_ready, x_turned, xt_hi_kept, xt_lo_kept, qkv_done, squared,
         raw_kept, ssq_ready, newton, factor_ready, qk_normed, qk_hi_kept, qk_lo_kept, qk_turned, qk_kept,
         max_scores, max_done, max_split, max_turned, max_kept,
         v_spread) = [sem(n) for n in (
             "ln1_stats", "ln1_var", "ln1_eps", "ln1_rstd", "xhat_ready", "x_turned", "xt_hi_kept", "xt_lo_kept",
             "qkv_done", "squared", "raw_kept", "ssq_ready", "newton", "factor_ready", "qk_normed", "qk_hi_kept",
             "qk_lo_kept", "qk_turned", "qk_kept", "max_scores", "max_done", "max_split", "max_turned", "max_kept",
             "v_spread")]
        (scores_done, exps_done, pv_done, oT_kept, o_back, recip_ready, o_normed, o_turned, ot_hi_kept, ot_lo_kept,
         projected, gated1_ready, x1_ready, ln2_stats, ln2_var, ln2_eps, ln2_rstd, xhat2_ready, ln2_turned,
         lt_hi_kept, lt_lo_kept) = [sem(n) for n in (
             "scores_done", "exps_done", "pv_done", "oT_kept", "o_back", "recip_ready", "o_normed", "o_turned",
             "ot_hi_kept", "ot_lo_kept", "projected", "gated1_ready", "x1_ready", "ln2_stats", "ln2_var", "ln2_eps",
             "ln2_rstd", "xhat2_ready", "ln2_turned", "lt_hi_kept", "lt_lo_kept")]
        (up_done, gelu_done, g_hi_kept, g_lo_kept, down_done, gated2_ready, y_ready) = [sem(n) for n in (
            "up_done", "gelu_done", "g_hi_kept", "g_lo_kept", "down_done", "gated2_ready", "y_ready")]
        NEWTON = 11

        with ExitStack() as prep:
            def tmp(name, shape, dt=F32):
                return prep.enter_context(nc.sbuf_tensor(name, shape, dt))

            def tsem(name):
                return prep.enter_context(nc.semaphore(name))

            wm = tmp("wm", [P, 3, 2 * HID])
            wqs = tmp("wqs", [P, 3, 3 * HID])
            c_in = tmp("c_in", [BATCH, HID])
            c_e = tmp("c_e", [BATCH, HID])
            c_r = tmp("c_r", [BATCH, HID])
            c_s = tmp("c_s", [BATCH, HID])
            cT = tmp("cT", [P, 3, BATCH])
            sc_rest = tmp("sc_rest", [BATCH, 2, CB])
            gqk = tmp("gqk", [P, 2, HD])
            gprod = tmp("gprod", [P, HD])
            gmax = tmp("gmax", [P, 3])
            head_mean = tmp("head_mean", [P, 3, 2 * NH])
            bq_row = tmp("bq_row", [1, 3 * HID])
            bq_mean = tmp("bq_mean", [1, 2 * NH])
            b_rows = tmp("b_rows", [1, 2, HID])
            b_hi = tmp("b_hi", [1, 2, HID], F32R)
            b_lo = tmp("b_lo", [1, 2, HID], F32R)
            ones_row = tmp("ones_row", [1, BATCH])
            b1_cols = tmp("b1_cols", [P, MT])
            shT = tmp("shT", [P, 2, 3, BATCH])
            raw = tmp("w1_raw", [P, 2 * MLP])
            mod = tmp("mod", [BATCH, 6 * HID])
            bias_parts_hi = tmp("bias_parts_hi", [BATCH, 2, HALF], F32R)
            bias_parts_lo = tmp("bias_parts_lo", [BATCH, 2, HALF], F32R)
            w1_raw = raw[:, 0:2 * MLP].rearrange("p (k n) -> p k n", k=2)
            w1_rawc = tmp("w1_rawc", [CB, MLP])
            wp_raw = tmp("wp_raw", [P, 3, HID])
            w2_raw = tmp("w2_raw", [P, MT, HID])

            (c_loaded, wm_in, wq_in, w1_in, wp_in, w2_in, g_in, small_in, id_set, set_up, silu_e, silu,
             cT_turned, cT_kept, mod_done, mod_kept, gates_out, shT_turned, shT_kept, centred, brow_done, brow_kept,
             brow_out, b2_done, split_hi, split_lo, rows_hi, rows_lo, rows_in, gains, sc_rest_kept, w1_lo_done, wq_hi_done, ones_set) = [tsem(n) for n in (
                 "c_loaded", "wm_in", "wq_in", "w1_in", "wp_in", "w2_in", "g_in", "small_in", "id_set",
                 "set_up", "silu_e", "silu", "cT_turned", "cT_kept", "mod_done", "mod_kept", "gates_out",
                 "shT_turned", "shT_kept", "centred", "brow_done", "brow_kept", "brow_out", "b2_done", "split_hi",
                 "split_lo", "rows_hi", "rows_lo", "rows_in", "gains", "sc_rest_kept", "w1_lo_done",
                 "wq_hi_done", "ones_set")]

            with nc.Block() as block:
                @block.sync
                def _(sp):
                    sp.dma_start(c_in[:, :], cond).then_inc(c_loaded, 16)
                    for part in range(3):
                        if part:
                            sp.wait_ge(mod_done, 2 * part)
                        cols = slice(part * 2 * HID, (part + 1) * 2 * HID)
                        sp.dma_start(wm[:, 0:2, :], w_mod[0:2 * P, cols].rearrange("(k p) n -> p k n", p=P)).then_inc(wm_in, 16)
                        sp.dma_start(wm[0:REST, 2, :], w_mod[2 * P:HID, cols]).then_inc(wm_in, 16)
                        sp.dma_start(wm[REST:REST + 1, 2, :], b_mod[cols].rearrange("(a n) -> a n", a=1)).then_inc(wm_in, 16)
                        if part == 0:
                            sp.dma_start(w1_raw, w1[0:2 * P, :].rearrange("(k p) n -> p k n", p=P)).then_inc(w1_in, 16)
                            for r in range(3):
                                sp.dma_start(w1_rawc[r * REST:(r + 1) * REST, :], w1[2 * P:HID, :]).then_inc(w1_in, 16)
                    sp.wait_ge(mod_kept, 6)
                    for g, chunk in ((0, 2), (1, 5)):
                        sp.dma_start(gates_dram[:, g, :], mod[:, chunk * HID:(chunk + 1) * HID]).then_inc(gates_out, 16)
                    sp.wait_ge(brow_kept, 8)
                    sp.dma_start(bias_dram[:, 0, :], bias_parts_hi[:, :, :].rearrange("b c n -> b (c n)").bitcast(F32)).then_inc(brow_out, 16)
                    sp.dma_start(bias_dram[:, 1, :], bias_parts_lo[:, :, :].rearrange("b c n -> b (c n)").bitcast(F32)).then_inc(brow_out, 16)
                    sp.wait_ge(gates_out, 32)
                    sp.wait_ge(brow_out, 32)

                @block.scalar
                def _(act):
                    act.dma_start(wqs[:, 0:2, :], w_qkv[0:2 * P, :].rearrange("(k p) n -> p k n", p=P)).then_inc(wq_in, 16)
                    for r in range(3):
                        act.dma_start(wqs[r * REST:(r + 1) * REST, 2, :], w_qkv[2 * P:HID, :]).then_inc(wq_in, 16)
                    act.dma_start(gqk[:, 0, :], g_q.partition_broadcast(P)).then_inc(g_in, 16)
                    act.dma_start(gqk[:, 1, :], g_k.partition_broadcast(P)).then_inc(g_in, 16)
                    act.dma_start(bq_row[:, :], b_qkv.rearrange("(a n) -> a n", a=1)).then_inc(small_in, 16)
                    act.dma_start(b_rows[:, 0, :], b_proj.rearrange("(a n) -> a n", a=1)).then_inc(small_in, 16)
                    act.dma_start(b_rows[:, 1, :], b2.rearrange("(a n) -> a n", a=1)).then_inc(small_in, 16)
                    act.dma_start(b1_cols[:, :], b1.rearrange("(m p) -> p m", p=P), allow_slow_non_contiguous=True).then_inc(small_in, 16)
                    act.dma_start(wp_raw[:, 0:2, :], w_proj[0:2 * P, :].rearrange("(k p) n -> p k n", p=P)).then_inc(wp_in, 16)
                    for r in range(3):
                        act.dma_start(wp_raw[r * REST:(r + 1) * REST, 2, :], w_proj[2 * P:HID, :]).then_inc(wp_in, 16)
                    act.dma_start(w2_raw[:, :, :], w2.rearrange("(m p) n -> p m n", p=P)).then_inc(w2_in, 16)
                    act.wait_ge(c_loaded, 16)
                    act.activation(c_e[:, :], c_in[:, :], ACT.Exp, scale=-1.0).then_inc(silu_e, 1)
                    for n in range(6):
                        act.wait_ge(mod_done, n + 1)
                        act.activation(mod[:, n * HID:(n + 1) * HID], ps_s[n % 2][0:BATCH, 512 * (n // 2 % 2):512 * (n // 2 % 2) + HID],
                                       ACT.Copy).then_inc(mod_kept, 1)
                    act.wait_ge(w1_in, 64)
                    act.activation(w1_hi[:, :, :], w1_raw, ACT.Copy).then_inc(split_hi, 1)
                    act.activation(w1_c[0:CB, :], w1_rawc[:, :], ACT.Copy).then_inc(split_hi, 1)
                    act.wait_ge(wp_in, 64)
                    act.activation(wp_hi[:, :, :], wp_raw[:, 0:2, :], ACT.Copy).then_inc(split_hi, 1)
                    act.activation(wp_c[0:CB, :], wp_raw[0:CB, 2, :], ACT.Copy).then_inc(split_hi, 1)
                    act.wait_ge(w2_in, 16)
                    act.activation(w2_hi[:, :, :], w2_raw[:, :, :], ACT.Copy).then_inc(split_hi, 1)
                    act.wait_ge(rows_hi, 1)
                    act.wait_ge(rows_lo, 1)
                    act.dma_start(wp_c[CB:CB + 1, :].bitcast(F32), b_hi[:, 0, :].bitcast(F32)).then_inc(rows_in, 16)
                    act.dma_start(wp_c[CB + 1:CK, :].bitcast(F32), b_lo[:, 0, :].bitcast(F32)).then_inc(rows_in, 16)
                    act.dma_start(w2_b[0:1, :].bitcast(F32), b_hi[:, 1, :].bitcast(F32)).then_inc(rows_in, 16)
                    act.dma_start(w2_b[1:2, :].bitcast(F32), b_lo[:, 1, :].bitcast(F32)).then_inc(rows_in, 16)
                    act.wait_ge(rows_in, 64)

                @block.gpsimd
                def _(pool):
                    pool.memset(ident[:, :], 0.0).then_inc(id_set, 1)
                    pool.memset(ident16[:, :], 0.0).then_inc(id_set, 1)
                    pool.wait_ge(id_set, 2)
                    for n, m in enumerate((ident, ident16)):
                        pool.affine_select(out=m[:, :], in_=m[:, :], compare_op=ALU.not_equal, fill=1.0, base=0,
                                           pattern=[[-1, P]], channel_multiplier=1).then_inc(id_set, 1)
                    pool.memset(neg_half[:, :], -0.5).then_inc(set_up, 1)
                    pool.memset(v[:, :, :, HD:HD + 1], 1.0).then_inc(set_up, 1)
                    pool.memset(v[:, :, :, HD + 1:32], 0.0).then_inc(set_up, 1)
                    pool.memset(stack[:, :, 0, :, MROW:SLOT], 0.0).then_inc(set_up, 1)
                    pool.memset(stack[:, :, 1, :, MROW:MROW + 2], 1.0).then_inc(set_up, 1)
                    pool.memset(stack[:, :, 1, :, MROW + 2:SLOT], 0.0).then_inc(set_up, 1)
                    pool.wait_ge(set_up, 6)
                    pool.wait_ge(split_hi, 2)
                    pool.tensor_tensor(w1_lo[:, 0, :], w1_raw[:, 0, :], w1_hi[:, 0, :].bitcast(F32), ALU.subtract).then_inc(w1_lo_done, 1)
                    pool.wait_ge(w1_lo_done, 1)

                @block.vector
                def _(dve):
                    dve.memset(ones_row[:, :], 1.0).then_inc(ones_set, 1)
                    dve.memset(xt_c[CB:CK, :].bitcast(F32), 1.0)
                    dve.memset(ot_c[CB:CK, :].bitcast(F32), 1.0)
                    dve.memset(ones2[:, :].bitcast(F32), 1.0)
                    dve.memset(columns[CB:P, :, :], 0.0)
                    dve.memset(cT[REST:REST + 1, 2, :], 1.0).then_inc(ones_set, 1)
                    dve.wait_ge(silu_e, 1)
                    dve.tensor_scalar_add(c_r[:, :], c_e[:, :], 1.0).then_inc(silu, 1)
                    dve.wait_ge(silu, 1)
                    dve.reciprocal(c_e[:, :], c_r[:, :]).then_inc(silu, 1)
                    dve.wait_ge(silu, 2)
                    dve.tensor_tensor(c_s[:, :], c_in[:, :], c_e[:, :], ALU.mult).then_inc(silu, 1)
                    dve.wait_ge(cT_turned, 1)
                    dve.tensor_copy(cT[:, 0:2, :], ps_m[:, 0:2 * BATCH].rearrange("p (k b) -> p k b", k=2)).then_inc(cT_kept, 1)
                    dve.tensor_copy(cT[0:REST, 2, :], ps_m[0:REST, 2 * BATCH:3 * BATCH]).then_inc(cT_kept, 1)
                    dve.wait_ge(wq_in, 64)
                    for k, rows in ((0, P), (1, P), (2, CB)):
                        dve.tensor_reduce(head_mean[0:rows, k, :], wqs[0:rows, k, 0:2 * HID].rearrange("p (h d) -> p h d", d=HD),
                                          AX.X, ALU.add).then_inc(centred, 1)
                    dve.wait_ge(small_in, 64)
                    dve.tensor_reduce(bq_mean[:, :], bq_row[:, 0:2 * HID].rearrange("p (h d) -> p h d", d=HD),
                                      AX.X, ALU.add).then_inc(centred, 1)
                    dve.wait_ge(centred, 4)
                    for k, rows in ((0, P), (1, P), (2, CB)):
                        w = wqs[0:rows, k, 0:2 * HID].rearrange("p (h d) -> p h d", d=HD)
                        dve.scalar_tensor_tensor(out=w, in0=head_mean[0:rows, k, :, None].broadcast_to([rows, 2 * NH, HD]),
                                                 scalar=-1.0 / HD, in1=w, op0=ALU.mult, op1=ALU.add).then_inc(centred, 1)
                    w = bq_row[:, 0:2 * HID].rearrange("p (h d) -> p h d", d=HD)
                    dve.scalar_tensor_tensor(out=w, in0=bq_mean[:, :, None].broadcast_to([1, 2 * NH, HD]),
                                             scalar=-1.0 / HD, in1=w, op0=ALU.mult, op1=ALU.add).then_inc(centred, 1)
                    dve.wait_ge(centred, 8)
                    wq_moves = []
                    for k in range(2):
                        wq_moves.append((wq_hi[:, k, :, 0:HID], wq_lo[:, k, :, 0:HID], wqs[:, k, 0:2 * HID].rearrange("p (c n) -> p c n", c=2)))
                        wq_moves.append((wq_hi[:, k, :, HID:HALF], wq_lo[:, k, :, HID:HALF], wqs[:, k, 2 * HID:].rearrange("p (c n) -> p c n", c=2)))
                    for hi, lo, src in wq_moves:
                        dve.tensor_copy(hi, src).then_inc(wq_hi_done, 1)
                    qk_c = wqs[0:CB, 2, 0:2 * HID].rearrange("p (c n) -> p c n", c=2)
                    v_c = wqs[0:CB, 2, 2 * HID:].rearrange("p (c n) -> p c n", c=2)
                    dve.tensor_copy(wq_c[0:CB, :, 0:HID], qk_c).then_inc(wq_hi_done, 1)
                    dve.tensor_copy(wq_c[0:CB, :, HID:HALF], v_c).then_inc(wq_hi_done, 1)
                    dve.wait_ge(wq_hi_done, 6)
                    dve.wait_ge(split_hi, 5)
                    for hi, lo, src in wq_moves:
                        dve.tensor_tensor(lo, src, hi.bitcast(F32), ALU.subtract).then_inc(split_lo, 1)
                    for dst, src in ((wq_c[2 * REST:CB, :, 0:HID], qk_c[2 * REST:CB]), (wq_c[2 * REST:CB, :, HID:HALF], v_c[2 * REST:CB]),
                                     (w1_c[2 * REST:CB, :], w1_rawc[2 * REST:CB, :]), (wp_c[2 * REST:CB, :], wp_raw[2 * REST:CB, 2, :])):
                        dve.tensor_tensor(dst, src, dst.bitcast(F32), ALU.subtract).then_inc(split_lo, 1)
                    dve.tensor_tensor(w1_lo[:, 1, :], w1_raw[:, 1, :], w1_hi[:, 1, :].bitcast(F32), ALU.subtract).then_inc(split_lo, 1)
                    dve.tensor_tensor(wp_lo[:, :, :], wp_raw[:, 0:2, :], wp_hi[:, :, :].bitcast(F32), ALU.subtract).then_inc(split_lo, 1)
                    dve.tensor_tensor(w2_lo[:, :, :], w2_raw[:, :, :], w2_hi[:, :, :].bitcast(F32), ALU.subtract).then_inc(split_lo, 1)
                    dve.tensor_copy(b_hi[:, :, :], b_rows[:, :, :]).then_inc(rows_hi, 1)
                    dve.wait_ge(rows_hi, 1)
                    dve.tensor_tensor(b_lo[:, :, :], b_rows[:, :, :], b_hi[:, :, :].bitcast(F32), ALU.subtract).then_inc(rows_lo, 1)
                    dve.wait_ge(g_in, 32)
                    dve.tensor_tensor(gprod[:, :], gqk[:, 0, :], gqk[:, 1, :], ALU.mult).then_inc(gains, 1)
                    dve.wait_ge(gains, 1)
                    dve.tensor_reduce(gmax[:, 0:1], gprod[:, :], AX.X, ALU.max, apply_absolute_value=True).then_inc(gains, 1)
                    dve.wait_ge(gains, 2)
                    dve.tensor_scalar_max(gmax[:, 1:2], gmax[:, 0:1], 1e-30).then_inc(gains, 1)
                    dve.wait_ge(gains, 3)
                    dve.reciprocal(gmax[:, 2:3], gmax[:, 1:2]).then_inc(gains, 1)
                    dve.tensor_scalar_mul(score_scale[:, :], gmax[:, 1:2], float(HD) ** -0.5).then_inc(gains, 1)
                    dve.wait_ge(gains, 5)
                    dve.tensor_scalar(gain[:, :], gprod[:, :], gmax[:, 2:3], None, ALU.mult).then_inc(gains, 1)
                    dve.wait_ge(gains, 6)
                    dve.wait_ge(mod_kept, 6)
                    for s, chunk in enumerate((1, 4)):
                        rest = mod[:, None, chunk * HID + 2 * P:(chunk + 1) * HID].broadcast_to([BATCH, 3, REST])
                        dve.tensor_copy(sc_rest[:, s, :].rearrange("b (r n) -> b r n", r=3), rest).then_inc(sc_rest_kept, 1)
                    dve.wait_ge(shT_turned, 1)
                    turned = ps_m[:, 64:64 + 4 * 3 * BATCH].rearrange("p (s k b) -> p s k b", s=4, k=3)
                    for s in range(2):
                        dve.tensor_copy(shT[:, s, 0:2, :], turned[:, s, 0:2, :]).then_inc(shT_kept, 1)
                        dve.tensor_copy(shT[0:REST, s, 2, :], turned[0:REST, s, 2, :]).then_inc(shT_kept, 1)
                        cols = columns[:, :, 3 * s:3 * s + 3].rearrange("p b k -> p k b")
                        dve.tensor_scalar_add(cols[:, 0:2, :], turned[:, 2 + s, 0:2, :], 1.0).then_inc(shT_kept, 1)
                        dve.tensor_scalar_add(cols[0:CB, 2, :], turned[0:CB, 2 + s, 2, :], 1.0).then_inc(shT_kept, 1)
                    dve.wait_ge(brow_done, 1)
                    rows_ps = ps_o[0:BATCH, :].rearrange("b (c n) -> b c n", c=2)
                    qk_ps = ((rows_ps[:, 0, 0:HID], 0, 0), (rows_ps[:, 0, HID:HALF], 1, 0), (rows_ps[:, 1, 0:VH], 1, VH))
                    flat = ps_o[0:BATCH, :]
                    pieces = (
                        (bias_parts_hi[:, 0, 0:HID], bias_parts_lo[:, 0, 0:HID], flat[:, 0:HID]),
                        (bias_parts_hi[:, 1, 0:VH], bias_parts_lo[:, 1, 0:VH], flat[:, HID:HALF]),
                        (bias_parts_hi[:, 1, VH:HID], bias_parts_lo[:, 1, VH:HID], flat[:, 512:512 + VH]),
                        (bias_parts_hi[:, :, HID:HALF], bias_parts_lo[:, :, HID:HALF],
                         flat[:, 512 + VH:512 + HALF].rearrange("b (c n) -> b c n", c=2)))
                    for hi, lo, src in pieces:
                        dve.tensor_copy(hi, src).then_inc(brow_kept, 1)
                    dve.wait_ge(brow_kept, 4)
                    for n, (hi, lo, src) in enumerate(pieces):
                        dve.tensor_tensor(lo, src, hi.bitcast(F32), ALU.subtract).then_inc(brow_kept, 1)
                    dve.wait_ge(b2_done, 1)
                    dve.tensor_tensor(columns[:, :, 6:6 + MT].rearrange("p b m -> p m b"),
                                      ps_s1[:, 0:MT * BATCH].rearrange("p (m b) -> p m b", m=MT),
                                      b1_cols[:, :, None].broadcast_to([P, MT, BATCH]), ALU.add).then_inc(shT_kept, 1)
                    dve.wait_ge(shT_kept, 9)
                    dve.wait_ge(split_lo, 11)

                @block.tensor
                def _(pe):
                    pe.wait_ge(id_set, 4)
                    pe.wait_ge(silu, 3)
                    for k, w in ((0, P), (1, P), (2, REST)):
                        mm = pe.transpose(ps_m[0:w, k * BATCH:(k + 1) * BATCH], c_s[:, k * P:k * P + w], ident[0:BATCH, 0:BATCH])
                    mm.then_inc(cT_turned, 1)
                    pe.wait_ge(cT_kept, 2)
                    pe.wait_ge(ones_set, 2)
                    for part in range(3):
                        pe.wait_ge(wm_in, 48 * (part + 1))
                        for h in range(2):
                            n = 2 * part + h
                            if n >= 4:
                                pe.wait_ge(mod_kept, n - 3)
                            dst = ps_s[n % 2][0:BATCH, 512 * (n // 2 % 2):512 * (n // 2 % 2) + HID]
                            for k, rows in ((0, P), (1, P), (2, REST + 1)):
                                mm = pe.matmul(dst, cT[0:rows, k, :], wm[0:rows, k, h * HID:(h + 1) * HID],
                                               start=(k == 0), stop=(k == 2))
                            mm.then_inc(mod_done, 1)
                    pe.wait_ge(mod_kept, 6)
                    pe.wait_ge(sc_rest_kept, 2)
                    for s, chunk in enumerate((0, 3, 1, 4)):
                        for k, w in ((0, P), (1, P), (2, REST)):
                            src = mod[:, chunk * HID + k * P:chunk * HID + k * P + w]
                            if k == 2 and s >= 2:
                                src, w = sc_rest[:, s - 2, :], CB
                            col = 64 + (s * 3 + k) * BATCH
                            mm = pe.transpose(ps_m[0:w, col:col + BATCH], src, ident[0:BATCH, 0:BATCH])
                    mm.then_inc(shT_turned, 1)
                    pe.wait_ge(shT_kept, 8)
                    pe.wait_ge(centred, 8)
                    for half in range(2):
                        cols = slice(half * HALF, (half + 1) * HALF)
                        dst = ps_o[0:BATCH, 512 * half:512 * half + HALF]
                        for k, rows in ((0, P), (1, P), (2, REST)):
                            pe.matmul(dst, shT[0:rows, 0, k, :], wqs[0:rows, k, cols], start=(k == 0), stop=False)
                        mm = pe.matmul(dst, ones_row[:, :], bq_row[:, cols], start=False, stop=True)
                    mm.then_inc(brow_done, 1)
                    pe.wait_ge(w1_in, 64)
                    for m in range(MT):
                        cols = slice(m * P, (m + 1) * P)
                        for k, rows in ((0, P), (1, P), (2, REST)):
                            w = w1_raw[:, k, cols] if k < 2 else w1_rawc[0:REST, cols]
                            mm = pe.matmul(ps_s1[:, m * BATCH:(m + 1) * BATCH], w, shT[0:rows, 1, k, :], start=(k == 0), stop=(k == 2))
                    mm.then_inc(b2_done, 1)

        x_a = sb("x_a", [P, TT, HID])
        waited = sb("waited", [P, 1])
        stats = sb("stats", [P, TT, 6])
        moments = sb("moments", [P, TT, 2])
        var_eps = sb("var_eps", [P, TT])
        rstd = sb("rstd", [P, TT])
        xhat = sb("xhat", [P, TT, WIDE])
        xt_hi = sb("xt_hi", [P, 2, TOK], F32R)
        xt_lo = sb("xt_lo", [P, 2, TOK], F32R)
        qkv_raw = sb("qkv_raw", [P, TT, 2, HALF])
        squares = sb("squares", [P, TT, 2 * HID])
        ssq = sb("ssq", [P, TT, 2 * NH])
        qk_var = sb("qk_var", [P, TT, 2 * NH])
        qk_r = sb("qk_r", [P, TT, 2 * NH])
        qk_tmp = sb("qk_tmp", [P, TT, 2 * NH])
        q_factor = sb("q_factor", [P, TT, HID])
        qk_n = sb("qk_n", [P, TT, 2, HID])
        qT = sb("qT", [P, NH // 2, TOK], F16)
        kT = sb("kT", [P, NH // 2, TOK], F16)
        neg_max = sb("neg_max", [P, TT, 2, NH // 2])
        max_parts = sb("max_parts", [P, TT, 2, 2, NH // 2], F16)
        max_rows = sb("max_rows", [2 * NH, TOK], F16)

        x_b = sb("x_b", [P, TT, HID])
        probs = sb("probs", [P, 2, 4 * TOK])
        oT = sb("oT", [P, QUADS * TOK])
        recip = sb("recip", [P, TT, NH])
        o_n = sb("o_n", [P, TT, WIDE])
        ot_hi = sb("ot_hi", [P, 2, TOK], F32R)
        ot_lo = sb("ot_lo", [P, 2, TOK], F32R)
        gated1 = sb("gated1", [P, TT, HID])
        x1_new = sb("x1_new", [P, TT, HID])
        stats2 = sb("stats2", [P, TT, 6])
        moments2 = sb("moments2", [P, TT, 2])
        var_eps2 = sb("var_eps2", [P, TT])
        rstd2 = sb("rstd2", [P, TT])
        xhat2 = sb("xhat2", [P, TT, WIDE])
        lt_hi = sb("lt_hi", [P, 2, TOK], F32R)
        lt_lo = sb("lt_lo", [P, 2, TOK], F32R)
        lt_c = sb("lt_c", [P, TOK], F32R)

        x1_c = sb("x1_c", [P, TT, HID])
        g_full = sb("g_full", [P, MT, TOK])
        g_hi = sb("g_hi", [P, MT, TOK], F32R)
        g_lo = sb("g_lo", [P, MT, TOK], F32R)
        gated2 = sb("gated2", [P, TT, HID])
        y = sb("y", [P, TT, HID])

        def place(j):
            return (2 * (j % 2) + j // 2) * TOK

        def reuse(eng, semaphore, per_sequence, n):
            if not (isinstance(n, int) and n == 0):
                eng.wait_ge(semaphore, per_sequence * n)

        def iterations(eng, body):
            def some(i):
                body(*(n if 0 <= n < BATCH else None for n in (i + 2, i + 1, i, i - 1, i - 2)))

            for i in range(-2, 3):
                some(i)
            with eng.Fori(3, BATCH - 2) as i:
                body(i + 2, i + 1, i, i - 1, i - 2)
            for i in range(BATCH - 2, BATCH + 2):
                some(i)

        x_t = x.rearrange("b (t p) n -> b p t n", p=P)
        out_t = out.rearrange("b (t p) n -> b p t n", p=P)

        with nc.Block() as block:
            @block.sync
            def _(sp):
                def body(q, a, b, c, d):
                    if q is not None:
                        reuse(sp, xhat_ready, 4, q)
                        sp.dma_start(x_a[:, :, :], x_t[q]).then_inc(x_a_in, 16)
                        reuse(sp, xt_hi_kept, 3, q)
                        reuse(sp, xt_lo_kept, 3, q)
                        sp.dma_start(sc1[:, :], columns[:, q, 0:3]).then_inc(sc1_in, 16)
                        reuse(sp, qkv_done, 2, q)
                        sp.dma_start(wq_c[CB:CK, :, :].bitcast(F32), bias_dram[q].rearrange("r (c n) -> r c n", c=2)).then_inc(bias_rows_in, 16)
                    if d is not None:
                        reuse(sp, gated2_ready, 2, d)
                        sp.dma_start(gate2[:, :], gates_dram[d, 1, :].partition_broadcast(P)).then_inc(gate2_in, 16)
                    if b is not None:
                        reuse(sp, x1_ready, 2, b)
                        sp.dma_start(x_b[:, :, :], x_t[b]).then_inc(x_b_in, 16)
                        reuse(sp, gated1_ready, 2, b)
                        sp.dma_start(gate1[:, :], gates_dram[b, 0, :].partition_broadcast(P)).then_inc(gate1_in, 16)
                    if c is not None:
                        reuse(sp, lt_hi_kept, 3, c)
                        reuse(sp, lt_lo_kept, 3, c)
                        sp.dma_start(sc2[:, :], columns[:, c, 3:6]).then_inc(sc2_in, 16)
                        reuse(sp, gelu_done, MT, c)
                        sp.dma_start(bias2[:, :], columns[:, c, 6:6 + MT]).then_inc(bias2_in, 16)
                    if d is not None:
                        sp.wait_ge(y_ready, 2 * (d + 1))
                        sp.dma_start(out_t[d], y[:, :, :]).then_inc(out_stored, 16)
                    if c is not None:
                        sp.wait_ge(x1_ready, 2 * (c + 1))
                        sp.dma_start(x1_c[:, :, :], x1_new[:, :, :]).then_inc(x1_moved, 16)
                    if a is not None:
                        sp.wait_ge(max_kept, a + 1)
                        for parity in range(2):
                            for part in range(2):
                                row = SLOT * parity + MROW + part
                                at = NH * parity + NH // 2 * part
                                sp.dma_start(qT[row:row + 1, :, :], max_rows[at:at + NH // 2, :]).then_inc(max_rows_in, 16)

                iterations(sp, body)
                sp.wait_ge(out_stored, 16 * BATCH)

            @block.tensor
            def _(pe):
                def attend(a, b, filler):
                    def pv(g):
                        quad, kt = g // 2, g % 2
                        pe.wait_ge(exps_done, GROUPS * b + g + 1)
                        for j in range(4):
                            at = place(j)
                            mm = pe.matmul(ps_o[32 * j:32 * j + 32, quad * TOK:(quad + 1) * TOK], v[:, kt, 4 * quad + j, :],
                                           probs[:, g % 2, at:at + TOK], start=(kt == 0), stop=(kt == 1))
                        mm.then_inc(pv_done, 1)

                    filler(0)
                    pe.wait_ge(max_rows_in, 64 * (b + 1))
                    reuse(pe, gated1_ready, 2, b)
                    for g in range(GROUPS):
                        quad, kt = g // 2, g % 2
                        if g >= 2:
                            pe.wait_ge(exps_done, GROUPS * b + g - 1)
                        for j in range(4):
                            h = 4 * quad + j
                            at = SLOT * (h % 2)
                            mm = pe.matmul(ps_s[g % 2][:, place(j):place(j) + TOK], kT[at:at + MROW + 2, h // 2, kt * P:(kt + 1) * P],
                                           qT[at:at + MROW + 2, h // 2, :], start=True, stop=True)
                        mm.then_inc(scores_done, 1)
                        if g >= 1:
                            filler(g)
                        if g == 1:
                            pe.wait_ge(v_spread, b + 1)
                            if a is not None:
                                pe.wait_ge(raw_kept, 2 * (a + 1))
                        if g >= 1:
                            pv(g - 1)
                    pv(GROUPS - 1)

                def turn(src, dst):
                    for k in range(3):
                        for t in range(TT):
                            rows = P if k < 2 else CB
                            mm = pe.transpose(dst[0:rows, k * TOK + t * P:k * TOK + (t + 1) * P], src[:, t, k * P:k * P + rows], ident[:, :])
                    return mm

                def turn_x(q, b):
                    pe.wait_ge(xhat_ready, 4 * (q + 1))
                    reuse(pe, raw_kept, 2, q)
                    if b is not None:
                        pe.wait_ge(oT_kept, 2 * (b + 1))
                    turn(xhat, ps_o).then_inc(x_turned, 1)

                def qkv(q, t):
                    if t == 0:
                        pe.wait_ge(xt_hi_kept, 3 * (q + 1))
                        pe.wait_ge(xt_lo_kept, 3 * (q + 1))
                        pe.wait_ge(bias_rows_in, 16 * (q + 1))
                    else:
                        pe.wait_ge(raw_kept, 2 * q + 1)
                    tok = slice(t * P, (t + 1) * P)
                    for half in range(2):
                        dst = ps_o[:, 512 * half:512 * half + HALF]
                        for k in range(2):
                            pe.matmul(dst, xt_hi[:, k, tok], wq_hi[:, k, half, :], start=(k == 0), stop=False)
                            pe.matmul(dst, xt_hi[:, k, tok], wq_lo[:, k, half, :], start=False, stop=False)
                            pe.matmul(dst, xt_lo[:, k, tok], wq_hi[:, k, half, :], start=False, stop=False)
                        mm = pe.matmul(dst, xt_c[0:CK, tok], wq_c[0:CK, half, :], start=False, stop=True)
                    mm.then_inc(qkv_done, 1)

                def turn_qk(a, b, t):
                    pe.wait_ge(qk_hi_kept, 4 * a + 2 * t + 2)
                    pe.wait_ge(qk_lo_kept, 4 * a + 2 * t + 2)
                    if b is not None:
                        pe.wait_ge(exps_done, GROUPS * b + GROUPS - 1 + t)
                    dst = ps_s[t][:, :].bitcast(F16)
                    for c in range(2):
                        for j in range(NH // 2):
                            mm = pe.transpose(dst[:, c * 1024 + j * P:c * 1024 + (j + 1) * P],
                                              stack[:, t, c, 2 * j:2 * j + 2, :].rearrange("p h s -> p (h s)"), ident16[:, :])
                        mm.then_inc(qk_turned, 1)

                def maxima(a, first, last):
                    for u in range(first, last):
                        quad, qt, parity = u // 4, u // 2 % 2, u % 2
                        if u == 0:
                            pe.wait_ge(qk_kept, 4 * (a + 1))
                        if u >= 2:
                            pe.wait_ge(max_done, MAXIMA * a + u - 1)
                        at = SLOT * parity
                        for jj in range(2):
                            j = 2 * quad + jj
                            mm = pe.matmul(ps_s1[:, 512 * parity + jj * TOK:512 * parity + (jj + 1) * TOK],
                                           qT[at:at + MROW, j, qt * P:(qt + 1) * P], kT[at:at + MROW, j, :], start=True, stop=True)
                        mm.then_inc(max_scores, 1)

                def turn_max(a):
                    pe.wait_ge(max_split, 2 * (a + 1))
                    dst = ps_s1[:, :].bitcast(F16)
                    for t in range(TT):
                        mm = pe.transpose(dst[0:2 * NH, t * P:(t + 1) * P],
                                          max_parts[:, t].rearrange("p a s j -> p (a s j)"), ident16[:, :])
                    mm.then_inc(max_turned, 1)

                def turn_o_back(a, b):
                    pe.wait_ge(oT_kept, 2 * (b + 1))
                    pe.wait_ge(exps_done, GROUPS * (b + 1))
                    if a is not None:
                        pe.wait_ge(qk_kept, 4 * a + 2)
                    for t in range(TT):
                        for quad in range(QUADS):
                            mm = pe.transpose(ps_s0[:, t * 512 + quad * P:t * 512 + (quad + 1) * P],
                                              oT[:, quad * TOK + t * P:quad * TOK + (t + 1) * P], ident[:, :])
                        mm.then_inc(o_back, 1)

                def turn_o(b):
                    pe.wait_ge(o_normed, 3 * (b + 1))
                    turn(o_n, ps_s0).then_inc(o_turned, 1)

                def project(b):
                    pe.wait_ge(ot_hi_kept, 2 * (b + 1))
                    pe.wait_ge(ot_lo_kept, 2 * (b + 1))
                    for t in range(TT):
                        tok = slice(t * P, (t + 1) * P)
                        dst = ps_s0[:, 512 * t:512 * t + HID]
                        for k in range(2):
                            pe.matmul(dst, ot_hi[:, k, tok], wp_hi[:, k, :], start=(k == 0), stop=False)
                            pe.matmul(dst, ot_hi[:, k, tok], wp_lo[:, k, :], start=False, stop=False)
                            pe.matmul(dst, ot_lo[:, k, tok], wp_hi[:, k, :], start=False, stop=False)
                        pe.matmul(dst, ot_c[0:CK, tok], wp_c[0:CK, :], start=False, stop=True).then_inc(projected, 1)

                def turn_ln2(c):
                    pe.wait_ge(xhat2_ready, 4 * (c + 1))
                    reuse(pe, gated2_ready, 2, c)
                    turn(xhat2, ps_m).then_inc(ln2_turned, 1)

                def mlp_up(c, m):
                    if m == 0:
                        pe.wait_ge(lt_hi_kept, 3 * (c + 1))
                        pe.wait_ge(lt_lo_kept, 3 * (c + 1))
                    if m >= 2:
                        pe.wait_ge(gelu_done, MT * c + m - 1)
                    dst = ps_m[:, 512 * (m % 2):512 * (m % 2) + TOK]
                    cols = slice(m * P, (m + 1) * P)
                    for k in range(2):
                        pe.matmul(dst, w1_hi[:, k, cols], lt_hi[:, k, :], start=(k == 0), stop=False)
                        pe.matmul(dst, w1_hi[:, k, cols], lt_lo[:, k, :], start=False, stop=False)
                        pe.matmul(dst, w1_lo[:, k, cols], lt_hi[:, k, :], start=False, stop=False)
                    pe.matmul(dst, w1_c[0:CB, cols], lt_c[0:CB, :], start=False, stop=True).then_inc(up_done, 1)

                def mlp_down(c, first, last):
                    for n in range(first, last):
                        t, r = n // (3 * MT + 1), n % (3 * MT + 1)
                        dst = ps_m[:, 512 * t:512 * t + HID]
                        tok = slice(t * P, (t + 1) * P)
                        if r == 0:
                            if t == 0:
                                pe.wait_ge(gelu_done, MT * (c + 1))
                            pe.matmul(dst, ones2[:, :], w2_b[:, :], start=True, stop=False)
                            continue
                        m, part = (r - 1) // 3, (r - 1) % 3
                        if t == 0 and part == 0:
                            pe.wait_ge(g_hi_kept, MT * c + m + 1)
                        if t == 0 and part == 2:
                            pe.wait_ge(g_lo_kept, MT * c + m + 1)
                        g = g_lo if part == 2 else g_hi
                        w = w2_lo if part == 1 else w2_hi
                        mm = pe.matmul(dst, g[:, m, tok], w[:, m, :], start=False, stop=(r == 3 * MT))
                        if r == 3 * MT:
                            mm.then_inc(down_done, 1)

                PIECE = 2 * (3 * MT + 1) // GROUPS

                def body(q, a, b, c, d):
                    Q, A, B, C, D = (n is not None for n in (q, a, b, c, d))

                    def filler(g):
                        if D:
                            mlp_down(d, g * PIECE, (g + 1) * PIECE)

                    def up(first, last):
                        if C:
                            for m in range(first, last):
                                mlp_up(c, m)

                    def max_of(first, last):
                        if A:
                            maxima(a, first, last)

                    if B:
                        attend(a, b, filler)
                    else:
                        for g in range(GROUPS):
                            filler(g)
                    if A:
                        turn_qk(a, b, 0)
                    if Q:
                        turn_x(q, b)
                    if A:
                        turn_qk(a, b, 1)
                    if C:
                        turn_ln2(c)
                    if B:
                        turn_o_back(a, b)
                    if Q:
                        qkv(q, 0)
                    max_of(0, 2)
                    up(0, 2)
                    if B:
                        turn_o(b)
                    max_of(2, 4)
                    up(2, 3)
                    if B:
                        project(b)
                    max_of(4, 6)
                    if Q:
                        qkv(q, 1)
                    max_of(6, 8)
                    up(3, 4)
                    max_of(8, 10)
                    up(4, 5)
                    max_of(10, 12)
                    up(5, 6)
                    max_of(12, 16)
                    up(6, 7)
                    if A:
                        turn_max(a)
                    up(7, 9)

                iterations(pe, body)

            @block.scalar
            def _(act):
                def exps(b, g):
                    act.wait_ge(scores_done, GROUPS * b + g + 1)
                    if g >= 2:
                        act.wait_ge(pv_done, GROUPS * b + g - 1)
                    act.activation(probs[:, g % 2, :], ps_s[g % 2][:, :], ACT.Exp, scale=score_scale[:, 0:1]).then_inc(exps_done, 1)

                def keep_oT(b, half):
                    act.wait_ge(pv_done, GROUPS * b + 4 * half + 4)
                    if half == 0:
                        reuse(act, o_back, 2, b)
                    act.activation(oT[:, half * 512:(half + 1) * 512], ps_o[:, half * 512:(half + 1) * 512], ACT.Copy).then_inc(oT_kept, 1)

                def keep_hi(n, ps, turned, scales_in, scales, hi, stacked, kept, used, used_per):
                    act.wait_ge(turned, n + 1)
                    act.wait_ge(scales_in, 16 * (n + 1))
                    reuse(act, used, used_per, n)
                    for k in range(2):
                        act.activation(hi[:, k, :], ps[:, k * TOK:(k + 1) * TOK], ACT.Copy, scale=scales[:, k:k + 1]).then_inc(kept, 1)
                    act.activation(stacked[0:CB, :], ps[0:CB, 512:512 + TOK], ACT.Copy, scale=scales[0:CB, 2:3]).then_inc(kept, 1)

                def keep_o_hi(b):
                    act.wait_ge(o_turned, b + 1)
                    reuse(act, projected, 2, b)
                    act.activation(ot_hi[:, :, :].rearrange("p k t -> p (k t)"), ps_s0[:, 0:512], ACT.Copy).then_inc(ot_hi_kept, 1)
                    act.activation(ot_c[0:CB, :], ps_s0[0:CB, 512:512 + TOK], ACT.Copy).then_inc(ot_hi_kept, 1)

                def square(a, t):
                    act.wait_ge(raw_kept, 2 * a + t + 1)
                    reuse(act, ssq_ready, 2, a)
                    act.activation(squares[:, t, :].rearrange("p (c n) -> p c n", c=2), qkv_raw[:, t, :, 0:HID], ACT.Square).then_inc(squared, 1)

                def keep_raw(q, t):
                    act.wait_ge(qkv_done, 2 * q + t + 1)
                    if t == 0:
                        reuse(act, qk_normed, 4, q)
                        reuse(act, v_spread, 1, q)
                    act.activation(qkv_raw[:, t, :, :], ps_o[:, :].rearrange("p (c n) -> p c n", c=2)[:, :, 0:HALF], ACT.Copy).then_inc(raw_kept, 1)

                def keep_qk_hi(a, t):
                    if t == 0:
                        reuse(act, qk_turned, 4, a)
                    for c, second in ((0, 2), (1, 1)):
                        act.wait_ge(qk_normed, 4 * a + 2 * t + c + 1)
                        dst = stack[:, t, c, :, 0:MROW].rearrange("p h (s d) -> p h s d", d=HD)[:, :, 0:second + 1:second, :]
                        src = qk_n[:, t, c, :].rearrange("p (h d) -> p h d", d=HD)[:, :, None, :].broadcast_to([P, NH, 2, HD])
                        act.activation(dst, src, ACT.Copy).then_inc(qk_hi_kept, 1)

                def keep_max(a):
                    act.wait_ge(max_turned, a + 1)
                    reuse(act, max_rows_in, 64, a)
                    act.activation(max_rows[:, :], ps_s1[0:2 * NH, :].bitcast(F16)[:, 0:TOK], ACT.Copy).then_inc(max_kept, 1)

                def gelu(c, m):
                    if m == 0:
                        act.wait_ge(bias2_in, 16 * (c + 1))
                        reuse(act, g_lo_kept, MT, c)
                        reuse(act, down_done, 2, c)
                    act.wait_ge(up_done, MT * c + m + 1)
                    act.activation(g_full[:, m, :], ps_m[:, 512 * (m % 2):512 * (m % 2) + TOK], ACT.Gelu_apprx_tanh,
                                   bias=bias2[:, m:m + 1]).then_inc(gelu_done, 1)

                def keep_g_hi(c, m):
                    act.wait_ge(gelu_done, MT * c + m + 1)
                    act.activation(g_hi[:, m, :], g_full[:, m, :], ACT.Copy).then_inc(g_hi_kept, 1)

                def gelus(c, first, last):
                    for m in range(first, last):
                        gelu(c, m)
                        if m > first:
                            keep_g_hi(c, m - 1)
                    keep_g_hi(c, last - 1)

                def body(q, a, b, c, d):
                    Q, A, B, C, D = (n is not None for n in (q, a, b, c, d))
                    if A:
                        square(a, 0)
                        square(a, 1)
                    for g in range(GROUPS):
                        if B:
                            exps(b, g)
                        if B and g == 5:
                            keep_oT(b, 0)
                        if A and g in (3, 5):
                            keep_qk_hi(a, g // 5)
                    if B:
                        keep_oT(b, 1)
                    if Q:
                        keep_hi(q, ps_o, x_turned, sc1_in, sc1, xt_hi, xt_c, xt_hi_kept, qkv_done, 2)
                    if C:
                        keep_hi(c, ps_m, ln2_turned, sc2_in, sc2, lt_hi, lt_c, lt_hi_kept, up_done, MT)
                    if Q:
                        keep_raw(q, 0)
                    if C:
                        gelus(c, 0, 2)
                    if B:
                        keep_o_hi(b)
                    if C:
                        gelus(c, 2, 3)
                    if Q:
                        keep_raw(q, 1)
                    if C:
                        gelus(c, 3, 7)
                    if A:
                        keep_max(a)
                    if C:
                        gelus(c, 7, 9)

                iterations(act, body)

            @block.vector
            def _(dve):
                def moments_of(n, src_in, src_count, src, st, mo, ve, stats_sem, var_sem, eps_sem):
                    dve.wait_ge(src_in, src_count * (n + 1))
                    for t in range(TT):
                        dve.bn_stats(st[:, t, :], src[:, t, :]).then_inc(stats_sem, 1)
                    dve.wait_ge(stats_sem, 2 * (n + 1))
                    dve.memset(waited[:, :], 0.0)
                    for t in range(TT):
                        dve.bn_aggr(mo[:, t, :], st[:, t, :]).then_inc(var_sem, 1)
                    dve.wait_ge(var_sem, 2 * (n + 1))
                    dve.tensor_scalar_add(ve[:, :], mo[:, :, 1], EPS).then_inc(eps_sem, 1)

                def normalise(n, src, mo, rs, rs_ready, dst, ready, turned):
                    dve.wait_ge(rs_ready, n + 1)
                    reuse(dve, turned, 1, n)
                    for t in range(TT):
                        dve.tensor_scalar(dst[:, t, 0:2 * P], src[:, t, 0:2 * P], mo[:, t, 0:1], rs[:, t:t + 1],
                                          ALU.subtract, ALU.mult).then_inc(ready, 1)
                        dve.tensor_scalar(dst[:, t, 2 * P:WIDE].rearrange("p (r n) -> p r n", r=3),
                                          src[:, t, None, 2 * P:HID].broadcast_to([P, 3, REST]), mo[:, t, 0:1], rs[:, t:t + 1],
                                          ALU.subtract, ALU.mult).then_inc(ready, 1)

                def keep_lo(n, ps, scales, hi, lo, stacked, hi_kept, kept):
                    dve.wait_ge(hi_kept, 3 * n + 2)
                    for k in range(2):
                        dve.scalar_tensor_tensor(out=lo[:, k, :], in0=ps[:, k * TOK:(k + 1) * TOK], scalar=scales[:, k:k + 1],
                                                 in1=hi[:, k, :].bitcast(F32), op0=ALU.mult, op1=ALU.subtract).then_inc(kept, 1)
                    dve.wait_ge(hi_kept, 3 * n + 3)
                    mid = slice(REST, 2 * REST)
                    dve.scalar_tensor_tensor(out=stacked[mid, :], in0=ps[mid, 512:512 + TOK], scalar=scales[mid, 2:3],
                                             in1=stacked[mid, :].bitcast(F32), op0=ALU.mult, op1=ALU.subtract).then_inc(kept, 1)

                def keep_o_lo(b):
                    dve.wait_ge(ot_hi_kept, 2 * b + 1)
                    dve.tensor_tensor(ot_lo[:, :, :].rearrange("p k t -> p (k t)"), ps_s0[:, 0:512],
                                      ot_hi[:, :, :].rearrange("p k t -> p (k t)").bitcast(F32), ALU.subtract).then_inc(ot_lo_kept, 1)
                    dve.wait_ge(ot_hi_kept, 2 * b + 2)
                    mid = slice(REST, 2 * REST)
                    dve.tensor_tensor(ot_c[mid, :], ps_s0[mid, 512:512 + TOK], ot_c[mid, :].bitcast(F32), ALU.subtract).then_inc(ot_lo_kept, 1)

                def o_over_sum(b):
                    reuse(dve, o_turned, 1, b)
                    for t in range(TT):
                        dve.wait_ge(o_back, 2 * b + t + 1)
                        heads = ps_s0[:, t * 512:(t + 1) * 512].rearrange("p (h e) -> p h e", e=32)
                        dve.reciprocal(recip[:, t, :], heads[:, :, HD]).then_inc(recip_ready, 1)
                        dve.wait_ge(recip_ready, 2 * b + t + 1)
                        dve.tensor_tensor(o_n[:, t, 0:HID].rearrange("p (h d) -> p h d", d=HD), heads[:, :, 0:HD],
                                          recip[:, t, :, None].broadcast_to([P, NH, HD]), ALU.mult).then_inc(o_normed, 1)
                    dve.wait_ge(o_normed, 3 * b + 2)
                    dve.tensor_copy(o_n[:, :, HID:WIDE].rearrange("p t (r n) -> p t r n", r=2),
                                    o_n[:, :, None, 2 * P:HID].broadcast_to([P, TT, 2, REST])).then_inc(o_normed, 1)

                def sum_squares(a, t):
                    dve.wait_ge(squared, 2 * a + t + 1)
                    dve.tensor_reduce(ssq[:, t, :], squares[:, t, :].rearrange("p (h d) -> p h d", d=HD), AX.X, ALU.add).then_inc(ssq_ready, 1)

                def rsqrt(a):
                    flat = lambda u: u[:, :, :].rearrange("p t h -> p (t h)")
                    var, r, tmp = flat(qk_var), flat(qk_r), flat(qk_tmp)
                    step = [NEWTON * a]

                    def link(ins):
                        ins.then_inc(newton, 1)
                        step[0] = step[0] + 1
                        dve.wait_ge(newton, step[0])

                    dve.wait_ge(ssq_ready, 2 * (a + 1))
                    link(dve.tensor_scalar(var, flat(ssq), 1.0 / HD, EPS, ALU.mult, ALU.add))
                    link(dve.tensor_scalar(r.bitcast(I32), var.bitcast(I32), -0.5, RSQRT_SEED, ALU.mult, ALU.add))
                    for _ in range(3):
                        link(dve.scalar_tensor_tensor(out=tmp, in0=r, scalar=-0.5, in1=r, op0=ALU.mult, op1=ALU.mult))
                        link(dve.tensor_tensor(tmp, tmp, var, ALU.mult))
                        link(dve.scalar_tensor_tensor(out=r, in0=tmp, scalar=1.5, in1=r, op0=ALU.add, op1=ALU.mult))

                def norm_qk(a, t):
                    if t == 0:
                        reuse(dve, qk_lo_kept, 4, a)
                        reuse(dve, qk_hi_kept, 4, a)
                    heads = lambda u: u.rearrange("p (h d) -> p h d", d=HD)
                    dve.wait_ge(factor_ready, 2 * a + t + 1)
                    dve.tensor_tensor(heads(qk_n[:, t, 0, :]), heads(qkv_raw[:, t, 0, 0:HID]), heads(q_factor[:, t, :]), ALU.mult).then_inc(qk_normed, 1)
                    dve.tensor_tensor(heads(qk_n[:, t, 1, :]), heads(qkv_raw[:, t, 1, 0:HID]),
                                      qk_r[:, t, NH:2 * NH, None].broadcast_to([P, NH, HD]), ALU.mult).then_inc(qk_normed, 1)

                def keep_qk(a, t, b):
                    if b is not None and t == 0:
                        dve.wait_ge(scores_done, GROUPS * (b + 1))
                    src = ps_s[t][:, :].bitcast(F16)
                    for c, dst in ((0, qT), (1, kT)):
                        dve.wait_ge(qk_turned, 4 * a + 2 * t + c + 1)
                        dve.tensor_copy(dst[:, :, t * P:(t + 1) * P],
                                        src[:, c * 1024:(c + 1) * 1024].rearrange("p (j n) -> p j n", n=P)).then_inc(qk_kept, 1)

                def row_max(a, first, last):
                    for u in range(first, last):
                        quad, qt, parity = u // 4, u // 2 % 2, u % 2
                        dve.wait_ge(max_scores, MAXIMA * a + u + 1)
                        dve.tensor_reduce(neg_max[:, qt, parity, 2 * quad:2 * quad + 2],
                                          ps_s1[:, 512 * parity:512 * (parity + 1)].rearrange("p (j n) -> p j n", j=2), AX.X, ALU.max,
                                          negate=True).then_inc(max_done, 1)

                def spread_v(a, b):
                    if b is not None:
                        dve.wait_ge(pv_done, GROUPS * (b + 1))
                    for t in range(TT):
                        dve.wait_ge(raw_kept, 2 * a + t + 1)
                        ins = dve.tensor_copy(v[:, t, :, 0:HD].rearrange("p (c h) d -> p c h d", c=2),
                                              qkv_raw[:, t, :, HID:HALF].rearrange("p c (h d) -> p c h d", d=HD))
                    ins.then_inc(v_spread, 1)

                def split_max(a):
                    dve.wait_ge(max_done, MAXIMA * (a + 1))
                    reuse(dve, max_turned, 1, a)
                    dve.tensor_copy(max_parts[:, :, :, 0, :], neg_max[:, :, :, :]).then_inc(max_split, 1)
                    dve.wait_ge(max_split, 2 * a + 1)
                    dve.tensor_tensor(max_parts[:, :, :, 1, :], neg_max[:, :, :, :], max_parts[:, :, :, 0, :], ALU.subtract).then_inc(max_split, 1)

                def gate(n, t, done, gate_in, src, g, dst, ready, used):
                    if t == 0:
                        dve.wait_ge(gate_in, 16 * (n + 1))
                        reuse(dve, used, 2, n)
                    dve.wait_ge(done, 2 * n + t + 1)
                    dve.tensor_tensor(dst[:, t, :], src[:, 512 * t:512 * t + HID], g[:, :], ALU.mult).then_inc(ready, 1)

                def body(q, a, b, c, d):
                    Q, A, B, C, D = (n is not None for n in (q, a, b, c, d))
                    if A:
                        sum_squares(a, 0)
                        sum_squares(a, 1)
                        rsqrt(a)
                        norm_qk(a, 0)
                        norm_qk(a, 1)
                    if Q:
                        moments_of(q, x_a_in, 16, x_a, stats, moments, var_eps, ln1_stats, ln1_var, ln1_eps)
                    if D:
                        gate(d, 0, down_done, gate2_in, ps_m, gate2, gated2, gated2_ready, y_ready)
                    if Q:
                        normalise(q, x_a, moments, rstd, ln1_rstd, xhat, xhat_ready, x_turned)
                    if C:
                        moments_of(c, x1_ready, 2, x1_new, stats2, moments2, var_eps2, ln2_stats, ln2_var, ln2_eps)
                        normalise(c, x1_new, moments2, rstd2, ln2_rstd, xhat2, xhat2_ready, ln2_turned)
                    if D:
                        gate(d, 1, down_done, gate2_in, ps_m, gate2, gated2, gated2_ready, y_ready)

                    def max_of(first, last):
                        if A:
                            row_max(a, first, last)

                    if A:
                        keep_qk(a, 0, b)
                    if Q:
                        dve.wait_ge(sc1_in, 16 * (q + 1))
                        keep_lo(q, ps_o, sc1, xt_hi, xt_lo, xt_c, xt_hi_kept, xt_lo_kept)
                    if A:
                        spread_v(a, b)
                        keep_qk(a, 1, b)
                    if C:
                        dve.wait_ge(sc2_in, 16 * (c + 1))
                        keep_lo(c, ps_m, sc2, lt_hi, lt_lo, lt_c, lt_hi_kept, lt_lo_kept)
                    if B:
                        o_over_sum(b)
                    max_of(0, 2)
                    if B:
                        keep_o_lo(b)
                    max_of(2, 6)
                    if B:
                        gate(b, 0, projected, gate1_in, ps_s0, gate1, gated1, gated1_ready, x1_ready)
                        gate(b, 1, projected, gate1_in, ps_s0, gate1, gated1, gated1_ready, x1_ready)
                    max_of(6, 16)
                    if A:
                        split_max(a)

                iterations(dve, body)

            @block.gpsimd
            def _(pool):
                def power(n, ve, eps_added, rs, ready):
                    pool.wait_ge(eps_added, n + 1)
                    pool.tensor_tensor(rs[:, :], ve[:, :], neg_half[:, :], ALU.pow).then_inc(ready, 1)

                def factor(a, t):
                    if t == 0:
                        pool.wait_ge(newton, NEWTON * (a + 1))
                    pool.tensor_tensor(q_factor[:, t, :].rearrange("p (h d) -> p h d", d=HD),
                                       qk_r[:, t, 0:NH, None].broadcast_to([P, NH, HD]),
                                       gain[:, None, :].broadcast_to([P, NH, HD]), ALU.mult).then_inc(factor_ready, 1)

                def keep_qk_lo(a, t):
                    for c, lo in ((0, 1), (1, 2)):
                        pool.wait_ge(qk_hi_kept, 4 * a + 2 * t + c + 1)
                        pool.tensor_tensor(stack[:, t, c, :, lo * HD:(lo + 1) * HD],
                                           qk_n[:, t, c, :].rearrange("p (h d) -> p h d", d=HD),
                                           stack[:, t, c, :, 0:HD], ALU.subtract).then_inc(qk_lo_kept, 1)

                def add_x(b):
                    pool.wait_ge(x_b_in, 16 * (b + 1))
                    reuse(pool, x1_moved, 16, b)
                    reuse(pool, xhat2_ready, 4, b)
                    for t in range(TT):
                        pool.wait_ge(gated1_ready, 2 * b + t + 1)
                        pool.tensor_tensor(x1_new[:, t, :], x_b[:, t, :], gated1[:, t, :], ALU.add).then_inc(x1_ready, 1)

                def keep_g_lo(c, m):
                    if m == 0:
                        reuse(pool, down_done, 2, c)
                    pool.wait_ge(g_hi_kept, MT * c + m + 1)
                    pool.tensor_tensor(g_lo[:, m, :], g_full[:, m, :], g_hi[:, m, :].bitcast(F32), ALU.subtract).then_inc(g_lo_kept, 1)

                def add_x1(d):
                    pool.wait_ge(x1_moved, 16 * (d + 1))
                    reuse(pool, out_stored, 16, d)
                    for t in range(TT):
                        pool.wait_ge(gated2_ready, 2 * d + t + 1)
                        pool.tensor_tensor(y[:, t, :], x1_c[:, t, :], gated2[:, t, :], ALU.add).then_inc(y_ready, 1)

                def body(q, a, b, c, d):
                    Q, A, B, C, D = (n is not None for n in (q, a, b, c, d))
                    if A:
                        factor(a, 0)
                        factor(a, 1)
                        keep_qk_lo(a, 0)
                    if Q:
                        power(q, var_eps, ln1_eps, rstd, ln1_rstd)
                    if A:
                        keep_qk_lo(a, 1)
                    if C:
                        power(c, var_eps2, ln2_eps, rstd2, ln2_rstd)
                    if D:
                        add_x1(d)
                    if C:
                        for m in range(0, 4):
                            keep_g_lo(c, m)
                    if B:
                        add_x(b)
                    if C:
                        for m in range(4, MT):
                            keep_g_lo(c, m)

                iterations(pool, body)


_INS = ['x', 'cond_1152', 'L0_cond_w_mod', 'L0_cond_b_mod', 'L0_cond_w_qkv', 'L0_cond_b_qkv', 'L0_cond_g_q',
        'L0_cond_g_k', 'L0_cond_w_proj', 'L0_cond_b_proj', 'L0_cond_w1', 'L0_cond_b1', 'L0_cond_w2', 'L0_cond_b2']
_OUT = ((BATCH, TOK, HID), 'float32')


def kernel(**inputs):
    import numpy as _np
    import concourse.bacc as _bacc
    from concourse import mybir as _mybir
    from concourse.bass_utils import run_bass_kernel_spmd as _run

    nc = _bacc.Bacc("TRN2", target_bir_lowering=False, num_devices=1)
    arrays, args = {}, []
    for name in _INS:
        a = _np.ascontiguousarray(inputs[name])
        arrays[f"in_{name}_dram"] = a
        args.append(nc.dram_tensor(f"in_{name}_dram", a.shape, _mybir.dt.from_np(a.dtype), kind="ExternalInput").ap())
    shape, dtype = _OUT
    args.append(nc.dram_tensor("out_0_dram", shape, _mybir.dt.from_np(_np.dtype(dtype)), kind="ExternalOutput").ap())
    cond_block_kernel(nc, *args)
    r = _run(nc, [arrays], core_ids=[0])
    return r.results[0]["out_0_dram"]
```

```python
import concourse.bass as bass
from concourse import mybir
from contextlib import ExitStack

F32 = mybir.dt.float32
F32R = mybir.dt.float32r
F16 = mybir.dt.float16
I32 = mybir.dt.int32
ALU = mybir.AluOpType
ACT = mybir.ActivationFunctionType
AX = mybir.AxisListType

BATCH, TOK, HID = 16, 256, 288
NH, HD, MLP = 16, 18, 1152
P = 128
TT = TOK // P
REST = HID - 2 * P
MT = MLP // P
QUADS = NH // 4
GROUPS = 2 * QUADS
MAXIMA = 2 * GROUPS
HALF = (3 * HID) // 2
VH = HID // 2
SLOT = 64
MROW = 3 * HD
EPS = 1e-6
RSQRT_SEED = float(0x5F3759DF)

CB = 96
CK = CB + 2
THIRD = MLP // 3
WIDE = 2 * P + CB


def cond_block_kernel(nc, x, cond, w_mod, b_mod, w_qkv, b_qkv, g_q, g_k, w_proj, b_proj, w1, b1, w2, b2, out):
    ctx = ExitStack()
    with ctx:
        def sb(name, shape, dt=F32):
            return ctx.enter_context(nc.sbuf_tensor(name, shape, dt))

        def sem(name):
            return ctx.enter_context(nc.semaphore(name))

        gates_dram = nc.dram_tensor("gates_scratch", [BATCH, 2, HID], F32).ap()
        bias_dram = nc.dram_tensor("bias_scratch", [BATCH, 2, 3 * HID], F32).ap()

        wq_hi = sb("wq_hi", [P, 2, 2, HALF], F32R)
        wq_lo = sb("wq_lo", [P, 2, 2, HALF], F32R)
        wq_c = sb("wq_c", [P, 2, HALF], F32R)
        wp_hi = sb("wp_hi", [P, 2, HID], F32R)
        wp_lo = sb("wp_lo", [P, 2, HID], F32R)
        wp_c = sb("wp_c", [P, HID], F32R)
        w1_hi = sb("w1_hi", [P, 2, MLP], F32R)
        w1_lo = sb("w1_lo", [P, 2, MLP], F32R)
        w1_c = sb("w1_c", [P, MLP], F32R)
        w2_hi = sb("w2_hi", [P, MT, HID], F32R)
        w2_lo = sb("w2_lo", [P, MT, HID], F32R)
        w2_raw = sb("w2_raw", [P, MT, HID])
        w2_b = sb("w2_b", [2, HID], F32R)
        ones2 = sb("ones2", [2, P], F32R)

        ident = sb("ident", [P, P])
        ident16 = sb("ident16", [P, P], F16)
        neg_half = sb("neg_half", [P, TT])
        one = sb("one", [P, 1])
        gain = sb("gain", [P, HD])
        score_scale = sb("score_scale", [P, 1])
        columns = sb("columns", [P, BATCH, 6 + MT])
        sc1 = sb("sc1", [P, 3])
        sc2 = sb("sc2", [P, 3])
        bias2 = sb("bias2", [P, MT])
        b1_cols = sb("b1_cols", [P, MT])
        sh_hi = sb("sh_hi", [P, 2, BATCH], F32R)
        sh_lo = sb("sh_lo", [P, 2, BATCH], F32R)
        sh_c = sb("sh_c", [CB, BATCH], F32R)
        gate1 = sb("gate1", [P, HID])
        gate2 = sb("gate2", [P, HID])
        x_a = sb("x_a", [P, TT, HID])
        waited = sb("waited", [P, 1])
        warm = sb("warm", [1, 1])
        unused = sb("unused", [1, 1])

        xt_c = sb("xt_c", [P, TOK], F32R)
        stack = sb("stack", [P, TT, 2, NH, SLOT], F16)
        v = sb("v", [P, TT, NH, 32])
        ot_c = sb("ot_c", [P, TOK], F32R)

        ps_s0 = ctx.enter_context(nc.psum_tensor("ps_s0", [P, 1024], F32))
        ps_s1 = ctx.enter_context(nc.psum_tensor("ps_s1", [P, 1024], F32))
        ps_o = ctx.enter_context(nc.psum_tensor("ps_o", [P, 1024], F32))
        ps_m = ctx.enter_context(nc.psum_tensor("ps_m", [P, 1024], F32))
        ps_s = (ps_s0, ps_s1)

        (x_a_in, bias_rows_in, sc1_in, x_b_in, gate1_in, sc2_in, gate2_in, bias2_in, x1_moved, out_stored,
         max_rows_in) = [sem(n) for n in (
             "x_a_in", "bias_rows_in", "sc1_in", "x_b_in", "gate1_in", "sc2_in", "gate2_in", "bias2_in",
             "x1_moved", "out_stored", "max_rows_in")]
        (ln1_stats, ln1_var, ln1_eps, ln1_rstd, xhat_ready, x_turned, xt_hi_kept, xt_lo_kept, qkv_done, squared,
         raw_kept, ssq_ready, newton, factor_ready, qk_normed, qk_hi_kept, qk_lo_kept, qk_turned, qk_kept,
         max_scores, max_done, max_split, max_turned, max_kept,
         v_spread) = [sem(n) for n in (
             "ln1_stats", "ln1_var", "ln1_eps", "ln1_rstd", "xhat_ready", "x_turned", "xt_hi_kept", "xt_lo_kept",
             "qkv_done", "squared", "raw_kept", "ssq_ready", "newton", "factor_ready", "qk_normed", "qk_hi_kept",
             "qk_lo_kept", "qk_turned", "qk_kept", "max_scores", "max_done", "max_split", "max_turned", "max_kept",
             "v_spread")]
        (scores_done, exps_done, pv_done, oT_kept, o_back, recip_ready, o_normed, o_turned, ot_hi_kept, ot_lo_kept,
         projected, gated1_ready, x1_ready, ln2_stats, ln2_var, ln2_eps, ln2_rstd, xhat2_ready, ln2_turned,
         lt_hi_kept, lt_lo_kept) = [sem(n) for n in (
             "scores_done", "exps_done", "pv_done", "oT_kept", "o_back", "recip_ready", "o_normed", "o_turned",
             "ot_hi_kept", "ot_lo_kept", "projected", "gated1_ready", "x1_ready", "ln2_stats", "ln2_var", "ln2_eps",
             "ln2_rstd", "xhat2_ready", "ln2_turned", "lt_hi_kept", "lt_lo_kept")]
        (up_done, gelu_done, g_hi_kept, g_lo_kept, down_done, gated2_ready, y_ready) = [sem(n) for n in (
            "up_done", "gelu_done", "g_hi_kept", "g_lo_kept", "down_done", "gated2_ready", "y_ready")]
        (warm_set, gates_out, brow_out, columns_set, w2_in, w2_hi_done, w2_lo_done, bias2_done,
         bias2_set, bias2_kept, bias2_turned) = (sem(n) for n in (
             "warm_set", "gates_out", "brow_out", "columns_set", "w2_in", "w2_hi_done", "w2_lo_done", "bias2_done",
             "bias2_set", "bias2_kept", "bias2_turned"))
        THIRD_PIECES = ((ps_s0, 0), (ps_s0, 512), (ps_s1, 0))
        NEWTON = 11

        with ExitStack() as prep:
            def tmp(name, shape, dt=F32):
                return prep.enter_context(nc.sbuf_tensor(name, shape, dt))

            def tsem(name):
                return prep.enter_context(nc.semaphore(name))

            wm = tmp("wm", [P, 3, 6 * HID])
            wqs = tmp("wqs", [P, 3, 3 * HID])
            c_in = tmp("c_in", [BATCH, HID])
            e_T = tmp("e_T", [P, 3, BATCH])
            r_T = tmp("r_T", [P, 3, BATCH])
            cT = tmp("cT", [P, 3, BATCH])
            rest = tmp("rest", [BATCH, 3, CB])
            gqk = tmp("gqk", [P, 2, HD])
            gprod = tmp("gprod", [P, HD])
            gmax = tmp("gmax", [P, 3])
            head_mean = tmp("head_mean", [P, 3, 2 * NH])
            bq_row = tmp("bq_row", [1, 3 * HID])
            bq_mean = tmp("bq_mean", [1, 2 * NH])
            b_rows = tmp("b_rows", [1, 2, HID])
            b_hi = tmp("b_hi", [1, 2, HID], F32R)
            b_lo = tmp("b_lo", [1, 2, HID], F32R)
            ones_row = tmp("ones_row", [1, BATCH])
            shT = tmp("shT", [P, 3, BATCH])
            w1_raw = tmp("w1_raw", [P, 2, MLP])
            mod = tmp("mod", [BATCH, 6 * HID])
            bias_parts_hi = tmp("bias_parts_hi", [BATCH, 2, HALF], F32R)
            bias_parts_lo = tmp("bias_parts_lo", [BATCH, 2, HALF], F32R)
            w1_rawc = tmp("w1_rawc", [CB, MLP])
            wp_raw = tmp("wp_raw", [P, 3, HID])

            (c_loaded, wm_in_0, wm_in_1, wm_in_2, wq_in, w1_in, wp_in, g_in, bq_in, small_in, id_set, set_up, silu_e, silu,
             cT_turned, cT_kept, mod_done, mod_kept, sh_turned, shT_kept, centred, brow_done, brow_kept,
             w1_hi_done, wp_hi_done, split_lo, rows_hi, rows_lo, rows_in, gains, rest_kept, pool_lo_done,
             wq_hi_done, ones_set, sh_split) = [tsem(n) for n in (
                 "c_loaded", "wm_in_0", "wm_in_1", "wm_in_2", "wq_in", "w1_in", "wp_in", "g_in", "bq_in", "small_in",
                 "id_set", "set_up", "silu_e", "silu", "cT_turned", "cT_kept", "mod_done", "mod_kept",
                 "sh_turned", "shT_kept", "centred", "brow_done", "brow_kept", "w1_hi_done",
                 "wp_hi_done", "split_lo", "rows_hi", "rows_lo", "rows_in", "gains",
                 "rest_kept", "pool_lo_done", "wq_hi_done", "ones_set", "sh_split")]

            wm_in = (wm_in_0, wm_in_1, wm_in_2)
            SHIFT_SCALE = ((0, 1), (3, 4))

            with nc.Block() as block:
                @block.sync
                def _(sp):
                    def two_tiles(w):
                        return w[0:2 * P].rearrange("(k p) n -> p k n", p=P)

                    def last_rows(w):
                        return w[None, 2 * P:HID].broadcast_to([3, REST, w.shape[1]])

                    def load_wm(part):
                        cols = slice(part * 2 * HID, (part + 1) * 2 * HID)
                        sp.dma_start(wm[:, 0:2, cols], two_tiles(w_mod[:, cols])).then_inc(wm_in[part], 16)
                        sp.dma_start(wm[0:REST, 2, cols], w_mod[2 * P:HID, cols]).then_inc(wm_in[part], 16)

                    sp.dma_start(c_in[:, :], cond).then_inc(c_loaded, 16)
                    load_wm(0)
                    sp.dma_start(wm[REST:REST + 1, 2, :], b_mod.rearrange("(a n) -> a n", a=1)).then_inc(wm_in[0], 16)
                    sp.dma_start(wqs[:, 0:2, :], two_tiles(w_qkv)).then_inc(wq_in, 16)
                    sp.dma_start(wqs[0:CB, 2, :], last_rows(w_qkv)).then_inc(wq_in, 16)
                    load_wm(1)
                    sp.dma_start(wp_raw[:, 0:2, :], two_tiles(w_proj)).then_inc(wp_in, 16)
                    sp.dma_start(wp_raw[0:CB, 2, :], last_rows(w_proj)).then_inc(wp_in, 16)
                    sp.dma_start(w1_raw[:, :, :], two_tiles(w1)).then_inc(w1_in, 16)
                    sp.dma_start(w1_rawc[:, :], last_rows(w1)).then_inc(w1_in, 16)
                    load_wm(2)
                    sp.dma_start(w2_raw[:, :, :], w2.rearrange("(m p) n -> p m n", p=P)).then_inc(w2_in, 16)
                    sp.dma_start(x_a[:, :, :], x.rearrange("b (t p) n -> b p t n", p=P)[0]).then_inc(x_a_in, 16)
                    sp.wait_ge(rows_hi, 1)
                    sp.wait_ge(rows_lo, 1)
                    sp.dma_start(wp_c[CB:CB + 1, :].bitcast(F32), b_hi[:, 0, :].bitcast(F32)).then_inc(rows_in, 16)
                    sp.dma_start(wp_c[CB + 1:CK, :].bitcast(F32), b_lo[:, 0, :].bitcast(F32)).then_inc(rows_in, 16)
                    sp.dma_start(w2_b[0:1, :].bitcast(F32), b_hi[:, 1, :].bitcast(F32)).then_inc(rows_in, 16)
                    sp.dma_start(w2_b[1:2, :].bitcast(F32), b_lo[:, 1, :].bitcast(F32)).then_inc(rows_in, 16)
                    sp.wait_ge(brow_kept, 8)
                    sp.dma_start(bias_dram[:, 0, :], bias_parts_hi[:, :, :].rearrange("b c n -> b (c n)").bitcast(F32)).then_inc(brow_out, 16)
                    sp.dma_start(bias_dram[:, 1, :], bias_parts_lo[:, :, :].rearrange("b c n -> b (c n)").bitcast(F32)).then_inc(brow_out, 16)
                    sp.wait_ge(mod_kept, 6)
                    for g, chunk in ((0, 2), (1, 5)):
                        sp.dma_start(gates_dram[:, g, :], mod[:, chunk * HID:(chunk + 1) * HID]).then_inc(gates_out, 16)
                    sp.wait_ge(rows_in, 64)

                @block.scalar
                def _(act):
                    act.dma_start(bq_row[:, :], b_qkv.rearrange("(a n) -> a n", a=1)).then_inc(bq_in, 16)
                    act.wait_ge(warm_set, 1)
                    act.activation(unused[:, :], warm[:, :], ACT.Exp)
                    act.dma_start(gqk[:, 0, :], g_q.partition_broadcast(P)).then_inc(g_in, 16)
                    act.wait_ge(cT_turned, 1)
                    act.activation(e_T[:, 0:2, :], ps_m[:, 0:2 * BATCH].rearrange("p (k b) -> p k b", k=2), ACT.Exp, scale=-1.0).then_inc(silu_e, 1)
                    act.activation(e_T[0:REST, 2, :], ps_m[0:REST, 2 * BATCH:3 * BATCH], ACT.Exp, scale=-1.0).then_inc(silu_e, 1)
                    act.dma_start(gqk[:, 1, :], g_k.partition_broadcast(P)).then_inc(g_in, 16)
                    act.dma_start(b_rows[:, 0, :], b_proj.rearrange("(a n) -> a n", a=1)).then_inc(small_in, 16)
                    act.dma_start(b_rows[:, 1, :], b2.rearrange("(a n) -> a n", a=1)).then_inc(small_in, 16)
                    act.dma_start(b1_cols[:, :], b1.rearrange("(m p) -> p m", p=P), allow_slow_non_contiguous=True).then_inc(small_in, 16)

                    def keep_mod(n):
                        act.wait_ge(mod_done, n + 1)
                        act.activation(mod[:, n * HID:(n + 1) * HID], ps_s[n % 2][0:BATCH, 512 * (n // 2 % 2):512 * (n // 2 % 2) + HID],
                                       ACT.Copy).then_inc(mod_kept, 1)

                    keep_mod(0)
                    keep_mod(1)
                    keep_mod(2)
                    act.wait_ge(wp_in, 32)
                    act.activation(wp_hi[:, :, :], wp_raw[:, 0:2, :], ACT.Copy).then_inc(wp_hi_done, 1)
                    act.activation(wp_c[0:CB, :], wp_raw[0:CB, 2, :], ACT.Copy).then_inc(wp_hi_done, 1)
                    act.wait_ge(w1_in, 32)
                    act.activation(w1_hi[:, 0, :], w1_raw[:, 0, :], ACT.Copy).then_inc(w1_hi_done, 1)
                    act.activation(w1_hi[:, 1, :], w1_raw[:, 1, :], ACT.Copy).then_inc(w1_hi_done, 1)
                    act.activation(w1_c[0:CB, :], w1_rawc[:, :], ACT.Copy).then_inc(w1_hi_done, 1)
                    keep_mod(3)
                    keep_mod(4)
                    keep_mod(5)

                @block.gpsimd
                def _(pool):
                    pool.memset(ident[:, :], 0.0).then_inc(id_set, 1)
                    pool.memset(ident16[:, :], 0.0).then_inc(id_set, 1)
                    pool.wait_ge(id_set, 2)
                    for n, m in enumerate((ident, ident16)):
                        pool.affine_select(out=m[:, :], in_=m[:, :], compare_op=ALU.not_equal, fill=1.0, base=0,
                                           pattern=[[-1, P]], channel_multiplier=1).then_inc(id_set, 1)
                    pool.memset(neg_half[:, :], -0.5).then_inc(set_up, 1)
                    pool.memset(one[:, :], 1.0).then_inc(set_up, 1)
                    pool.memset(v[:, :, :, HD:HD + 1], 1.0).then_inc(set_up, 1)
                    pool.memset(v[:, :, :, HD + 1:32], 0.0).then_inc(set_up, 1)
                    pool.memset(stack[:, :, 0, :, MROW:SLOT], 0.0).then_inc(set_up, 1)
                    pool.memset(stack[:, :, 1, :, MROW:MROW + 2], 1.0).then_inc(set_up, 1)
                    pool.memset(stack[:, :, 1, :, MROW + 2:SLOT], 0.0).then_inc(set_up, 1)
                    pool.wait_ge(set_up, 7)
                    low = ((w1_hi_done, 1, w1_lo[:, 0, :], w1_raw[:, 0, :], w1_hi[:, 0, :]),
                           (w1_hi_done, 2, w1_lo[:, 1, :], w1_raw[:, 1, :], w1_hi[:, 1, :]))
                    for n, (hi_done, count, dst, src, hi) in enumerate(low):
                        pool.wait_ge(hi_done, count)
                        pool.tensor_tensor(dst, src, hi.bitcast(F32), ALU.subtract).then_inc(pool_lo_done, 1)
                        pool.wait_ge(pool_lo_done, n + 1)

                @block.vector
                def _(dve):
                    dve.memset(warm[:, :], 0.0).then_inc(warm_set, 1)
                    dve.memset(ones_row[:, :], 1.0).then_inc(ones_set, 1)
                    dve.memset(xt_c[CB:CK, :].bitcast(F32), 1.0)
                    dve.memset(ot_c[CB:CK, :].bitcast(F32), 1.0)
                    dve.memset(ones2[:, :].bitcast(F32), 1.0)
                    dve.memset(columns[CB:P, :, :], 0.0)
                    dve.memset(cT[REST:REST + 1, 2, :], 1.0).then_inc(ones_set, 1)
                    dve.wait_ge(silu_e, 2)
                    parts = ((e_T[:, 0:2, :], r_T[:, 0:2, :], ps_m[:, 0:2 * BATCH].rearrange("p (k b) -> p k b", k=2), cT[:, 0:2, :]),
                             (e_T[0:REST, 2, :], r_T[0:REST, 2, :], ps_m[0:REST, 2 * BATCH:3 * BATCH], cT[0:REST, 2, :]))
                    for e, _, _, _ in parts:
                        dve.tensor_scalar_add(e, e, 1.0).then_inc(silu, 1)
                    dve.wait_ge(silu, 2)
                    for e, inv, _, _ in parts:
                        dve.reciprocal(inv, e).then_inc(silu, 1)
                    dve.wait_ge(silu, 4)
                    for _, inv, c_ps, dst in parts:
                        dve.tensor_tensor(dst, c_ps, inv, ALU.mult).then_inc(cT_kept, 1)
                    dve.wait_ge(g_in, 32)
                    dve.tensor_tensor(gprod[:, :], gqk[:, 0, :], gqk[:, 1, :], ALU.mult).then_inc(gains, 1)
                    dve.wait_ge(gains, 1)
                    dve.tensor_reduce(gmax[:, 0:1], gprod[:, :], AX.X, ALU.max, apply_absolute_value=True).then_inc(gains, 1)
                    dve.wait_ge(gains, 2)
                    dve.tensor_scalar_max(gmax[:, 1:2], gmax[:, 0:1], 1e-30).then_inc(gains, 1)
                    dve.wait_ge(gains, 3)
                    dve.reciprocal(gmax[:, 2:3], gmax[:, 1:2]).then_inc(gains, 1)
                    dve.tensor_scalar_mul(score_scale[:, :], gmax[:, 1:2], float(HD) ** -0.5).then_inc(gains, 1)
                    dve.wait_ge(gains, 5)
                    dve.tensor_scalar(gain[:, :], gprod[:, :], gmax[:, 2:3], None, ALU.mult).then_inc(gains, 1)
                    dve.wait_ge(bq_in, 16)
                    dve.tensor_reduce(bq_mean[:, :], bq_row[:, 0:2 * HID].rearrange("p (h d) -> p h d", d=HD),
                                      AX.X, ALU.add).then_inc(centred, 1)
                    dve.wait_ge(centred, 1)
                    w = bq_row[:, 0:2 * HID].rearrange("p (h d) -> p h d", d=HD)
                    dve.scalar_tensor_tensor(out=w, in0=bq_mean[:, :, None].broadcast_to([1, 2 * NH, HD]),
                                             scalar=-1.0 / HD, in1=w, op0=ALU.mult, op1=ALU.add).then_inc(centred, 1)
                    dve.wait_ge(wq_in, 32)
                    for k, rows in ((0, P), (1, P), (2, CB)):
                        dve.tensor_reduce(head_mean[0:rows, k, :], wqs[0:rows, k, 0:2 * HID].rearrange("p (h d) -> p h d", d=HD),
                                          AX.X, ALU.add).then_inc(centred, 1)

                    def centre(k, rows):
                        w = wqs[0:rows, k, 0:2 * HID].rearrange("p (h d) -> p h d", d=HD)
                        dve.scalar_tensor_tensor(out=w, in0=head_mean[0:rows, k, :, None].broadcast_to([rows, 2 * NH, HD]),
                                                 scalar=-1.0 / HD, in1=w, op0=ALU.mult, op1=ALU.add).then_inc(centred, 1)

                    def repeat_rest(n, chunk):
                        dve.wait_ge(mod_kept, chunk + 1)
                        last = mod[:, None, chunk * HID + 2 * P:(chunk + 1) * HID].broadcast_to([BATCH, 3, REST])
                        dve.tensor_copy(rest[:, n, :].rearrange("b (r n) -> b r n", r=3), last).then_inc(rest_kept, 1)

                    turned = ps_m[:, 64:64 + 4 * 3 * BATCH].rearrange("p (s c k b) -> p s c k b", s=2, c=2, k=3)

                    def keep_scale(s):
                        cols = columns[:, :, 3 * s:3 * s + 3].rearrange("p b k -> p k b")
                        dve.tensor_scalar_add(cols[:, 0:2, :], turned[:, s, 1, 0:2, :], 1.0).then_inc(columns_set, 1)
                        dve.tensor_scalar_add(cols[0:CB, 2, :], turned[0:CB, s, 1, 2, :], 1.0).then_inc(columns_set, 1)

                    dve.wait_ge(centred, 5)
                    centre(0, P)
                    centre(1, P)
                    repeat_rest(0, 1)
                    centre(2, CB)
                    dve.wait_ge(sh_turned, 1)
                    dve.tensor_copy(shT[:, 0:2, :], turned[:, 0, 0, 0:2, :]).then_inc(shT_kept, 1)
                    dve.tensor_copy(shT[0:REST, 2, :], turned[0:REST, 0, 0, 2, :]).then_inc(shT_kept, 1)
                    keep_scale(0)
                    dve.wait_ge(centred, 8)
                    wq_moves = []
                    for k in range(2):
                        wq_moves.append((wq_hi[:, k, :, 0:HID], wq_lo[:, k, :, 0:HID], wqs[:, k, 0:2 * HID].rearrange("p (c n) -> p c n", c=2)))
                        wq_moves.append((wq_hi[:, k, :, HID:HALF], wq_lo[:, k, :, HID:HALF], wqs[:, k, 2 * HID:].rearrange("p (c n) -> p c n", c=2)))
                    for hi, lo, src in wq_moves:
                        dve.tensor_copy(hi, src).then_inc(wq_hi_done, 1)
                    qk_c = wqs[0:CB, 2, 0:2 * HID].rearrange("p (c n) -> p c n", c=2)
                    v_c = wqs[0:CB, 2, 2 * HID:].rearrange("p (c n) -> p c n", c=2)
                    dve.tensor_copy(wq_c[0:CB, :, 0:HID], qk_c).then_inc(wq_hi_done, 1)
                    dve.tensor_copy(wq_c[0:CB, :, HID:HALF], v_c).then_inc(wq_hi_done, 1)
                    dve.wait_ge(wq_hi_done, 6)
                    for hi, lo, src in wq_moves:
                        dve.tensor_tensor(lo, src, hi.bitcast(F32), ALU.subtract).then_inc(split_lo, 1)
                    for dst, src in ((wq_c[2 * REST:CB, :, 0:HID], qk_c[2 * REST:CB]), (wq_c[2 * REST:CB, :, HID:HALF], v_c[2 * REST:CB])):
                        dve.tensor_tensor(dst, src, dst.bitcast(F32), ALU.subtract).then_inc(split_lo, 1)
                    dve.wait_ge(small_in, 48)
                    dve.tensor_copy(b_hi[:, :, :], b_rows[:, :, :]).then_inc(rows_hi, 1)
                    dve.wait_ge(rows_hi, 1)
                    dve.tensor_tensor(b_lo[:, :, :], b_rows[:, :, :], b_hi[:, :, :].bitcast(F32), ALU.subtract).then_inc(rows_lo, 1)
                    dve.wait_ge(brow_done, 1)
                    flat = ps_o[0:BATCH, :]
                    pieces = (
                        (bias_parts_hi[:, 0, 0:HID], bias_parts_lo[:, 0, 0:HID], flat[:, 0:HID]),
                        (bias_parts_hi[:, 1, 0:VH], bias_parts_lo[:, 1, 0:VH], flat[:, HID:HALF]),
                        (bias_parts_hi[:, 1, VH:HID], bias_parts_lo[:, 1, VH:HID], flat[:, 512:512 + VH]),
                        (bias_parts_hi[:, :, HID:HALF], bias_parts_lo[:, :, HID:HALF],
                         flat[:, 512 + VH:512 + HALF].rearrange("b (c n) -> b c n", c=2)))
                    for hi, lo, src in pieces:
                        dve.tensor_copy(hi, src).then_inc(brow_kept, 1)
                    dve.wait_ge(brow_kept, 4)
                    for n, (hi, lo, src) in enumerate(pieces):
                        dve.tensor_tensor(lo, src, hi.bitcast(F32), ALU.subtract).then_inc(brow_kept, 1)
                    dve.wait_ge(wp_hi_done, 2)
                    dve.tensor_tensor(wp_lo[:, :, :], wp_raw[:, 0:2, :], wp_hi[:, :, :].bitcast(F32), ALU.subtract).then_inc(split_lo, 1)
                    dve.tensor_tensor(wp_c[2 * REST:CB, :], wp_raw[2 * REST:CB, 2, :], wp_c[2 * REST:CB, :].bitcast(F32), ALU.subtract).then_inc(split_lo, 1)
                    repeat_rest(1, 3)
                    repeat_rest(2, 4)
                    dve.wait_ge(w1_hi_done, 3)
                    dve.tensor_tensor(w1_c[2 * REST:CB, :], w1_rawc[2 * REST:CB, :], w1_c[2 * REST:CB, :].bitcast(F32), ALU.subtract).then_inc(split_lo, 1)
                    dve.wait_ge(sh_turned, 2)
                    keep_scale(1)
                    dve.tensor_copy(sh_hi[:, :, :], turned[:, 1, 0, 0:2, :]).then_inc(sh_split, 1)
                    dve.tensor_copy(sh_c[:, :], turned[0:CB, 1, 0, 2, :]).then_inc(sh_split, 1)
                    dve.wait_ge(sh_split, 2)
                    dve.tensor_tensor(sh_lo[:, :, :], turned[:, 1, 0, 0:2, :], sh_hi[:, :, :].bitcast(F32), ALU.subtract).then_inc(sh_split, 1)
                    mid = slice(REST, 2 * REST)
                    dve.tensor_tensor(sh_c[mid, :], turned[mid, 1, 0, 2, :], sh_c[mid, :].bitcast(F32), ALU.subtract).then_inc(sh_split, 1)
                    dve.wait_ge(sh_split, 4)
                    dve.wait_ge(columns_set, 4)
                    dve.wait_ge(gains, 6)
                    dve.wait_ge(split_lo, 9)

                @block.tensor
                def _(pe):
                    pe.wait_ge(id_set, 4)
                    pe.wait_ge(c_loaded, 16)
                    for k, w in ((0, P), (1, P), (2, REST)):
                        mm = pe.transpose(ps_m[0:w, k * BATCH:(k + 1) * BATCH], c_in[:, k * P:k * P + w], ident[0:BATCH, 0:BATCH])
                    mm.then_inc(cT_turned, 1)
                    pe.wait_ge(cT_kept, 2)
                    pe.wait_ge(ones_set, 2)
                    def modulate(n):
                        pe.wait_ge(wm_in[n // 2], 48 if n < 2 else 32)
                        if n >= 4:
                            pe.wait_ge(mod_kept, n - 3)
                        dst = ps_s[n % 2][0:BATCH, 512 * (n // 2 % 2):512 * (n // 2 % 2) + HID]
                        for k, rows in ((0, P), (1, P), (2, REST + 1)):
                            mm = pe.matmul(dst, cT[0:rows, k, :], wm[0:rows, k, n * HID:(n + 1) * HID], start=(k == 0), stop=(k == 2))
                        mm.then_inc(mod_done, 1)

                    def turn_mod(s):
                        pe.wait_ge(rest_kept, 2 * s + 1)
                        for c, chunk in enumerate(SHIFT_SCALE[s]):
                            for k, w in ((0, P), (1, P), (2, REST)):
                                src = mod[:, chunk * HID + k * P:chunk * HID + k * P + w]
                                if k == 2 and s + c > 0:
                                    src, w = rest[:, s + c - (1 - s), :], CB
                                col = 64 + ((2 * s + c) * 3 + k) * BATCH
                                mm = pe.transpose(ps_m[0:w, col:col + BATCH], src, ident[0:BATCH, 0:BATCH])
                        mm.then_inc(sh_turned, 1)

                    for n in range(3):
                        modulate(n)
                    turn_mod(0)
                    pe.wait_ge(shT_kept, 2)
                    pe.wait_ge(centred, 8)
                    for half in range(2):
                        cols = slice(half * HALF, (half + 1) * HALF)
                        dst = ps_o[0:BATCH, 512 * half:512 * half + HALF]
                        for k, rows in ((0, P), (1, P), (2, REST)):
                            pe.matmul(dst, shT[0:rows, k, :], wqs[0:rows, k, cols], start=(k == 0), stop=False)
                        mm = pe.matmul(dst, ones_row[:, :], bq_row[:, cols], start=False, stop=True)
                    mm.then_inc(brow_done, 1)
                    modulate(3)
                    modulate(4)
                    modulate(5)
                    pe.wait_ge(columns_set, 2)
                    turn_mod(1)

        stats = sb("stats", [P, TT, 6])
        moments = sb("moments", [P, TT, 2])
        var_eps = sb("var_eps", [P, TT])
        rstd = sb("rstd", [P, TT])
        xhat = sb("xhat", [P, TT, WIDE])
        xt_hi = sb("xt_hi", [P, 2, TOK], F32R)
        xt_lo = sb("xt_lo", [P, 2, TOK], F32R)
        qkv_raw = sb("qkv_raw", [P, TT, 2, HALF])
        squares = sb("squares", [P, TT, 2 * HID])
        ssq = sb("ssq", [P, TT, 2 * NH])
        qk_var = sb("qk_var", [P, TT, 2 * NH])
        qk_r = sb("qk_r", [P, TT, 2 * NH])
        qk_tmp = sb("qk_tmp", [P, TT, 2 * NH])
        q_factor = sb("q_factor", [P, TT, HID])
        qk_n = sb("qk_n", [P, TT, 2, HID])
        qT = sb("qT", [P, NH // 2, TOK], F16)
        kT = sb("kT", [P, NH // 2, TOK], F16)
        neg_max = sb("neg_max", [P, TT, 2, NH // 2])
        max_parts = sb("max_parts", [P, TT, 2, 2, NH // 2], F16)
        max_rows = sb("max_rows", [2 * NH, TOK], F16)

        x_b = sb("x_b", [P, TT, HID])
        probs = sb("probs", [P, 2, 4 * TOK])
        oT = sb("oT", [P, QUADS * TOK])
        recip = sb("recip", [P, TT, NH])
        o_n = sb("o_n", [P, TT, WIDE])
        ot_hi = sb("ot_hi", [P, 2, TOK], F32R)
        ot_lo = sb("ot_lo", [P, 2, TOK], F32R)
        gated1 = sb("gated1", [P, TT, HID])
        x1_new = sb("x1_new", [P, TT, HID])
        stats2 = sb("stats2", [P, TT, 6])
        moments2 = sb("moments2", [P, TT, 2])
        var_eps2 = sb("var_eps2", [P, TT])
        rstd2 = sb("rstd2", [P, TT])
        xhat2 = sb("xhat2", [P, TT, WIDE])
        lt_hi = sb("lt_hi", [P, 2, TOK], F32R)
        lt_lo = sb("lt_lo", [P, 2, TOK], F32R)
        lt_c = sb("lt_c", [P, TOK], F32R)

        x1_c = sb("x1_c", [P, TT, HID])
        g_full = sb("g_full", [P, MT, TOK])
        bias2_rows = g_full[0:BATCH, :, :].rearrange("p m t -> p (m t)")[:, 0:MLP]
        g_hi = sb("g_hi", [P, MT, TOK], F32R)
        g_lo = sb("g_lo", [P, MT, TOK], F32R)
        gated2 = sb("gated2", [P, TT, HID])
        y = sb("y", [P, TT, HID])

        def place(j):
            return (2 * (j % 2) + j // 2) * TOK

        def is_last(n):
            return isinstance(n, int) and n == BATCH - 1

        def ps_up(c):
            return ps_o if is_last(c) else ps_m

        def reuse(eng, semaphore, per_sequence, n):
            if not (isinstance(n, int) and n == 0):
                eng.wait_ge(semaphore, per_sequence * n)

        def iterations(eng, body):
            def some(i):
                body(*(n if 0 <= n < BATCH else None for n in (i + 3, i + 2, i + 1, i, i - 1, i - 2)))

            for i in range(-3, 3):
                some(i)
            with eng.Fori(3, BATCH - 3) as i:
                body(i + 3, i + 2, i + 1, i, i - 1, i - 2)
            for i in range(BATCH - 3, BATCH + 2):
                some(i)

        x_t = x.rearrange("b (t p) n -> b p t n", p=P)
        out_t = out.rearrange("b (t p) n -> b p t n", p=P)

        with nc.Block() as block:
            @block.sync
            def _(sp):
                def body(l, q, a, b, c, d):
                    if isinstance(q, int) and q == 0:
                        sp.wait_ge(brow_out, 32)
                    if isinstance(b, int) and b == 0:
                        sp.wait_ge(gates_out, 32)
                    if isinstance(c, int) and c == 0:
                        sp.wait_ge(bias2_set, 1)
                    if q is not None:
                        reuse(sp, xt_hi_kept, 3, q)
                        reuse(sp, xt_lo_kept, 3, q)
                        sp.dma_start(sc1[:, :], columns[:, q, 0:3]).then_inc(sc1_in, 16)
                        reuse(sp, qkv_done, 2, q)
                        sp.dma_start(wq_c[CB:CK, :, :].bitcast(F32), bias_dram[q].rearrange("r (c n) -> r c n", c=2)).then_inc(bias_rows_in, 16)
                    if d is not None:
                        reuse(sp, gated2_ready, 2, d)
                        sp.dma_start(gate2[:, :], gates_dram[d, 1, :].partition_broadcast(P)).then_inc(gate2_in, 16)
                    if b is not None:
                        reuse(sp, x1_ready, 2, b)
                        sp.dma_start(x_b[:, :, :], x_t[b]).then_inc(x_b_in, 16)
                        reuse(sp, gated1_ready, 2, b)
                        sp.dma_start(gate1[:, :], gates_dram[b, 0, :].partition_broadcast(P)).then_inc(gate1_in, 16)
                    if c is not None:
                        reuse(sp, lt_hi_kept, 3, c)
                        reuse(sp, lt_lo_kept, 3, c)
                        sp.dma_start(sc2[:, :], columns[:, c, 3:6]).then_inc(sc2_in, 16)
                        reuse(sp, gelu_done, MT, c)
                        sp.dma_start(bias2[:, :], columns[:, c, 6:6 + MT]).then_inc(bias2_in, 16)
                    if d is not None:
                        sp.wait_ge(y_ready, 2 * (d + 1))
                        sp.dma_start(out_t[d], y[:, :, :]).then_inc(out_stored, 16)
                    if c is not None:
                        sp.wait_ge(x1_ready, 2 * (c + 1))
                        sp.dma_start(x1_c[:, :, :], x1_new[:, :, :]).then_inc(x1_moved, 16)
                    if l is not None and not (isinstance(l, int) and l == 0):
                        reuse(sp, xhat_ready, 4, l)
                        sp.dma_start(x_a[:, :, :], x_t[l]).then_inc(x_a_in, 16)
                    if a is not None:
                        sp.wait_ge(max_kept, a + 1)
                        for parity in range(2):
                            row = SLOT * parity + MROW
                            sp.dma_start(qT[row:row + 2, :, :], max_rows[NH * parity:NH * (parity + 1), :]).then_inc(max_rows_in, 16)

                iterations(sp, body)
                sp.wait_ge(out_stored, 16 * BATCH)

            @block.tensor
            def _(pe):
                def attend(a, b, filler):
                    def pv(g):
                        quad, kt = g // 2, g % 2
                        pe.wait_ge(exps_done, GROUPS * b + g + 1)
                        for j in range(4):
                            at = place(j)
                            mm = pe.matmul(ps_o[32 * j:32 * j + 32, quad * TOK:(quad + 1) * TOK], v[:, kt, 4 * quad + j, :],
                                           probs[:, g % 2, at:at + TOK], start=(kt == 0), stop=(kt == 1))
                        mm.then_inc(pv_done, 1)

                    filler(0)
                    pe.wait_ge(max_rows_in, 32 * (b + 1))
                    reuse(pe, gated1_ready, 2, b)
                    for g in range(GROUPS):
                        quad, kt = g // 2, g % 2
                        if g >= 2:
                            pe.wait_ge(exps_done, GROUPS * b + g - 1)
                        for j in range(4):
                            h = 4 * quad + j
                            at = SLOT * (h % 2)
                            mm = pe.matmul(ps_s[g % 2][:, place(j):place(j) + TOK], kT[at:at + MROW + 2, h // 2, kt * P:(kt + 1) * P],
                                           qT[at:at + MROW + 2, h // 2, :], start=True, stop=True)
                        mm.then_inc(scores_done, 1)
                        if g == 1:
                            filler(1)
                            filler(2)
                        if g >= 3:
                            filler(g)
                        if g == 1:
                            pe.wait_ge(v_spread, 2 * (b + 1))
                            if a is not None:
                                pe.wait_ge(raw_kept, 2 * (a + 1))
                        if g >= 1:
                            pv(g - 1)
                    pv(GROUPS - 1)

                def turn(src, dst):
                    for k in range(3):
                        for t in range(TT):
                            rows = P if k < 2 else CB
                            mm = pe.transpose(dst[0:rows, k * TOK + t * P:k * TOK + (t + 1) * P], src[:, t, k * P:k * P + rows], ident[:, :])
                    return mm

                def turn_x(q, b):
                    if isinstance(q, int) and q == 0:
                        keep_warm(11)
                    pe.wait_ge(xhat_ready, 4 * (q + 1))
                    reuse(pe, raw_kept, 2, q)
                    if b is not None:
                        pe.wait_ge(oT_kept, 2 * (b + 1))
                    turn(xhat, ps_o).then_inc(x_turned, 1)

                def qkv(q, t, half):
                    if t == 0 and half == 1:
                        if isinstance(q, int) and q == 0:
                            keep_warm(10)
                        pe.wait_ge(xt_hi_kept, 3 * (q + 1))
                        pe.wait_ge(xt_lo_kept, 3 * q + 1)
                    if t == 1 and half == 1:
                        pe.wait_ge(raw_kept, 2 * q + 1)
                    tok = slice(t * P, (t + 1) * P)
                    dst = ps_o[:, 512 * half:512 * half + HALF]
                    for k in range(2):
                        pe.matmul(dst, xt_hi[:, k, tok], wq_hi[:, k, half, :], start=(k == 0), stop=False)
                        pe.matmul(dst, xt_hi[:, k, tok], wq_lo[:, k, half, :], start=False, stop=False)
                    if t == 0 and half == 1:
                        pe.wait_ge(xt_lo_kept, 3 * (q + 1))
                        pe.wait_ge(bias_rows_in, 16 * (q + 1))
                    for k in range(2):
                        pe.matmul(dst, xt_lo[:, k, tok], wq_hi[:, k, half, :], start=False, stop=False)
                    mm = pe.matmul(dst, xt_c[0:CK, tok], wq_c[0:CK, half, :], start=False, stop=True)
                    if half == 0:
                        mm.then_inc(qkv_done, 1)

                def turn_qk(a, b, t):
                    pe.wait_ge(qk_hi_kept, 4 * a + 2 * t + 2)
                    pe.wait_ge(qk_lo_kept, 4 * a + 2 * t + 2)
                    if b is not None:
                        pe.wait_ge(exps_done, GROUPS * b + GROUPS - 1 + t)
                    dst = ps_s[t][:, :].bitcast(F16)
                    for c in range(2):
                        for j in range(NH // 2):
                            mm = pe.transpose(dst[:, c * 1024 + j * P:c * 1024 + (j + 1) * P],
                                              stack[:, t, c, 2 * j:2 * j + 2, :].rearrange("p h s -> p (h s)"), ident16[:, :])
                        mm.then_inc(qk_turned, 1)

                def maxima(a, first, last):
                    for u in range(first, last):
                        quad, qt, parity = u // 4, u // 2 % 2, u % 2
                        if u == 0:
                            pe.wait_ge(qk_kept, 4 * (a + 1))
                        if u >= 2:
                            pe.wait_ge(max_done, MAXIMA * a + u - 1)
                        at = SLOT * parity
                        for jj in range(2):
                            j = 2 * quad + jj
                            mm = pe.matmul(ps_s1[:, 512 * parity + jj * TOK:512 * parity + (jj + 1) * TOK],
                                           qT[at:at + MROW, j, qt * P:(qt + 1) * P], kT[at:at + MROW, j, :], start=True, stop=True)
                        mm.then_inc(max_scores, 1)

                def turn_max(a):
                    pe.wait_ge(max_split, 2 * (a + 1))
                    dst = ps_s1[:, :].bitcast(F16)
                    for t in range(TT):
                        mm = pe.transpose(dst[0:2 * NH, t * P:(t + 1) * P],
                                          max_parts[:, t].rearrange("p a s j -> p (a s j)"), ident16[:, :])
                    mm.then_inc(max_turned, 1)

                def turn_o_back(a, b):
                    pe.wait_ge(oT_kept, 2 * (b + 1))
                    pe.wait_ge(exps_done, GROUPS * (b + 1))
                    if a is not None:
                        pe.wait_ge(qk_kept, 4 * a + 2)
                    for t in range(TT):
                        for quad in range(QUADS):
                            mm = pe.transpose(ps_s0[:, t * 512 + quad * P:t * 512 + (quad + 1) * P],
                                              oT[:, quad * TOK + t * P:quad * TOK + (t + 1) * P], ident[:, :])
                        mm.then_inc(o_back, 1)

                def turn_o(b):
                    pe.wait_ge(o_normed, 3 * (b + 1))
                    turn(o_n, ps_s0).then_inc(o_turned, 1)

                def project(b, t):
                    if t == 0:
                        pe.wait_ge(ot_hi_kept, 2 * (b + 1))
                        pe.wait_ge(ot_lo_kept, 2 * (b + 1))
                    tok = slice(t * P, (t + 1) * P)
                    dst = ps_s0[:, 512 * t:512 * t + HID]
                    for k in range(2):
                        pe.matmul(dst, ot_hi[:, k, tok], wp_hi[:, k, :], start=(k == 0), stop=False)
                        pe.matmul(dst, ot_hi[:, k, tok], wp_lo[:, k, :], start=False, stop=False)
                        pe.matmul(dst, ot_lo[:, k, tok], wp_hi[:, k, :], start=False, stop=False)
                    pe.matmul(dst, ot_c[0:CK, tok], wp_c[0:CK, :], start=False, stop=True).then_inc(projected, 1)

                def turn_ln2(c):
                    pe.wait_ge(xhat2_ready, 4 * (c + 1))
                    if isinstance(c, int) and c == 0:
                        pe.wait_ge(bias2_set, 1)
                    if is_last(c):
                        pe.wait_ge(oT_kept, 2 * (c + 1))
                    else:
                        reuse(pe, gated2_ready, 2, c)
                    turn(xhat2, ps_up(c)).then_inc(ln2_turned, 1)

                def mlp_up(c, m):
                    if m == 0:
                        pe.wait_ge(lt_hi_kept, 3 * (c + 1))
                        pe.wait_ge(lt_lo_kept, 3 * (c + 1))
                    if m >= 2:
                        pe.wait_ge(gelu_done, MT * c + m - 1)
                    dst = ps_up(c)[:, 512 * (m % 2):512 * (m % 2) + TOK]
                    cols = slice(m * P, (m + 1) * P)
                    for k in range(2):
                        pe.matmul(dst, w1_hi[:, k, cols], lt_hi[:, k, :], start=(k == 0), stop=False)
                        pe.matmul(dst, w1_hi[:, k, cols], lt_lo[:, k, :], start=False, stop=False)
                        pe.matmul(dst, w1_lo[:, k, cols], lt_hi[:, k, :], start=False, stop=False)
                    pe.matmul(dst, w1_c[0:CB, cols], lt_c[0:CB, :], start=False, stop=True).then_inc(up_done, 1)

                def mlp_down(c, first, last):
                    if isinstance(c, int) and c == 0 and first == 0:
                        pe.wait_ge(w2_hi_done, 1)
                        pe.wait_ge(w2_lo_done, 1)
                    for n in range(first, last):
                        t, r = n // (3 * MT + 1), n % (3 * MT + 1)
                        dst = ps_m[:, 512 * (1 - t):512 * (1 - t) + HID]
                        tok = slice(t * P, (t + 1) * P)
                        if r == 0:
                            if is_last(c):
                                reuse(pe, gated2_ready, 2, c)
                            else:
                                pe.wait_ge(gelu_done, MT * c + MT - 1 + t)
                            pe.matmul(dst, ones2[:, :], w2_b[:, :], start=True, stop=False)
                            continue
                        m, part = (r - 1) // 3, (r - 1) % 3
                        if t == 0 and part == 0:
                            pe.wait_ge(g_hi_kept, MT * c + m + 1)
                        if t == 0 and part == 2:
                            pe.wait_ge(g_lo_kept, MT * c + m + 1)
                        g = g_lo if part == 2 else g_hi
                        w = w2_lo if part == 1 else w2_hi
                        mm = pe.matmul(dst, g[:, m, tok], w[:, m, :], start=False, stop=(r == 3 * MT))
                        if r == 3 * MT:
                            mm.then_inc(down_done, 1)

                def bias2_of_all():
                    for n, (ps, at) in enumerate(THIRD_PIECES):
                        dst = ps[0:BATCH, at:at + THIRD]
                        cols = slice(n * THIRD, (n + 1) * THIRD)
                        for k in range(2):
                            pe.matmul(dst, sh_hi[:, k, :], w1_hi[:, k, cols], start=(k == 0), stop=False)
                            pe.matmul(dst, sh_hi[:, k, :], w1_lo[:, k, cols], start=False, stop=False)
                            pe.matmul(dst, sh_lo[:, k, :], w1_hi[:, k, cols], start=False, stop=False)
                        pe.matmul(dst, sh_c[:, :], w1_c[0:CB, cols], start=False, stop=True).then_inc(bias2_done, 1)

                def turn_bias2():
                    pe.wait_ge(bias2_kept, 3)
                    for m in range(MT):
                        mm = pe.transpose(ps_m[:, 512 + m * BATCH:512 + (m + 1) * BATCH], bias2_rows[:, m * P:(m + 1) * P],
                                          ident[0:BATCH, 0:BATCH])
                    mm.then_inc(bias2_turned, 1)

                def keep_warm(count):
                    for _ in range(count):
                        pe.matmul(ps_m[:, 0:THIRD], w1_hi[:, 0, 0:P], w1_hi[:, 0, 0:THIRD], start=True, stop=True)

                PIECE = 2 * (3 * MT + 1) // GROUPS

                def body(l, q, a, b, c, d):
                    Q, A, B, C, D = (n is not None for n in (q, a, b, c, d))

                    first = isinstance(a, int) and a == 0

                    def filler(g):
                        if D:
                            mlp_down(d, g * PIECE, (g + 1) * PIECE)
                        elif B and g >= 1:
                            keep_warm(5 if g < 3 else 2)

                    def up(begin, end):
                        if C:
                            for m in range(begin, end):
                                mlp_up(c, m)
                        elif B:
                            keep_warm(2 * (end - begin) if end < MT else 24)

                    def max_of(first_unit, last_unit):
                        if A and first:
                            for u in range(first_unit, last_unit):
                                maxima(a, u, u + 1)
                                keep_warm(2)
                        elif A:
                            maxima(a, first_unit, last_unit)

                    if B:
                        attend(a, b, filler)
                    else:
                        for g in range(GROUPS):
                            if C and g == 2:
                                turn_ln2(c)
                            filler(g)
                    if A:
                        turn_qk(a, b, 0)
                    if Q and not first:
                        turn_x(q, b)
                    if A:
                        turn_qk(a, b, 1)
                    if C and B:
                        turn_ln2(c)
                    if B:
                        turn_o_back(a, b)
                    max_of(0, 2)
                    if first:
                        turn_x(q, b)
                        max_of(2, 6)
                        qkv(q, 0, 1)
                        max_of(6, 8)
                        qkv(q, 0, 0)
                        max_of(8, MAXIMA)
                        turn_max(a)
                        qkv(q, 1, 1)
                        qkv(q, 1, 0)
                    else:
                        if Q:
                            qkv(q, 0, 1)
                        max_of(2, 4)
                        if Q:
                            qkv(q, 0, 0)
                        up(0, 2)
                        if B:
                            turn_o(b)
                        max_of(4, 6)
                        early = 3 if A else 4
                        up(2, early)
                        max_of(6, 7)
                        if Q:
                            qkv(q, 1, 1)
                        max_of(7, 8)
                        if B:
                            project(b, 0)
                        max_of(8, 10)
                        if B:
                            project(b, 1)
                        max_of(10, 11)
                        up(early, 4)
                        max_of(11, 13)
                        up(4, 5)
                        max_of(13, 15)
                        up(5, 6)
                        max_of(15, MAXIMA)
                        if Q:
                            qkv(q, 1, 0)
                        if A:
                            turn_max(a)
                        up(6, MT)
                    if isinstance(q, int) and q == 0:
                        bias2_of_all()
                        keep_warm(10)
                        turn_bias2()
                        keep_warm(16)

                iterations(pe, body)

            @block.scalar
            def _(act):
                def exps(b, g):
                    act.wait_ge(scores_done, GROUPS * b + g + 1)
                    if g >= 2:
                        act.wait_ge(pv_done, GROUPS * b + g - 1)
                    act.activation(probs[:, g % 2, :], ps_s[g % 2][:, :], ACT.Exp, scale=score_scale[:, 0:1]).then_inc(exps_done, 1)

                def keep_oT(b, half):
                    act.wait_ge(pv_done, GROUPS * b + 4 * half + 4)
                    if half == 0:
                        reuse(act, o_back, 2, b)
                    act.activation(oT[:, half * 512:(half + 1) * 512], ps_o[:, half * 512:(half + 1) * 512], ACT.Copy).then_inc(oT_kept, 1)

                def keep_hi(n, ps, turned, scales_in, scales, hi, stacked, kept, used, used_per):
                    act.wait_ge(turned, n + 1)
                    act.wait_ge(scales_in, 16 * (n + 1))
                    reuse(act, used, used_per, n)
                    act.activation(stacked[0:CB, :], ps[0:CB, 512:512 + TOK], ACT.Copy, scale=scales[0:CB, 2:3]).then_inc(kept, 1)
                    for k in range(2):
                        act.activation(hi[:, k, :], ps[:, k * TOK:(k + 1) * TOK], ACT.Copy, scale=scales[:, k:k + 1]).then_inc(kept, 1)

                def keep_o_hi(b):
                    act.wait_ge(o_turned, b + 1)
                    reuse(act, projected, 2, b)
                    act.activation(ot_hi[:, :, :].rearrange("p k t -> p (k t)"), ps_s0[:, 0:512], ACT.Copy).then_inc(ot_hi_kept, 1)
                    act.activation(ot_c[0:CB, :], ps_s0[0:CB, 512:512 + TOK], ACT.Copy).then_inc(ot_hi_kept, 1)

                def square(a, t):
                    act.wait_ge(raw_kept, 2 * a + t + 1)
                    reuse(act, ssq_ready, 2, a)
                    act.activation(squares[:, t, :].rearrange("p (c n) -> p c n", c=2), qkv_raw[:, t, :, 0:HID], ACT.Square).then_inc(squared, 1)

                def keep_raw(q, t):
                    act.wait_ge(qkv_done, 2 * q + t + 1)
                    if t == 0:
                        reuse(act, qk_normed, 4, q)
                        reuse(act, v_spread, 2, q)
                    act.activation(qkv_raw[:, t, :, :], ps_o[:, :].rearrange("p (c n) -> p c n", c=2)[:, :, 0:HALF], ACT.Copy).then_inc(raw_kept, 1)

                def keep_qk_hi(a, t):
                    if t == 0:
                        reuse(act, qk_turned, 4, a)
                    for n, (c, second) in enumerate(((1, 1), (0, 2))):
                        act.wait_ge(qk_normed, 4 * a + 2 * t + n + 1)
                        dst = stack[:, t, c, :, 0:MROW].rearrange("p h (s d) -> p h s d", d=HD)[:, :, 0:second + 1:second, :]
                        src = qk_n[:, t, c, :].rearrange("p (h d) -> p h d", d=HD)[:, :, None, :].broadcast_to([P, NH, 2, HD])
                        act.activation(dst, src, ACT.Copy).then_inc(qk_hi_kept, 1)

                def keep_max(a):
                    act.wait_ge(max_turned, a + 1)
                    reuse(act, max_rows_in, 32, a)
                    act.activation(max_rows[:, :], ps_s1[0:2 * NH, :].bitcast(F16)[:, 0:TOK], ACT.Copy).then_inc(max_kept, 1)

                def gelu(c, m):
                    if m == 0:
                        act.wait_ge(bias2_in, 16 * (c + 1))
                        reuse(act, g_lo_kept, MT, c)
                        reuse(act, down_done, 2, c)
                    act.wait_ge(up_done, MT * c + m + 1)
                    act.activation(g_full[:, m, :], ps_up(c)[:, 512 * (m % 2):512 * (m % 2) + TOK], ACT.Gelu_apprx_tanh,
                                   bias=bias2[:, m:m + 1]).then_inc(gelu_done, 1)

                def keep_g_hi(c, m):
                    act.wait_ge(gelu_done, MT * c + m + 1)
                    act.activation(g_hi[:, m, :], g_full[:, m, :], ACT.Copy).then_inc(g_hi_kept, 1)

                def gelus(c, first, last):
                    for m in range(first, last):
                        gelu(c, m)
                        if m > first:
                            keep_g_hi(c, m - 1)
                    keep_g_hi(c, last - 1)

                def body(l, q, a, b, c, d):
                    Q, A, B, C, D = (n is not None for n in (q, a, b, c, d))
                    if isinstance(q, int) and q == 0:
                        act.wait_ge(w2_in, 16)
                        act.activation(w2_hi[:, :, :], w2_raw[:, :, :], ACT.Copy).then_inc(w2_hi_done, 1)
                    for g in range(GROUPS):
                        if B:
                            exps(b, g)
                        if D and g < 2:
                            keep_g_hi(d, MT - 2 + g)
                        if B and g == 5:
                            keep_oT(b, 0)
                        if A and g in (3, 5):
                            keep_qk_hi(a, g // 5)
                    if B:
                        keep_oT(b, 1)
                    if Q:
                        keep_hi(q, ps_o, x_turned, sc1_in, sc1, xt_hi, xt_c, xt_hi_kept, qkv_done, 2)
                    if C:
                        keep_hi(c, ps_up(c), ln2_turned, sc2_in, sc2, lt_hi, lt_c, lt_hi_kept, up_done, MT)
                    if C:
                        act.activation(unused[:, :], warm[:, :], ACT.Gelu_apprx_tanh)
                    if Q:
                        keep_raw(q, 0)
                    if C:
                        gelu(c, 0)
                        gelu(c, 1)
                        keep_g_hi(c, 0)
                    if B:
                        keep_o_hi(b)
                    if C:
                        keep_g_hi(c, 1)
                        gelu(c, 2)
                        keep_g_hi(c, 2)
                    if Q:
                        square(q, 0)
                    if C:
                        gelus(c, 3, 6)
                    if A:
                        keep_max(a)
                    if Q:
                        keep_raw(q, 1)
                    if C:
                        gelu(c, 6)
                        gelu(c, 7)
                        keep_g_hi(c, 6)
                    if Q:
                        square(q, 1)
                    if C:
                        gelu(c, 8)
                    if isinstance(q, int) and q == 0:
                        for n, (ps, at) in enumerate(THIRD_PIECES):
                            act.wait_ge(bias2_done, n + 1)
                            act.activation(bias2_rows[:, n * THIRD:(n + 1) * THIRD], ps[0:BATCH, at:at + THIRD], ACT.Copy).then_inc(bias2_kept, 1)
                    if A:
                        act.activation(unused[:, :], warm[:, :], ACT.Exp)

                iterations(act, body)

            @block.vector
            def _(dve):
                def moments_of(n, src_in, src_count, src, st, mo, ve, stats_sem, var_sem, eps_sem):
                    dve.wait_ge(src_in, src_count * (n + 1))
                    for t in range(TT):
                        dve.bn_stats(st[:, t, :], src[:, t, :]).then_inc(stats_sem, 1)
                    dve.wait_ge(stats_sem, 2 * (n + 1))
                    dve.memset(waited[:, :], 0.0)
                    for t in range(TT):
                        dve.bn_aggr(mo[:, t, :], st[:, t, :]).then_inc(var_sem, 1)
                    dve.wait_ge(var_sem, 2 * (n + 1))
                    dve.tensor_scalar_add(ve[:, :], mo[:, :, 1], EPS).then_inc(eps_sem, 1)

                def normalise(n, src, mo, rs, rs_ready, dst, ready, turned):
                    dve.wait_ge(rs_ready, n + 1)
                    reuse(dve, turned, 1, n)
                    for t in range(TT):
                        dve.tensor_scalar(dst[:, t, 0:2 * P], src[:, t, 0:2 * P], mo[:, t, 0:1], rs[:, t:t + 1],
                                          ALU.subtract, ALU.mult).then_inc(ready, 1)
                        dve.tensor_scalar(dst[:, t, 2 * P:WIDE].rearrange("p (r n) -> p r n", r=3),
                                          src[:, t, None, 2 * P:HID].broadcast_to([P, 3, REST]), mo[:, t, 0:1], rs[:, t:t + 1],
                                          ALU.subtract, ALU.mult).then_inc(ready, 1)

                def keep_lo(n, ps, scales, hi, lo, stacked, hi_kept, kept):
                    dve.wait_ge(hi_kept, 3 * n + 1)
                    mid = slice(REST, 2 * REST)
                    dve.scalar_tensor_tensor(out=stacked[mid, :], in0=ps[mid, 512:512 + TOK], scalar=scales[mid, 2:3],
                                             in1=stacked[mid, :].bitcast(F32), op0=ALU.mult, op1=ALU.subtract).then_inc(kept, 1)
                    dve.wait_ge(hi_kept, 3 * n + 3)
                    for k in range(2):
                        dve.scalar_tensor_tensor(out=lo[:, k, :], in0=ps[:, k * TOK:(k + 1) * TOK], scalar=scales[:, k:k + 1],
                                                 in1=hi[:, k, :].bitcast(F32), op0=ALU.mult, op1=ALU.subtract).then_inc(kept, 1)

                def keep_mlp_lo(c):
                    dve.wait_ge(sc2_in, 16 * (c + 1))
                    keep_lo(c, ps_up(c), sc2, lt_hi, lt_lo, lt_c, lt_hi_kept, lt_lo_kept)

                def keep_o_lo(b):
                    dve.wait_ge(ot_hi_kept, 2 * b + 1)
                    dve.tensor_tensor(ot_lo[:, :, :].rearrange("p k t -> p (k t)"), ps_s0[:, 0:512],
                                      ot_hi[:, :, :].rearrange("p k t -> p (k t)").bitcast(F32), ALU.subtract).then_inc(ot_lo_kept, 1)
                    dve.wait_ge(ot_hi_kept, 2 * b + 2)
                    mid = slice(REST, 2 * REST)
                    dve.tensor_tensor(ot_c[mid, :], ps_s0[mid, 512:512 + TOK], ot_c[mid, :].bitcast(F32), ALU.subtract).then_inc(ot_lo_kept, 1)

                def o_over_sum(b):
                    reuse(dve, o_turned, 1, b)
                    for t in range(TT):
                        dve.wait_ge(o_back, 2 * b + t + 1)
                        heads = ps_s0[:, t * 512:(t + 1) * 512].rearrange("p (h e) -> p h e", e=32)
                        dve.reciprocal(recip[:, t, :], heads[:, :, HD]).then_inc(recip_ready, 1)
                        dve.wait_ge(recip_ready, 2 * b + t + 1)
                        dve.tensor_tensor(o_n[:, t, 0:HID].rearrange("p (h d) -> p h d", d=HD), heads[:, :, 0:HD],
                                          recip[:, t, :, None].broadcast_to([P, NH, HD]), ALU.mult).then_inc(o_normed, 1)
                    dve.wait_ge(o_normed, 3 * b + 2)
                    dve.tensor_copy(o_n[:, :, HID:WIDE].rearrange("p t (r n) -> p t r n", r=2),
                                    o_n[:, :, None, 2 * P:HID].broadcast_to([P, TT, 2, REST])).then_inc(o_normed, 1)

                def sum_squares(a, t):
                    dve.wait_ge(squared, 2 * a + t + 1)
                    dve.tensor_reduce(ssq[:, t, :], squares[:, t, :].rearrange("p (h d) -> p h d", d=HD), AX.X, ALU.add).then_inc(ssq_ready, 1)

                def rsqrt(a):
                    flat = lambda u: u[:, :, :].rearrange("p t h -> p (t h)")
                    var, r, tmp = flat(qk_var), flat(qk_r), flat(qk_tmp)
                    step = [NEWTON * a]

                    def link(ins):
                        ins.then_inc(newton, 1)
                        step[0] = step[0] + 1
                        dve.wait_ge(newton, step[0])

                    dve.wait_ge(ssq_ready, 2 * (a + 1))
                    link(dve.tensor_scalar(var, flat(ssq), 1.0 / HD, EPS, ALU.mult, ALU.add))
                    link(dve.tensor_scalar(r.bitcast(I32), var.bitcast(I32), -0.5, RSQRT_SEED, ALU.mult, ALU.add))
                    for _ in range(3):
                        link(dve.scalar_tensor_tensor(out=tmp, in0=r, scalar=-0.5, in1=r, op0=ALU.mult, op1=ALU.mult))
                        link(dve.tensor_tensor(tmp, tmp, var, ALU.mult))
                        link(dve.scalar_tensor_tensor(out=r, in0=tmp, scalar=1.5, in1=r, op0=ALU.add, op1=ALU.mult))

                def norm_qk(a, t):
                    if t == 0:
                        reuse(dve, qk_lo_kept, 4, a)
                        reuse(dve, qk_hi_kept, 4, a)
                    heads = lambda u: u.rearrange("p (h d) -> p h d", d=HD)
                    dve.tensor_tensor(heads(qk_n[:, t, 1, :]), heads(qkv_raw[:, t, 1, 0:HID]),
                                      qk_r[:, t, NH:2 * NH, None].broadcast_to([P, NH, HD]), ALU.mult).then_inc(qk_normed, 1)
                    dve.wait_ge(factor_ready, 2 * a + t + 1)
                    dve.tensor_tensor(heads(qk_n[:, t, 0, :]), heads(qkv_raw[:, t, 0, 0:HID]), heads(q_factor[:, t, :]), ALU.mult).then_inc(qk_normed, 1)

                def keep_qk(a, t, b):
                    if b is not None and t == 0:
                        dve.wait_ge(scores_done, GROUPS * (b + 1))
                    src = ps_s[t][:, :].bitcast(F16)
                    for c, dst in ((0, qT), (1, kT)):
                        dve.wait_ge(qk_turned, 4 * a + 2 * t + c + 1)
                        dve.tensor_copy(dst[:, :, t * P:(t + 1) * P],
                                        src[:, c * 1024:(c + 1) * 1024].rearrange("p (j n) -> p j n", n=P)).then_inc(qk_kept, 1)

                def row_max(a, first, last):
                    for u in range(first, last):
                        quad, qt, parity = u // 4, u // 2 % 2, u % 2
                        dve.wait_ge(max_scores, MAXIMA * a + u + 1)
                        dve.tensor_reduce(neg_max[:, qt, parity, 2 * quad:2 * quad + 2],
                                          ps_s1[:, 512 * parity:512 * (parity + 1)].rearrange("p (j n) -> p j n", j=2), AX.X, ALU.max,
                                          negate=True).then_inc(max_done, 1)

                def split_max(a):
                    dve.wait_ge(max_done, MAXIMA * (a + 1))
                    reuse(dve, max_turned, 1, a)
                    dve.tensor_copy(max_parts[:, :, :, 0, :], neg_max[:, :, :, :]).then_inc(max_split, 1)
                    dve.wait_ge(max_split, 2 * a + 1)
                    dve.tensor_tensor(max_parts[:, :, :, 1, :], neg_max[:, :, :, :], max_parts[:, :, :, 0, :], ALU.subtract).then_inc(max_split, 1)

                def gate(n, t, done, gate_in, src, g, dst, ready, used):
                    if t == 0:
                        dve.wait_ge(gate_in, 16 * (n + 1))
                        reuse(dve, used, 2, n)
                    dve.wait_ge(done, 2 * n + t + 1)
                    dve.tensor_tensor(dst[:, t, :], src[:, 0:HID], g[:, :], ALU.mult).then_inc(ready, 1)

                def body(l, q, a, b, c, d):
                    Q, A, B, C, D = (n is not None for n in (q, a, b, c, d))
                    first = isinstance(a, int) and a == 0
                    if first:
                        norm_qk(a, 0)
                        norm_qk(a, 1)
                    if Q:
                        moments_of(q, x_a_in, 16, x_a, stats, moments, var_eps, ln1_stats, ln1_var, ln1_eps)
                    if A and not first:
                        norm_qk(a, 0)
                        norm_qk(a, 1)
                    if Q and not first:
                        normalise(q, x_a, moments, rstd, ln1_rstd, xhat, xhat_ready, x_turned)
                    if C:
                        moments_of(c, x1_ready, 2, x1_new, stats2, moments2, var_eps2, ln2_stats, ln2_var, ln2_eps)
                    if is_last(c):
                        normalise(c, x1_new, moments2, rstd2, ln2_rstd, xhat2, xhat2_ready, ln2_turned)
                        keep_mlp_lo(c)
                    if D:
                        gate(d, 0, down_done, gate2_in, ps_m[:, 512:], gate2, gated2, gated2_ready, y_ready)
                    if C and not is_last(c):
                        normalise(c, x1_new, moments2, rstd2, ln2_rstd, xhat2, xhat2_ready, ln2_turned)
                    if D:
                        gate(d, 1, down_done, gate2_in, ps_m[:, 0:], gate2, gated2, gated2_ready, y_ready)

                    def max_of(first, last):
                        if A:
                            row_max(a, first, last)

                    if isinstance(c, int) and c == 0:
                        dve.wait_ge(bias2_turned, 1)
                        dve.tensor_tensor(columns[:, :, 6:6 + MT].rearrange("p b m -> p m b"),
                                          ps_m[:, 512:512 + MT * BATCH].rearrange("p (m b) -> p m b", m=MT),
                                          b1_cols[:, :, None].broadcast_to([P, MT, BATCH]), ALU.add).then_inc(bias2_set, 1)
                    if A:
                        keep_qk(a, 0, b)
                        keep_qk(a, 1, b)
                    if Q and first:
                        normalise(q, x_a, moments, rstd, ln1_rstd, xhat, xhat_ready, x_turned)
                        max_of(0, 4)
                    if Q:
                        dve.wait_ge(sc1_in, 16 * (q + 1))
                        keep_lo(q, ps_o, sc1, xt_hi, xt_lo, xt_c, xt_hi_kept, xt_lo_kept)
                    if not first:
                        max_of(0, 2)
                    if C and not is_last(c):
                        keep_mlp_lo(c)
                    if B:
                        o_over_sum(b)
                    max_of(4 if first else 2, 6)
                    if B:
                        keep_o_lo(b)
                    max_of(6, 16)
                    if A:
                        split_max(a)
                    if B:
                        gate(b, 0, projected, gate1_in, ps_s0[:, 0:], gate1, gated1, gated1_ready, x1_ready)
                        gate(b, 1, projected, gate1_in, ps_s0[:, 512:], gate1, gated1, gated1_ready, x1_ready)
                    if Q:
                        sum_squares(q, 0)
                        sum_squares(q, 1)
                        rsqrt(q)

                iterations(dve, body)

            @block.gpsimd
            def _(pool):
                def power(n, ve, eps_added, rs, ready):
                    pool.wait_ge(eps_added, n + 1)
                    pool.tensor_tensor(rs[:, :], ve[:, :], neg_half[:, :], ALU.pow).then_inc(ready, 1)

                def factor(a, t):
                    if t == 0:
                        pool.wait_ge(newton, NEWTON * (a + 1))
                    pool.tensor_tensor(q_factor[:, t, :].rearrange("p (h d) -> p h d", d=HD),
                                       qk_r[:, t, 0:NH, None].broadcast_to([P, NH, HD]),
                                       gain[:, None, :].broadcast_to([P, NH, HD]), ALU.mult).then_inc(factor_ready, 1)

                def keep_qk_lo(a, t):
                    for n, (c, lo) in enumerate(((1, 2), (0, 1))):
                        pool.wait_ge(qk_hi_kept, 4 * a + 2 * t + n + 1)
                        pool.tensor_tensor(stack[:, t, c, :, lo * HD:(lo + 1) * HD],
                                           qk_n[:, t, c, :].rearrange("p (h d) -> p h d", d=HD),
                                           stack[:, t, c, :, 0:HD], ALU.subtract).then_inc(qk_lo_kept, 1)

                def spread_v(a, b):
                    if b is not None:
                        pool.wait_ge(pv_done, GROUPS * (b + 1))
                    for t in range(TT):
                        pool.wait_ge(raw_kept, 2 * a + t + 1)
                        raw_v = qkv_raw[:, t, :, HID:HALF].rearrange("p c (h d) -> p c h d", d=HD)
                        pool.tensor_tensor(v[:, t, :, 0:HD].rearrange("p (c h) d -> p c h d", c=2), raw_v,
                                           one[:, :, None, None].broadcast_to([P, 2, NH // 2, HD]), ALU.mult).then_inc(v_spread, 1)

                def add_x(b):
                    pool.wait_ge(x_b_in, 16 * (b + 1))
                    reuse(pool, x1_moved, 16, b)
                    reuse(pool, xhat2_ready, 4, b)
                    for t in range(TT):
                        pool.wait_ge(gated1_ready, 2 * b + t + 1)
                        pool.tensor_tensor(x1_new[:, t, :], x_b[:, t, :], gated1[:, t, :], ALU.add).then_inc(x1_ready, 1)

                def keep_g_lo(c, m):
                    if m == 0:
                        reuse(pool, down_done, 2, c)
                    pool.wait_ge(g_hi_kept, MT * c + m + 1)
                    pool.tensor_tensor(g_lo[:, m, :], g_full[:, m, :], g_hi[:, m, :].bitcast(F32), ALU.subtract).then_inc(g_lo_kept, 1)

                def add_x1(d):
                    pool.wait_ge(x1_moved, 16 * (d + 1))
                    reuse(pool, out_stored, 16, d)
                    for t in range(TT):
                        pool.wait_ge(gated2_ready, 2 * d + t + 1)
                        pool.tensor_tensor(y[:, t, :], x1_c[:, t, :], gated2[:, t, :], ALU.add).then_inc(y_ready, 1)

                def body(l, q, a, b, c, d):
                    Q, A, B, C, D = (n is not None for n in (q, a, b, c, d))
                    if A:
                        factor(a, 0)
                        factor(a, 1)
                    first = isinstance(a, int) and a == 0
                    if Q and not first:
                        power(q, var_eps, ln1_eps, rstd, ln1_rstd)
                    if isinstance(q, int) and q == 0:
                        pool.wait_ge(w2_hi_done, 1)
                        pool.tensor_tensor(w2_lo[:, :, :], w2_raw[:, :, :], w2_hi[:, :, :].bitcast(F32), ALU.subtract).then_inc(w2_lo_done, 1)
                    if C and not is_last(c):
                        add_x(c)
                    if A:
                        keep_qk_lo(a, 0)
                    if C and not is_last(c):
                        power(c, var_eps2, ln2_eps, rstd2, ln2_rstd)
                    if A:
                        keep_qk_lo(a, 1)
                    if Q and first:
                        power(q, var_eps, ln1_eps, rstd, ln1_rstd)
                    if D:
                        add_x1(d)
                    if A:
                        spread_v(a, b)
                    if C:
                        for m in range(MT):
                            if is_last(b) and m == 3:
                                add_x(b)
                            if is_last(b) and m == 5:
                                power(b, var_eps2, ln2_eps, rstd2, ln2_rstd)
                            keep_g_lo(c, m)

                iterations(pool, body)


_INS = ['x', 'cond_1152', 'L0_cond_w_mod', 'L0_cond_b_mod', 'L0_cond_w_qkv', 'L0_cond_b_qkv', 'L0_cond_g_q',
        'L0_cond_g_k', 'L0_cond_w_proj', 'L0_cond_b_proj', 'L0_cond_w1', 'L0_cond_b1', 'L0_cond_w2', 'L0_cond_b2']
_OUT = ((BATCH, TOK, HID), 'float32')


def kernel(**inputs):
    import numpy as _np
    import concourse.bacc as _bacc
    from concourse import mybir as _mybir
    from concourse.bass_utils import run_bass_kernel_spmd as _run

    nc = _bacc.Bacc("TRN2", target_bir_lowering=False, num_devices=1)
    arrays, args = {}, []
    for name in _INS:
        a = _np.ascontiguousarray(inputs[name])
        arrays[f"in_{name}_dram"] = a
        args.append(nc.dram_tensor(f"in_{name}_dram", a.shape, _mybir.dt.from_np(a.dtype), kind="ExternalInput").ap())
    shape, dtype = _OUT
    args.append(nc.dram_tensor("out_0_dram", shape, _mybir.dt.from_np(_np.dtype(dtype)), kind="ExternalOutput").ap())
    cond_block_kernel(nc, *args)
    r = _run(nc, [arrays], core_ids=[0])
    return r.results[0]["out_0_dram"]
```
